# Optimizing a Trainium2 kernel written in Bass

```python
import numpy as np
import jax
import jax.numpy as jnp

def _softmax(x, axis=-1):
    return jax.nn.softmax(x, axis=axis)

def _gelu(x):
    return jax.nn.gelu(x, approximate=True)

def _silu(x):
    return jax.nn.silu(x)

def _sigmoid(x):
    return jax.nn.sigmoid(x)

def _layernorm(x, axis=-1, eps=1e-05):
    m = jnp.mean(x, axis=axis, keepdims=True)
    v = jnp.var(x, axis=axis, keepdims=True)
    return (x - m) / jnp.sqrt(v + eps)

def _scatter_add(tgt, idx, src, axis=0):
    return tgt.at[idx].add(src)

def _segment_sum(src, seg, n):
    return jax.ops.segment_sum(src, seg, n)
kernel_name = 'mk_seq_postln_d1_jaxref_r8_aacaab'

def setup_inputs(seed: int=0):
    np.random.seed(seed)
    _w = jnp.asarray

    def _L0_attn_setup():
        import jax, jax.numpy as jnp
        import numpy as np
        NUM_HEADS = 16
        key = jax.random.key(seed)
        x = jax.random.normal(key, (4, 256, 128), dtype=jnp.float32)
        return {'x': x}
    _L0_attn_in = _L0_attn_setup()

    def _L0_ffn_setup():
        import jax, jax.numpy as jnp
        import numpy as np
        E, K, NG, TG = (64, 8, 8, 4)
        CAP = 128
        SCALE = 2.5

        def _route(x_flat, gate_weight, e_bias):
            T = x_flat.shape[0]
            logits = x_flat.astype(jnp.float32) @ gate_weight.astype(jnp.float32).T
            scores = jax.nn.sigmoid(logits)
            sfc = scores + e_bias[None, :]
            group_scores = jax.lax.top_k(sfc.reshape(T, NG, E // NG), 2)[0].sum(-1)
            _, gidx = jax.lax.top_k(group_scores, TG)
            gmask = jnp.zeros((T, NG), jnp.float32).at[jnp.arange(T)[:, None], gidx].set(1.0)
            smask = jnp.repeat(gmask, E // NG, axis=1)
            tmp = jnp.where(smask > 0, sfc, 0.0)
            _, topk_idx = jax.lax.top_k(tmp, K)
            topk_w = jnp.take_along_axis(scores, topk_idx, axis=1)
            topk_w = topk_w / (topk_w.sum(-1, keepdims=True) + 1e-20)
            return (topk_idx, topk_w * SCALE)

        def _moe_forward(hidden_states, gate_weight, e_bias, w1, w2, w3, shared_gate, shared_up, shared_down):
            B, S, H = hidden_states.shape
            T = B * S
            x = hidden_states.reshape(T, H)
            topk_idx, topk_w = _route(x, gate_weight, e_bias)
            Sk = T * K
            flat_e = topk_idx.reshape(-1)
            order = jnp.argsort(flat_e)
            sorted_e = flat_e[order]
            counts = jax.ops.segment_sum(jnp.ones((Sk,), jnp.int32), flat_e, num_segments=E)
            offsets = jnp.cumsum(counts) - counts
            pos = jnp.arange(Sk) - offsets[sorted_e]
            tok_sorted = x[order // K]
            xe = jnp.zeros((E, CAP, H), x.dtype).at[sorted_e, pos].set(tok_sorted, mode='drop')
            h = jax.nn.silu(jnp.einsum('ech,efh->ecf', xe, w1)) * jnp.einsum('ech,efh->ecf', xe, w3)
            ye = jnp.einsum('ecf,ehf->ech', h, w2)
            pos_c = jnp.minimum(pos, CAP - 1)
            vals = ye[sorted_e, pos_c]
            vals = jnp.where((pos < CAP)[:, None], vals, 0.0)
            flat_w = topk_w.reshape(-1)[order].astype(vals.dtype)
            flat_t = (jnp.arange(Sk) // K)[order]
            out = jax.ops.segment_sum(vals * flat_w[:, None], flat_t, num_segments=T)
            shared = jax.nn.silu(x @ shared_gate.T) * (x @ shared_up.T) @ shared_down.T
            return (out + shared).reshape(B, S, H)
        key = jax.random.key(seed)
        ks = jax.random.split(key, 9)
        B, S, H, F = (1, 256, 128, 64)
        bound = 1.0 / 32.0
        return {'hidden_states': jax.random.normal(ks[0], (B, S, H), jnp.float32), 'gate_weight': jax.random.uniform(ks[1], (E, H), jnp.float32, -bound, bound), 'e_bias': jnp.zeros((E,), jnp.float32), 'w1': jax.random.normal(ks[2], (E, F, H), jnp.float32) * 0.02, 'w2': jax.random.normal(ks[3], (E, H, F), jnp.float32) * 0.02, 'w3': jax.random.normal(ks[4], (E, F, H), jnp.float32) * 0.02, 'shared_gate': jax.random.normal(ks[5], (2 * F, H), jnp.float32) * 0.02, 'shared_up': jax.random.normal(ks[6], (2 * F, H), jnp.float32) * 0.02, 'shared_down': jax.random.normal(ks[7], (H, 2 * F), jnp.float32) * 0.02}
    _L0_ffn_in = _L0_ffn_setup()
    _d = {'L0_attn_x': _L0_attn_in['x'], 'L0_ffn_gate_weight': _L0_ffn_in['gate_weight'], 'L0_ffn_e_bias': _L0_ffn_in['e_bias'], 'L0_ffn_w1': _L0_ffn_in['w1'], 'L0_ffn_w2': _L0_ffn_in['w2'], 'L0_ffn_w3': _L0_ffn_in['w3'], 'L0_ffn_shared_gate': _L0_ffn_in['shared_gate'], 'L0_ffn_shared_up': _L0_ffn_in['shared_up'], 'L0_ffn_shared_down': _L0_ffn_in['shared_down']}
    _x0 = _d['L0_attn_x']
    _d['L0_attn_x'] = jax.random.normal(jax.random.fold_in(jax.random.key(seed), 1), (8, 512, 128), dtype=_x0.dtype)
    del _x0
    return _d

def reference(L0_attn_x, L0_ffn_gate_weight, L0_ffn_e_bias, L0_ffn_w1, L0_ffn_w2, L0_ffn_w3, L0_ffn_shared_gate, L0_ffn_shared_up, L0_ffn_shared_down):

    def _L0_attn_ref(x):
        import jax, jax.numpy as jnp
        import numpy as np
        NUM_HEADS = 16
        B, T, D = x.shape
        H = NUM_HEADS
        hd = D // H
        xh = x.reshape(B, T, H, hd)
        x_centered = xh - jnp.mean(xh, axis=1, keepdims=True)
        corr = jnp.einsum('bthd,bThd->bhtT', x_centered, x_centered)
        corr = jax.nn.softmax(corr, axis=-1)
        out = jnp.einsum('bhtT,bThd->bthd', corr, xh)
        return out.reshape(B, T, D)

    def _L0_ffn_ref(hidden_states, gate_weight, e_bias, w1, w2, w3, shared_gate, shared_up, shared_down):
        import jax, jax.numpy as jnp
        import numpy as np
        E, K, NG, TG = (64, 8, 8, 4)
        CAP = 128
        SCALE = 2.5

        def _route(x_flat, gate_weight, e_bias):
            T = x_flat.shape[0]
            logits = x_flat.astype(jnp.float32) @ gate_weight.astype(jnp.float32).T
            scores = jax.nn.sigmoid(logits)
            sfc = scores + e_bias[None, :]
            group_scores = jax.lax.top_k(sfc.reshape(T, NG, E // NG), 2)[0].sum(-1)
            _, gidx = jax.lax.top_k(group_scores, TG)
            gmask = jnp.zeros((T, NG), jnp.float32).at[jnp.arange(T)[:, None], gidx].set(1.0)
            smask = jnp.repeat(gmask, E // NG, axis=1)
            tmp = jnp.where(smask > 0, sfc, 0.0)
            _, topk_idx = jax.lax.top_k(tmp, K)
            topk_w = jnp.take_along_axis(scores, topk_idx, axis=1)
            topk_w = topk_w / (topk_w.sum(-1, keepdims=True) + 1e-20)
            return (topk_idx, topk_w * SCALE)

        def _moe_forward(hidden_states, gate_weight, e_bias, w1, w2, w3, shared_gate, shared_up, shared_down):
            B, S, H = hidden_states.shape
            T = B * S
            x = hidden_states.reshape(T, H)
            topk_idx, topk_w = _route(x, gate_weight, e_bias)
            Sk = T * K
            flat_e = topk_idx.reshape(-1)
            order = jnp.argsort(flat_e)
            sorted_e = flat_e[order]
            counts = jax.ops.segment_sum(jnp.ones((Sk,), jnp.int32), flat_e, num_segments=E)
            offsets = jnp.cumsum(counts) - counts
            pos = jnp.arange(Sk) - offsets[sorted_e]
            tok_sorted = x[order // K]
            xe = jnp.zeros((E, CAP, H), x.dtype).at[sorted_e, pos].set(tok_sorted, mode='drop')
            h = jax.nn.silu(jnp.einsum('ech,efh->ecf', xe, w1)) * jnp.einsum('ech,efh->ecf', xe, w3)
            ye = jnp.einsum('ecf,ehf->ech', h, w2)
            pos_c = jnp.minimum(pos, CAP - 1)
            vals = ye[sorted_e, pos_c]
            vals = jnp.where((pos < CAP)[:, None], vals, 0.0)
            flat_w = topk_w.reshape(-1)[order].astype(vals.dtype)
            flat_t = (jnp.arange(Sk) // K)[order]
            out = jax.ops.segment_sum(vals * flat_w[:, None], flat_t, num_segments=T)
            shared = jax.nn.silu(x @ shared_gate.T) * (x @ shared_up.T) @ shared_down.T
            return (out + shared).reshape(B, S, H)
        return _moe_forward(hidden_states, gate_weight, e_bias, w1, w2, w3, shared_gate, shared_up, shared_down)
    x = L0_attn_x
    x = _layernorm(x + _L0_attn_ref(x), axis=-1)
    x = _layernorm(x + _L0_ffn_ref(x, L0_ffn_gate_weight, L0_ffn_e_bias, L0_ffn_w1, L0_ffn_w2, L0_ffn_w3, L0_ffn_shared_gate, L0_ffn_shared_up, L0_ffn_shared_down), axis=-1)
    return x

_drawn_inputs = setup_inputs


def setup_inputs(seed=0):
    import zlib

    import numpy as np

    out = dict(_drawn_inputs(seed))
    spreads = {'L0_ffn_e_bias': (0.0, 0.8)}
    factors = {'L0_ffn_gate_weight': 8.0,
     'L0_ffn_w1': 8.0,
     'L0_ffn_w2': 8.0,
     'L0_ffn_w3': 8.0,
     'L0_ffn_shared_gate': 8.0,
     'L0_ffn_shared_up': 8.0,
     'L0_ffn_shared_down': 8.0}
    for name, (base, spread) in spreads.items():
        noise = np.random.default_rng([zlib.crc32(name.encode()), seed]).standard_normal(out[name].shape)
        drawn = base * np.exp(spread * noise) if base else spread * noise
        out[name] = jnp.asarray(drawn.astype(out[name].dtype))
    for name, factor in factors.items():
        out[name] = (out[name] * factor).astype(out[name].dtype)
    return out
```

```python
from contextlib import ExitStack

import concourse.bass as bass
from concourse import mybir

ALU = mybir.AluOpType
ACT = mybir.ActivationFunctionType
AX = mybir.AxisListType
F32 = mybir.dt.float32
BF16 = mybir.dt.bfloat16
I32 = mybir.dt.int32
U32 = mybir.dt.uint32

P = 128
BATCHES, TOKENS, DIM = 8, 512, 128
HEADS = 16
HD = DIM // HEADS
TILES = TOKENS // P
VCOLS = HD + 1
PARTS = 3
ROWS = 6 * HD
HEAD_ROWS = 64
SHIFT_LIMIT = 60.0

EXPERTS, TOP, GROUPS, TOP_GROUPS = 64, 8, 8, 4
PER_GROUP = EXPERTS // GROUPS
CAP = 128
SLOTS = EXPERTS * CAP
FF = 64
SCALE = 2.5
NORM_EPS = 1e-5
ALL_TOKENS = BATCHES * TOKENS
REC = DIM + EXPERTS + 1
W_COL, TOK_COL = DIM, DIM + EXPERTS
SUMS = 4
ACC_ROWS = ALL_TOKENS + CAP
GROUP_OF = 4
STEPS = EXPERTS // GROUP_OF
BELOW_ALL = -1e30

QUAD = 4
QUADS = HEADS // QUAD
UNITS = 2 * QUADS
SLOTS_PER_BATCH = 2 * UNITS
CHUNKS = 2 * HEADS

BANK = {"mean": 0, "xt": 1, "gate": 0, "logits": 1, "up": 0, "down": 1, "pos": 1, "totals": 1,
        "lr0": 0, "lr1": 0, "lr2": 0, "lr3": 1, "lr4": 0, "lr5": 1, "lr6": 0, "lr7": 1}
SLOT_OF = {"mean": 0, "xt": 3, "gate": 4, "logits": 5, "up": 6, "down": 8, "lr0": 8, "pos": 9, "lr1": 9,
           "totals": 10, "lr2": 10, "lr3": 11, "lr4": 12, "lr5": 13, "lr6": 15, "lr7": 15}
PREP_JOBS = ["mean"] + [f"lr{j}" for j in range(8)]
POST_JOBS = ["xt", "gate", "logits", "up", "down", "pos", "totals"]
WEIGHT_JOBS = EXPERTS // 4 + EXPERTS // 8
PHASES = {"prologue": PREP_JOBS, "first": PREP_JOBS, "mid": list(SLOT_OF), "last": POST_JOBS, "epilogue": POST_JOBS}
RUNS = {"prologue": 1, "first": 1, "mid": BATCHES - 2, "last": 1, "epilogue": 1}

PREP_STEPS = ["high", "rest", "middle", "low", "square", "norms", "largest",
              "r24", "r40", "l0", "l24", "l40", "slow", "neg_small", "shift"]
POST_STEPS = (["y"] + [f"stats{i}" for i in range(4)] + [f"moments{i}" for i in range(4)]
              + ["veps", "r2", "vr2", "corr", "rstd"] + [f"x1_{i}" for i in range(4)]
              + ["g1", "grec", "s1", "scores", "sfc", "hi4", "lo4", "hi2", "t2", "u2", "lo2", "hi1", "t1", "u1",
                 "lo1", "gs", "ge", "gt", "geL", "beats", "rank", "keep", "tmp", "tmp0"]
              + [f"top{i}" for i in range(4)] + [f"rest{i}" for i in range(4)]
              + ["mask", "maskb", "wsel", "wsum", "wsum2", "wrec", "recw", "recx", "rectok", "tokens",
                 "kept", "room", "key"] + [f"slots{i}" for i in range(4)] + ["index"])
ACT_POST_STEPS = ["log", "rstd0", "exp_gate"]
FIN_STEPS = (["a01", "a23", "sum", "y"] + [f"stats{i}" for i in range(4)] + [f"moments{i}" for i in range(4)]
             + ["veps", "r2", "vr2", "corr", "rstd"] + [f"out{i}" for i in range(4)])


def post_norm_block(nc, x, gate_w, e_bias, w1, w2, w3, s_gate, s_up, s_down, out):
    with ExitStack() as ctx:
        def sb(name, shape, dt=F32):
            return ctx.enter_context(nc.sbuf_tensor(name, shape, dt))

        def psum(name, shape, dt=F32):
            return ctx.enter_context(nc.psum_tensor(name, shape, dt))

        def sem(name):
            return ctx.enter_context(nc.semaphore(name))

        records = nc.dram_tensor("records", (SLOTS, REC), F32, kind="Internal").ap()
        sums = [nc.dram_tensor(f"sums{j}", (ACC_ROWS, DIM), F32, kind="Internal").ap() for j in range(SUMS)]

        ident = sb("ident", [P, P])
        ident_b = sb("ident_b", [P, P], BF16)
        mean_w = sb("mean_w", [P, P])
        before_b = sb("before_b", [P, P], BF16)
        ones_b = sb("ones_b", [P, P], BF16)
        lower = sb("lower", [P, GROUPS, GROUPS])
        slot_base_i = sb("slot_base_i", [P, EXPERTS], I32)
        slot_base = sb("slot_base", [P, EXPERTS])
        token_i = sb("token_i", [P, TILES], I32)
        token = sb("token", [P, TILES])
        eps = sb("eps", [P, 1])
        blank_i = sb("blank_i", [P, 1], I32)
        blank = sb("blank", [P, REC])
        bias = sb("bias", [P, EXPERTS])
        small_w = sb("small_w", [P, 4, P])
        small_T = sb("small_T", [P, 4, P])
        w13 = sb("w13", [P, EXPERTS, P])
        w2n = sb("w2n", [P, EXPERTS, FF])
        X = sb("X", [P, BATCHES * TILES * DIM])
        V = sb("V", [P, TILES, HEADS, VCOLS])
        centred = sb("centred", [P, 3, TILES * DIM])
        xc, rest, square = (centred[:, k, :] for k in range(3))
        norms = sb("norms", [P, TILES * HEADS])
        largest = sb("largest", [P, 1])
        largest_all = sb("largest_all", [P, 1])
        slow_flag = sb("slow_flag", [P, BATCHES], I32)
        neg_small = sb("neg_small", [P, 1])
        shift = sb("shift", [P, BATCHES])
        AK = sb("AK", [P, TILES, HEADS, HEAD_ROWS], BF16)
        AQ = sb("AQ", [P, TILES, HEADS, HEAD_ROWS], BF16)
        LR = sb("LR", [P, HEADS // 2, 2, TOKENS], BF16)
        E = sb("E", [P, 2, QUAD, 2, TOKENS])
        OT = sb("OT", [P, TOKENS])
        rden = sb("rden", [P, TILES, QUAD])
        O = sb("O", [P, TILES, DIM])
        row_max = sb("row_max", [P, HEADS, TILES])
        row_rest = sb("row_rest", [P, HEADS, TILES])
        stats = sb("stats", [P, TILES, 6])
        moments = sb("moments", [P, TILES, 2])
        log_v = sb("log_v", [P, TILES])
        rstd0 = sb("rstd0", [P, TILES])
        veps = sb("veps", [P, TILES])
        r2 = sb("r2", [P, TILES])
        rstd = sb("rstd", [P, TILES])
        x1 = sb("x1", [P, TILES, DIM])
        x1T = sb("x1T", [P, TOKENS])
        eg = sb("eg", [P, TOKENS])
        sg = sb("sg", [P, TOKENS])
        hT = sb("hT", [P, TOKENS])
        el = sb("el", [P, TILES * EXPERTS])
        scores = sb("scores", [P, TILES * EXPERTS])
        sfc = sb("sfc", [P, TILES * EXPERTS])
        hi4 = sb("hi4", [P, 32, 4])
        lo4 = sb("lo4", [P, 32, 4])
        hi2 = sb("hi2", [P, 32, 2])
        t2 = sb("t2", [P, 32, 2])
        u2 = sb("u2", [P, 32, 2])
        lo2 = sb("lo2", [P, 32, 2])
        hi1 = sb("hi1", [P, 32])
        t1 = sb("t1", [P, 32])
        u1 = sb("u1", [P, 32])
        lo1 = sb("lo1", [P, 32])
        gs = sb("gs", [P, TILES, GROUPS])
        ge = sb("ge", [P, TILES, GROUPS, GROUPS])
        gt = sb("gt", [P, TILES, GROUPS, GROUPS])
        rank = sb("rank", [P, TILES * GROUPS])
        keep = sb("keep", [P, TILES * GROUPS])
        tmp = sb("tmp", [P, TILES * EXPERTS])
        top = sb("top", [P, TILES, 8])
        left = sb("left", [P, TILES * EXPERTS])
        mask = sb("mask", [P, TILES * EXPERTS])
        mask_b = sb("mask_b", [P, TILES, EXPERTS], BF16)
        wsel = sb("wsel", [P, TILES * EXPERTS])
        wsum = sb("wsum", [P, TILES])
        count = sb("count", [P, EXPERTS])
        pos = sb("pos", [P, TILES * EXPERTS])
        kept = sb("kept", [P, TILES * EXPERTS])
        key = sb("key", [P, TILES * EXPERTS])
        best = sb("best", [P, TILES, 8])
        index = sb("index", [P, TILES * 8], U32)
        rec = sb("rec", [P, TILES, REC])
        Z = sb("Z", [P, BATCHES * TILES * DIM])
        w2bd = E[:, :, :, :, :].rearrange("p a b c d -> p (a b c d)").rearrange("p (r c) -> p r c", c=2 * DIM)
        free_f32 = AK[:, :, :, :].rearrange("p a b c -> p (a b c)").bitcast(F32)
        slots_in = X[:, 0:4 * GROUP_OF * REC].rearrange("p (s r) -> p s r", s=4)
        eh = X[:, 4 * GROUP_OF * REC:4 * GROUP_OF * REC + 2 * GROUP_OF * FF].rearrange(
            "p (s i f) -> p s i f", s=2, i=GROUP_OF)
        xeT = free_f32[:, 0:2 * GROUP_OF * CAP].rearrange("p (s c) -> p s c", s=2)
        h = free_f32[:, 8 * CAP:8 * CAP + 8 * FF].rearrange("p (s f) -> p s f", s=2)
        ehT = free_f32[:, 8 * CAP + 8 * FF:12 * CAP + 8 * FF].rearrange("p (s c) -> p s c", s=2)
        ye = centred[:, 0:2, :].rearrange("p s (i d) -> p s i d", i=GROUP_OF)
        target = sb("target", [P, 2, GROUP_OF], U32)
        sums_in = LR[:, :, :, :].rearrange("p a b c -> p (a b c)").bitcast(F32).rearrange("p (s t) -> p s t", s=8)
        normed = AQ[:, :, :, :].rearrange("p a b c -> p (a b c)").bitcast(F32).rearrange("p (s t) -> p s t", s=4)

        S = psum("S", [P, 4, 512])
        PV = [psum(f"PV{o}", [P, 512]) for o in range(2)]
        M = [psum(f"M{o}", [P, 512]) for o in range(2)]
        Mb = [m[:, :].bitcast(BF16) for m in M]

        setup = sem("setup")
        constants = sem("constants")
        x_loaded = sem("x_loaded")
        small_loaded = sem("small_loaded")
        small_turned = sem("small_turned")
        small_ready = sem("small_ready")
        weights_loaded = sem("weights_loaded")
        records_blank = sem("records_blank")
        dram_blank = sem("dram_blank")
        written = [sem(f"written{o}") for o in range(2)]
        read = [sem(f"read{o}") for o in range(2)]
        prep = sem("prep")
        all_reduced = sem("all_reduced")
        scored = sem("scored")
        exp_done = sem("exp_done")
        unit_weighed = sem("unit_weighed")
        quad_copied = sem("quad_copied")
        quad_turned = sem("quad_turned")
        banks_clear = sem("banks_clear")
        pv_recip = sem("pv_recip")
        pv_read = sem("pv_read")
        v_built = sem("v_built")
        row_scored = sem("row_scored")
        row_read = sem("row_read")
        row_parts = sem("row_parts")
        post = sem("post")
        act_post = sem("act_post")
        scattered = sem("scattered")
        record_free = sem("record_free")
        w2_cleared = sem("w2_cleared")
        w2_ready = sem("w2_ready")
        slots_loaded = sem("slots_loaded")
        x_turned = sem("x_turned")
        x_copied = sem("x_copied")
        up_done = sem("up_done")
        exp_up = sem("exp_up")
        silu = sem("silu")
        h_turned = sem("h_turned")
        h_copied = sem("h_copied")
        down_done = sem("down_done")
        weighted = sem("weighted")
        aimed = sem("aimed")
        added = [sem(f"added{j}") for j in range(SUMS)]
        parts_loaded = [sem(f"parts_loaded{j}") for j in range(2)]
        fin = sem("fin")
        act_fin = sem("act_fin")
        stored = [sem(f"stored{j}") for j in range(2)]
        carrier = sem("carrier")

        block = ctx.enter_context(nc.Block())

        def wait(eng, s, value):
            if isinstance(value, int):
                if value > 0:
                    eng.wait_ge(s, value)
            else:
                eng.wait_ge(s, value)
                eng.sem_inc(carrier, 1)

        def jobs_before(phase, b, bank):
            n = 0
            for name, jobs in PHASES.items():
                here = sum(BANK[j] == bank for j in jobs)
                if name == phase:
                    return n + (here * (b - 1) if name == "mid" else 0)
                n += here * RUNS[name]

        def job(phase, b, name):
            bank = BANK[name]
            here = [j for j in PHASES[phase] if BANK[j] == bank]
            return bank, jobs_before(phase, b, bank) + here.index(name)

        epilogue_end = [jobs_before("epilogue", 0, o) + sum(BANK[j] == o for j in POST_JOBS) for o in range(2)]

        def prep_at(q, step):
            return q * len(PREP_STEPS) + PREP_STEPS.index(step) + 1

        def post_at(p, step):
            return p * len(POST_STEPS) + POST_STEPS.index(step) + 1

        def act_post_at(p, step):
            return p * len(ACT_POST_STEPS) + ACT_POST_STEPS.index(step) + 1

        def fin_at(q, step):
            return q * len(FIN_STEPS) + FIN_STEPS.index(step) + 1

        def tokens_of(t, q, i=0, n=TILES):
            return t[:, bass.ds(q * TILES * DIM + i * DIM, n * DIM)]

        def iterations(eng, body):
            body("first", 0)
            with eng.Fori(1, BATCHES - 1) as b:
                body("mid", b)
            body("last", BATCHES - 1)

        SETUP = 16

        @block.sync
        def _(sp):
            for q in range(BATCHES):
                if q > 0:
                    sp.wait_ge(x_loaded, 16 * q)
                sp.dma_start(tokens_of(X, q).rearrange("p (i d) -> p i d", i=TILES),
                             x[q].rearrange("(i p) d -> p i d", p=P)).then_inc(x_loaded, 16)
                if q == 0:
                    sp.dma_start(small_w[0:EXPERTS, 0, :], gate_w).then_inc(small_loaded, 16)
                    sp.dma_start(small_w[:, 1, :], s_gate).then_inc(small_loaded, 16)
                    sp.dma_start(small_w[:, 2, :], s_up).then_inc(small_loaded, 16)
                    sp.dma_start(small_w[:, 3, :], s_down).then_inc(small_loaded, 16)
                    sp.dma_start(bias[:, :], e_bias.rearrange("(a e) -> a e", a=1).to_broadcast([P, EXPERTS])
                                 ).then_inc(small_loaded, 16)
            sp.wait_ge(setup, SETUP)
            sp.wait_ge(small_ready, 3)
            sp.dma_start(records.rearrange("(e c) r -> c e r", c=CAP),
                         blank[:, :].unsqueeze(1).to_broadcast([P, EXPERTS, REC])).then_inc(records_blank, 16)
            for j in range(SUMS):
                sp.dma_start(sums[j].rearrange("(p r) d -> p r d", p=P),
                             blank[:, 0:DIM].unsqueeze(1).to_broadcast([P, ACC_ROWS // P, DIM])
                             ).then_inc(dram_blank, 16)
            sp.dma_start(w13[0:FF, :, :], w1.rearrange("e f h -> f e h")).then_inc(weights_loaded, 16)
            sp.dma_start(w13[FF:P, :, :], w3.rearrange("e f h -> f e h")).then_inc(weights_loaded, 16)
            sp.dma_start(w2n[:, :, :], w2.rearrange("e h f -> h e f")).then_inc(weights_loaded, 16)
            sp.wait_ge(scattered, 16 * BATCHES * TILES * TOP)

            def load_slots(s, u):
                if not isinstance(s, int) or s >= 4:
                    wait(sp, weighted, s - 3)
                    wait(sp, aimed, s - 3)
                if not isinstance(s, int) or s >= 1:
                    wait(sp, slots_loaded, 16 * s)
                sp.dma_start(slots_in[:, u, :].rearrange("p (i r) -> p i r", i=GROUP_OF),
                             records[bass.ds(s * GROUP_OF * CAP, GROUP_OF * CAP), :].rearrange("(i c) r -> c i r", c=CAP)
                             ).then_inc(slots_loaded, 16)

            for s in range(4):
                load_slots(s, s)
            with sp.Fori(1, STEPS // 4) as r:
                for u in range(4):
                    load_slots(4 * r + u, u)

            for j in range(SUMS):
                sp.wait_ge(added[j], 16 * STEPS)

            def load_parts(q, u):
                if not isinstance(q, int) or q >= 2:
                    wait(sp, fin, fin_at(q - 2, "sum"))
                for j in range(SUMS):
                    sp.dma_start(sums_in[:, SUMS * u + j, :].rearrange("p (i d) -> p i d", i=TILES),
                                 sums[j][bass.ds(q * TOKENS, TOKENS), :].rearrange("(i p) d -> p i d", p=P)
                                 ).then_inc(parts_loaded[u], 16)

            def store(q, u):
                wait(sp, fin, fin_at(q, "out3"))
                sp.dma_start(out[bass.ds(q, 1)].rearrange("a (i p) d -> p (a i) d", p=P),
                             normed[:, u, :].rearrange("p (i d) -> p i d", i=TILES)).then_inc(stored[u], 16)

            load_parts(0, 0)
            load_parts(1, 1)
            with sp.Fori(0, BATCHES // 2 - 1) as r:
                for u in range(2):
                    store(2 * r + u, u)
                    load_parts(2 * r + 2 + u, u)
            for u in range(2):
                store(BATCHES - 2 + u, u)
            for u in range(2):
                sp.wait_ge(stored[u], 16 * BATCHES // 2)

        @block.gpsimd
        def _(pool):
            def fill(t, value):
                nc.gpsimd.memset(t, value).then_inc(setup, 1)

            fill(mean_w[:, :], 1.0 / TOKENS)
            fill(ident[:, :], 0.0)
            fill(ident_b[:, :], 0.0)
            fill(ones_b[:, :], 1.0)
            fill(before_b[:, :], 1.0)
            fill(lower[:, :, :], 1.0)
            fill(AQ[:, :, :, :], 0.0)
            fill(AK[:, :, :, 0:ROWS], 0.0)
            fill(AK[:, :, :, ROWS:HEAD_ROWS], 0.0)
            fill(V[:, :, :, HD:VCOLS], 1.0)
            fill(count[:, :], 0.0)
            fill(eps[:, :], NORM_EPS)
            fill(blank[:, 0:TOK_COL], 0.0)
            nc.gpsimd.iota(slot_base_i[:, :], [[-CAP, EXPERTS]], base=SLOTS, channel_multiplier=0).then_inc(setup, 1)
            nc.gpsimd.iota(token_i[:, :], [[P, TILES]], base=0, channel_multiplier=1).then_inc(setup, 1)
            nc.gpsimd.iota(blank_i[:, :], [[0, 1]], base=ALL_TOKENS, channel_multiplier=1).then_inc(setup, 1)
            pool.wait_ge(setup, SETUP)
            for t, op, step, off in ((ident, ALU.not_equal, -1, 0), (ident_b, ALU.not_equal, -1, 0)):
                nc.gpsimd.affine_select(out=t[:, :], in_=t[:, :], compare_op=op, fill=1.0, base=off,
                                        pattern=[[step, P]], channel_multiplier=1).then_inc(constants, 1)
            nc.gpsimd.affine_select(out=before_b[:, :], in_=before_b[:, :], compare_op=ALU.is_gt, fill=0.0, base=0,
                                    pattern=[[1, P]], channel_multiplier=-1).then_inc(constants, 1)
            nc.gpsimd.affine_select(out=lower[:, :, :], in_=lower[:, :, :], compare_op=ALU.is_gt, fill=0.0, base=0,
                                    pattern=[[1, GROUPS], [-1, GROUPS]], channel_multiplier=0).then_inc(constants, 1)
            nc.gpsimd.memset(AK[:, :, :, ROWS:ROWS + PARTS], 1.0).then_inc(constants, 1)

            def reduce_all(q):
                wait(pool, prep, prep_at(q, "largest"))
                nc.gpsimd.partition_all_reduce(largest_all[:, :], largest[:, :], P, bass.bass_isa.ReduceOp.max
                                               ).then_inc(all_reduced, 1)

            def scatter(p):
                wait(pool, post, post_at(p, "index"))
                for i in range(TILES):
                    for k in range(TOP):
                        pool.indirect_dma_start(
                            records, bass.IndirectOffsetOnAxis(ap=index[:, i * TOP + k:i * TOP + k + 1], axis=0),
                            rec[:, i, :], None, bounds_check=SLOTS - 1, oob_is_err=False).then_inc(scattered, 16)
                wait(pool, scattered, 16 * TILES * TOP * (p + 1))
                pool.sem_inc(record_free, 1)

            def batch(phase, b):
                if phase != "last":
                    reduce_all(b + 1)
                if phase != "first":
                    scatter(b - 1)

            reduce_all(0)
            pool.wait_ge(records_blank, 16)
            pool.sem_inc(record_free, 1)
            iterations(pool, batch)
            scatter(BATCHES - 1)
            pool.wait_ge(dram_blank, 16 * SUMS)

            def add_rows(s, u):
                wait(pool, weighted, s + 1)
                wait(pool, aimed, s + 1)
                for j in range(SUMS):
                    if not isinstance(s, int) or s >= 1:
                        wait(pool, added[j], 16 * s)
                    pool.indirect_dma_start(
                        sums[j], bass.IndirectOffsetOnAxis(ap=target[:, u, j:j + 1], axis=0),
                        ye[:, u, j, :], None, bounds_check=ACC_ROWS - 1, oob_is_err=True,
                        compute_op=ALU.add).then_inc(added[j], 16)

            add_rows(0, 0)
            add_rows(1, 1)
            with pool.Fori(1, STEPS // 2) as r:
                for u in range(2):
                    add_rows(2 * r + u, u)

        @block.tensor
        def _(pe):
            def begin(phase, b, name):
                bank, n = job(phase, b, name)
                wait(pe, read[bank], n)
                return bank

            def mean(phase, b, q):
                wait(pe, x_loaded, 16 * (q + 1))
                m = begin(phase, b, "mean")
                for i in range(TILES):
                    mm = pe.matmul(M[m][:, 0:DIM], mean_w[:, :], tokens_of(X, q, i, 1), start=i == 0, stop=i == TILES - 1)
                mm.then_inc(written[m], 1)

            def turn(phase, b, q, j):
                if j == 0:
                    wait(pe, prep, prep_at(q, "l40"))
                m = begin(phase, b, f"lr{j}")
                for side, A in enumerate((AK, AQ)):
                    for i in range(TILES):
                        mm = pe.transpose(Mb[m][:, side * TOKENS + i * P:side * TOKENS + (i + 1) * P],
                                          A[:, i, 2 * j:2 * j + 2, :].rearrange("p a c -> p (a c)"), ident_b[:, :])
                mm.then_inc(written[m], 1)

            def xt(phase, b, p):
                wait(pe, post, post_at(p, "x1_3"))
                m = begin(phase, b, "xt")
                for i in range(TILES):
                    mm = pe.transpose(M[m][:, i * P:(i + 1) * P], x1[:, i, :], ident[:, :])
                mm.then_inc(written[m], 1)

            def xt_copied(phase, b):
                bank, n = job(phase, b, "xt")
                wait(pe, read[bank], n + 1)

            def gate(phase, b, p):
                xt_copied(phase, b)
                m = begin(phase, b, "gate")
                pe.matmul(M[m][:, :], small_T[:, 1, :], x1T[:, :], start=True, stop=True).then_inc(written[m], 1)

            def logits(phase, b, p):
                m = begin(phase, b, "logits")
                for i in range(TILES):
                    mm = pe.matmul(M[m][:, i * EXPERTS:(i + 1) * EXPERTS], x1T[:, i * P:(i + 1) * P],
                                   small_T[:, 0, 0:EXPERTS], start=True, stop=True)
                mm.then_inc(written[m], 1)

            def up(phase, b, p):
                m = begin(phase, b, "up")
                pe.matmul(M[m][:, :], small_T[:, 2, :], x1T[:, :], start=True, stop=True).then_inc(written[m], 1)

            def down(phase, b, p):
                bank, n = job(phase, b, "up")
                wait(pe, read[bank], n + 1)
                m = begin(phase, b, "down")
                for i in range(TILES):
                    mm = pe.matmul(M[m][:, i * DIM:(i + 1) * DIM], hT[:, i * P:(i + 1) * P], small_T[:, 3, :],
                                   start=True, stop=True)
                mm.then_inc(written[m], 1)

            def positions(phase, b, p):
                wait(pe, post, post_at(p, "maskb"))
                m = begin(phase, b, "pos")
                for i in range(TILES):
                    o = M[m][:, i * EXPERTS:(i + 1) * EXPERTS]
                    mm = pe.matmul(o, before_b[:, :], mask_b[:, i, :], start=True, stop=i == 0)
                    for k in range(i):
                        mm = pe.matmul(o, ones_b[:, :], mask_b[:, k, :], start=False, stop=k == i - 1)
                mm.then_inc(written[m], 1)

            def totals(phase, b, p):
                m = begin(phase, b, "totals")
                for i in range(TILES):
                    mm = pe.matmul(M[m][:, 0:EXPERTS], ones_b[:, :], mask_b[:, i, :], start=i == 0, stop=i == TILES - 1)
                mm.then_inc(written[m], 1)

            def run_job(phase, b, name):
                if name == "mean":
                    mean(phase, b, b + 1)
                elif name.startswith("lr"):
                    turn(phase, b, b + 1, int(name[2:]))
                else:
                    {"xt": xt, "gate": gate, "logits": logits, "up": up, "down": down, "pos": positions,
                     "totals": totals}[name](phase, b, b - 1)

            def score(b, u, i):
                hd, c = QUAD * (u // 2) + i, u % 2
                q, half, n = hd // 2, HEAD_ROWS * (hd % 2), QUAD * u + i
                if not isinstance(b, int) or b > 0 or n >= 2:
                    wait(pe, exp_done, b * CHUNKS + n - 1)
                for k in range(2):
                    tile = 2 * c + k
                    mm = pe.matmul(S[:, 2 * (n % 2) + k, :], LR[half:half + HEAD_ROWS, q, 0, tile * P:(tile + 1) * P],
                                   LR[half:half + HEAD_ROWS, q, 1, :], start=True, stop=True)
                mm.then_inc(scored, 1)

            def weigh(b, u, k):
                g, c = u // 2, u % 2
                if k == 0:
                    wait(pe, exp_done, b * CHUNKS + QUAD * (u + 1))
                    if u == 0:
                        wait(pe, v_built, b + 1)
                    if c == 0 and (g >= 2 or not isinstance(b, int) or b > 0):
                        wait(pe, pv_read, QUADS * b + g - 1)
                for i in range(QUAD):
                    mm = pe.matmul(PV[g % 2][32 * i:32 * i + VCOLS, :], V[:, 2 * c + k, QUAD * g + i, :],
                                   E[:, u % 2, i, k, :], start=c == 0 and k == 0, stop=c == 1 and k == 1,
                                   tile_position=(0, 32 * i))
                if k == 1:
                    mm.then_inc(unit_weighed, 1)

            def turn_quad(b, g):
                wait(pe, quad_copied, QUADS * b + g + 1)
                for i in range(TILES):
                    mm = pe.transpose(PV[g % 2][:, i * P:(i + 1) * P], OT[:, i * P:(i + 1) * P], ident[:, :])
                mm.then_inc(quad_turned, 1)

            def row_maxima(b):
                flag = pe.value_load(slow_flag[0:1, bass.ds(b, 1)], min_val=0, max_val=1)
                with pe.If(flag > 0):
                    if not isinstance(b, int) or b > 0:
                        wait(pe, exp_done, b * CHUNKS)
                    for hd in range(HEADS):
                        q, half = hd // 2, HEAD_ROWS * (hd % 2)
                        if hd > 0 or not isinstance(b, int) or b > 0:
                            wait(pe, row_read, b * 24 + hd)
                        for i in range(TILES):
                            mm = pe.matmul(S[:, i, :], LR[half:half + HEAD_ROWS, q, 1, i * P:(i + 1) * P],
                                           LR[half:half + HEAD_ROWS, q, 0, :], start=True, stop=True)
                        mm.then_inc(row_scored, 1)
                    wait(pe, row_parts, b * 6 + 5)
                    Sb = S[:, 0, :].bitcast(BF16)
                    for q in range(HEADS // 2):
                        wait(pe, row_read, b * 24 + HEADS + q)
                        for i in range(TILES):
                            mm = pe.transpose(Sb[:, i * P:(i + 1) * P],
                                              AQ[:, i, 2 * q:2 * q + 2, :].rearrange("p a c -> p (a c)"), ident_b[:, :])
                        mm.then_inc(row_scored, 1)
                    wait(pe, row_read, b * 24 + 24)
                with pe.Else():
                    pe.sem_inc(row_scored, 24)

            def batch(phase, b):
                for o in range(2):
                    wait(pe, read[o], jobs_before(phase, b, o))
                wait(pe, prep, prep_at(b, "shift"))
                row_maxima(b)
                for slot in range(SLOTS_PER_BATCH):
                    u, half = slot // 2, slot % 2
                    score(b, u, 2 * half)
                    score(b, u, 2 * half + 1)
                    if u > 0:
                        weigh(b, u - 1, half)
                    if slot == 0 and phase != "first":
                        turn_quad(b - 1, QUADS - 1)
                    if slot in (6, 10, 14):
                        turn_quad(b, (slot - 6) // 4)
                    for name, at in SLOT_OF.items():
                        if at == slot and name in PHASES[phase]:
                            run_job(phase, b, name)
                for half in range(2):
                    weigh(b, UNITS - 1, half)

            pe.wait_ge(constants, 5)
            mean("prologue", 0, 0)
            for j in range(8):
                turn("prologue", 0, 0, j)
            pe.wait_ge(small_loaded, 16 * 5)
            pe.wait_ge(banks_clear, 2)
            for k in range(4):
                rows = EXPERTS if k == 0 else P
                mm = pe.transpose(PV[1][:, k * P:k * P + rows], small_w[0:rows, k, :], ident[0:rows, 0:rows])
            mm.then_inc(small_turned, 1)
            pe.wait_ge(small_ready, 5)
            iterations(pe, batch)
            turn_quad(BATCHES - 1, QUADS - 1)
            for name in POST_JOBS:
                run_job("epilogue", BATCHES, name)

            pe.wait_ge(weights_loaded, 16 * 3)
            for n in range(WEIGHT_JOBS):
                bank = n % 2
                pe.wait_ge(read[bank], epilogue_end[bank] + n // 2)
                for i in range(4):
                    if n < EXPERTS // 4:
                        src = w13[:, 4 * n + i, :]
                    else:
                        r = 4 * (n - EXPERTS // 4) + i
                        src = w2n[:, 2 * r:2 * r + 2, :].rearrange("p a c -> p (a c)")
                    mm = pe.transpose(M[bank][:, i * P:(i + 1) * P], src, ident[:, :])
                mm.then_inc(written[bank], 1)

            def turn_x(s, u):
                if not isinstance(s, int) or s >= 2:
                    wait(pe, x_copied, s - 1)
                wait(pe, slots_loaded, 16 * (s + 1))
                for i in range(GROUP_OF):
                    mm = pe.transpose(S[:, u % 2, i * CAP:(i + 1) * CAP], slots_in[:, u % 4, i * REC:i * REC + DIM],
                                      ident[:, :])
                mm.then_inc(x_turned, 1)

            def up_step(s, u):
                if not isinstance(s, int) or s >= 2:
                    wait(pe, silu, 4 * s - 4)
                wait(pe, x_copied, s + 1)
                for i in range(GROUP_OF):
                    mm = pe.matmul(S[:, 2 + u % 2, i * P:(i + 1) * P], xeT[:, u % 2, i * CAP:(i + 1) * CAP],
                                   w13_flat[:, bass.ds((GROUP_OF * s + i) * P, P)], start=True, stop=True)
                mm.then_inc(up_done, 1)

            def turn_h(s, u):
                if not isinstance(s, int) or s >= 2:
                    wait(pe, h_copied, s - 1)
                wait(pe, silu, 4 * s + 4)
                for r in range(2):
                    mm = pe.transpose(PV[u % 2][:, r * P:(r + 1) * P], h[:, u % 2, r * P:(r + 1) * P], ident[:, :])
                mm.then_inc(h_turned, 1)

            def down_step(s, u):
                wait(pe, h_copied, s + 1)
                for r in range(2):
                    mm = pe.matmul(M[u % 2][:, 2 * r * DIM:(2 * r + 2) * DIM], ehT[:, u % 2, r * CAP:(r + 1) * CAP],
                                   w2bd_flat[:, bass.ds((2 * s + r) * 2 * DIM, 2 * DIM)], start=True, stop=True)
                mm.then_inc(down_done, 1)

            w13_flat = w13[:, :, :].rearrange("p e c -> p (e c)")
            w2bd_flat = w2bd.rearrange("p r c -> p (r c)")
            for o in range(2):
                pe.wait_ge(read[o], epilogue_end[o] + WEIGHT_JOBS // 2)
            pe.wait_ge(pv_read, QUADS * BATCHES)
            pe.wait_ge(exp_done, CHUNKS * BATCHES)

            def step(s, u):
                whole = not isinstance(s, int)
                if whole or s < STEPS:
                    turn_x(s, u)
                if whole or 0 <= s - 1 < STEPS:
                    up_step(s - 1, u - 1)
                if whole or 0 <= s - 2 < STEPS:
                    turn_h(s - 2, u - 2)
                if whole or 0 <= s - 3 < STEPS:
                    if whole or s - 3 >= 2:
                        wait(pe, weighted, s - 4)
                    down_step(s - 3, u - 3)

            for s in range(8):
                step(s, s)
            with pe.Fori(2, STEPS // 4) as r:
                for u in range(4):
                    step(4 * r + u, u + 4)
            for s in range(STEPS, STEPS + 3):
                step(s, s)

        @block.scalar
        def _(act):
            def norm_start(p):
                wait(act, post, post_at(p, "moments3"))
                nc.scalar.activation(log_v[:, :], moments[:, :, 1], ACT.Ln, bias=eps[:, :]).then_inc(act_post, 1)
                wait(act, act_post, act_post_at(p, "log"))
                nc.scalar.activation(rstd0[:, :], log_v[:, :], ACT.Exp, scale=-0.5).then_inc(act_post, 1)

            def exp_gate(phase, b, p):
                bank, n = job(phase, b, "gate")
                wait(act, written[bank], n + 1)
                nc.scalar.activation(eg[:, :], M[bank][:, :], ACT.Exp, scale=-1.0).then_inc(act_post, 1)

            def exp_logits(phase, b, p):
                bank, n = job(phase, b, "logits")
                wait(act, written[bank], n + 1)
                nc.scalar.activation(el[:, :], M[bank][:, 0:TILES * EXPERTS], ACT.Exp, scale=-1.0
                                     ).then_inc(read[bank], 1)

            def copy_quad(b, g):
                wait(act, unit_weighed, UNITS * b + 2 * g + 2)
                if not isinstance(b, int) or b > 0 or g > 0:
                    wait(act, quad_turned, QUADS * b + g)
                nc.scalar.copy(OT[:, :], PV[g % 2][:, :]).then_inc(quad_copied, 1)

            def batch(phase, b):
                wait(act, prep, prep_at(b, "shift"))
                for slot in range(SLOTS_PER_BATCH):
                    u = slot // 2
                    for i in range(2 * (slot % 2), 2 * (slot % 2) + 2):
                        n = QUAD * u + i
                        if i == 0 and (u >= 2 or not isinstance(b, int) or b > 0):
                            wait(act, unit_weighed, b * UNITS + u - 1)
                        wait(act, scored, b * CHUNKS + n + 1)
                        nc.scalar.activation(E[:, u % 2, i, :, :], S[:, 2 * (n % 2):2 * (n % 2) + 2, :], ACT.Exp,
                                             bias=shift[:, bass.ds(b, 1)]).then_inc(exp_done, 1)
                        if slot == 0 and i == 0 and phase != "first":
                            copy_quad(b - 1, QUADS - 1)
                        if slot in (6, 10, 14) and i == 0:
                            copy_quad(b, (slot - 6) // 4)
                    if slot == 0:
                        wait(act, unit_weighed, b * UNITS)
                        wait(act, x_loaded, 16 * (b + 1))
                        nc.scalar.copy(V[:, :, :, 0:HD],
                                       tokens_of(X, b).rearrange("p (i h d) -> p i h d", i=TILES, h=HEADS)
                                       ).then_inc(v_built, 1)
                    if phase != "first":
                        if slot == 2:
                            norm_start(b - 1)
                        if slot == SLOT_OF["gate"]:
                            exp_gate(phase, b, b - 1)
                        if slot == SLOT_OF["logits"]:
                            exp_logits(phase, b, b - 1)

            act.wait_ge(setup, SETUP)
            act.wait_ge(banks_clear, 2)
            iterations(act, batch)
            copy_quad(BATCHES - 1, QUADS - 1)
            norm_start(BATCHES - 1)
            exp_gate("epilogue", BATCHES, BATCHES - 1)
            exp_logits("epilogue", BATCHES, BATCHES - 1)

            for n in range(1, WEIGHT_JOBS, 2):
                act.wait_ge(written[1], epilogue_end[1] + n // 2 + 1)
                if n < EXPERTS // 4:
                    nc.scalar.copy(w13[:, 4 * n:4 * n + 4, :], M[1][:, :].rearrange("p (a c) -> p a c", a=4)
                                   ).then_inc(read[1], 1)
                else:
                    r = 4 * (n - EXPERTS // 4)
                    act.wait_ge(w2_cleared, 1)
                    src = M[1][:, :].rearrange("p (a c) -> p a c", a=4)
                    nc.scalar.copy(w2bd[0:FF, r:r + 4, 0:DIM], src[0:FF, :, :])
                    nc.scalar.copy(w2bd[FF:P, r:r + 4, DIM:2 * DIM], src[FF:P, :, :]).then_inc(read[1], 1)

            def copy_x(s, u):
                wait(act, x_turned, s + 1)
                if not isinstance(s, int) or s >= 2:
                    wait(act, up_done, s - 1)
                nc.scalar.copy(xeT[:, u % 2, :], S[:, u % 2, :]).then_inc(x_copied, 1)

            def exp_step(s, u):
                wait(act, up_done, s + 1)
                if not isinstance(s, int) or s >= 2:
                    wait(act, silu, 4 * s - 4)
                nc.scalar.activation(eh[:, u % 2, :, :], S[:, 2 + u % 2, :].rearrange(
                    "p (i c) -> p i c", i=GROUP_OF)[:, :, 0:FF], ACT.Exp, scale=-1.0).then_inc(exp_up, 1)

            def step(s, u):
                whole = not isinstance(s, int)
                if whole or s < STEPS:
                    copy_x(s, u)
                if whole or 0 <= s - 1 < STEPS:
                    exp_step(s - 1, u - 1)

            step(0, 0)
            step(1, 1)
            with act.Fori(1, STEPS // 2) as r:
                for u in range(2):
                    step(2 * r + u, u + 2)
            step(STEPS, STEPS)

            def last_norm(q):
                wait(act, fin, fin_at(q, "moments3"))
                nc.scalar.activation(log_v[:, :], moments[:, :, 1], ACT.Ln, bias=eps[:, :]).then_inc(act_fin, 1)
                wait(act, act_fin, 2 * q + 1)
                nc.scalar.activation(rstd0[:, :], log_v[:, :], ACT.Exp, scale=-0.5).then_inc(act_fin, 1)

            with act.Fori(0, BATCHES) as q:
                last_norm(q)

        @block.vector
        def _(dve):
            v = nc.vector

            def refine(step, after, ready):
                after("moments3")
                step("veps", v.tensor_scalar(veps[:, :], moments[:, :, 1], NORM_EPS, None, ALU.add))
                ready()
                step("r2", v.tensor_tensor(r2[:, :], rstd0[:, :], rstd0[:, :], ALU.mult))
                after("r2")
                step("vr2", v.tensor_tensor(r2[:, :], r2[:, :], veps[:, :], ALU.mult))
                after("vr2")
                step("corr", v.tensor_scalar(r2[:, :], r2[:, :], -0.5, 1.5, ALU.mult, ALU.add))
                after("corr")
                step("rstd", v.tensor_tensor(rstd[:, :], r2[:, :], rstd0[:, :], ALU.mult))
                after("rstd")

            def moments_of(step, after):
                for i in range(TILES):
                    step(f"stats{i}", v.bn_stats(stats[:, i, :], O[:, i, :]))
                for i in range(TILES):
                    after(f"stats{i}")
                    step(f"moments{i}", v.bn_aggr(moments[:, i, :], stats[:, i, :]))

            def leave(b, g):
                src = PV[g % 2][:, :].rearrange("p (i h c) -> p i h c", i=TILES, h=QUAD)
                wait(dve, quad_turned, QUADS * b + g + 1)
                wait(dve, pv_read, QUADS * b + g)
                v.reciprocal(rden[:, :, :], src[:, :, :, HD]).then_inc(pv_recip, 1)
                wait(dve, pv_recip, QUADS * b + g + 1)
                dst = O[:, :, g * QUAD * HD:(g + 1) * QUAD * HD].rearrange("p i (h d) -> p i h d", h=QUAD)
                v.tensor_tensor(dst, src[:, :, :, 0:HD], rden[:, :, :].unsqueeze(3).to_broadcast([P, TILES, QUAD, HD]),
                                ALU.mult).then_inc(pv_read, 1)

            def row_maxima(b):
                flag = dve.value_load(slow_flag[0:1, bass.ds(b, 1)], min_val=0, max_val=1)
                with dve.If(flag > 0):
                    for hd in range(HEADS):
                        wait(dve, row_scored, b * 24 + hd + 1)
                        v.tensor_reduce(row_max[:, hd, :], S[:, :, :], AX.X, ALU.max, negate=True).then_inc(row_read, 1)
                    wait(dve, row_read, b * 24 + HEADS)
                    wait(dve, row_parts, b * 6)
                    left_over = row_max
                    for k in range(PARTS):
                        col = AQ[:, :, :, ROWS + k].rearrange("p i h -> p h i")
                        v.tensor_copy(col, left_over[:, :, :]).then_inc(row_parts, 1)
                        wait(dve, row_parts, b * 6 + 2 * k + 1)
                        if k < PARTS - 1:
                            v.tensor_tensor(row_rest[:, :, :], left_over[:, :, :], col, ALU.subtract).then_inc(row_parts, 1)
                            wait(dve, row_parts, b * 6 + 2 * k + 2)
                            left_over = row_rest
                    Sb = S[:, 0, :].bitcast(BF16)
                    for q in range(HEADS // 2):
                        wait(dve, row_scored, b * 24 + HEADS + q + 1)
                        v.tensor_copy(LR[:, q, 1, :], Sb[:, 0:TOKENS]).then_inc(row_read, 1)
                    v.memset(AQ[:, :, :, ROWS:ROWS + PARTS], 0.0).then_inc(row_parts, 1)
                with dve.Else():
                    dve.sem_inc(row_read, 24)
                    dve.sem_inc(row_parts, 6)

            def operand(A, lo, hi):
                return A[:, :, :, lo:hi].rearrange("p i h c -> p (i h) c")

            def prep_parts(phase, b, q, step, after):
                bank, n = job(phase, b, "mean")
                wait(dve, written[bank], n + 1)
                wait(dve, x_loaded, 16 * (q + 1))
                v.tensor_tensor(xc[:, :].rearrange("p (i d) -> p i d", i=TILES),
                                tokens_of(X, q).rearrange("p (i d) -> p i d", i=TILES),
                                M[bank][:, 0:DIM].unsqueeze(1).to_broadcast([P, TILES, DIM]),
                                ALU.subtract).then_inc(read[bank], 1)
                wait(dve, read[bank], n + 1)
                x3 = xc[:, :].rearrange("p (g d) -> p g d", d=HD)
                r3 = rest[:, :].rearrange("p (g d) -> p g d", d=HD)
                step("high", v.tensor_copy(operand(AQ, 0, HD), x3))
                after("high")
                step("rest", v.tensor_tensor(r3, x3, operand(AQ, 0, HD), ALU.subtract))
                after("rest")
                step("middle", v.tensor_copy(operand(AQ, HD, 2 * HD), r3))
                after("middle")
                step("low", v.tensor_tensor(operand(AQ, 2 * HD, 3 * HD), r3, operand(AQ, HD, 2 * HD), ALU.subtract))

            def prep_rows(step, after):
                step("square", v.tensor_tensor(square[:, :], xc[:, :], xc[:, :], ALU.mult))
                after("square")
                step("norms", v.tensor_reduce(norms[:, :], square[:, :].rearrange("p (g d) -> p g d", d=HD), AX.X, ALU.add))
                after("norms")
                step("largest", v.tensor_reduce(largest[:, :], norms[:, :], AX.X, ALU.max))

                def repeat(part, times):
                    return operand(AQ, part * HD, (part + 1) * HD).unsqueeze(2).to_broadcast(
                        [P, TILES * HEADS, times, HD])

                def key_rows(lo, times):
                    return operand(AK, lo * HD, (lo + times) * HD).rearrange("p g (r d) -> p g r d", r=times)

                step("r24", v.tensor_copy(operand(AQ, 3 * HD, 5 * HD), operand(AQ, 0, 2 * HD)))
                step("r40", v.tensor_copy(operand(AQ, 5 * HD, 6 * HD), operand(AQ, 0, HD)))
                step("l0", v.tensor_copy(key_rows(0, 3), repeat(0, 3)))
                step("l24", v.tensor_copy(key_rows(3, 2), repeat(1, 2)))
                step("l40", v.tensor_copy(key_rows(5, 1), repeat(2, 1)))

            def prep_shift(q, step, after):
                wait(dve, all_reduced, q + 1)
                step("slow", v.tensor_scalar(slow_flag[:, bass.ds(q, 1)], largest_all[:, :], SHIFT_LIMIT, None, ALU.is_gt))
                step("neg_small", v.tensor_scalar(neg_small[:, :], largest_all[:, :], SHIFT_LIMIT, -1.0,
                                                  ALU.is_le, ALU.mult))
                after("neg_small")
                step("shift", v.tensor_tensor(shift[:, bass.ds(q, 1)], neg_small[:, :], largest_all[:, :], ALU.mult))

            def take_turned(phase, b, j):
                bank, n = job(phase, b, f"lr{j}")
                wait(dve, written[bank], n + 1)
                v.tensor_copy(LR[:, j, :, :].rearrange("p a t -> p (a t)"), Mb[bank]).then_inc(read[bank], 1)

            class Steps:
                def __init__(self, s, names, base):
                    self.s, self.names, self.base, self.order = s, names, base, 0

                def step(self, name, ins):
                    assert self.names[self.order] == name, (self.names[self.order], name)
                    self.order += 1
                    ins.then_inc(self.s, 1)

                def after(self, name):
                    wait(dve, self.s, self.base + self.names.index(name) + 1)

            def post_norm(p, t):
                t.step("y", v.tensor_tensor(O[:, :, :].rearrange("p i d -> p (i d)"), O[:, :, :].rearrange("p i d -> p (i d)"),
                                            tokens_of(X, p), ALU.add))
                t.after("y")
                moments_of(t.step, t.after)

            def post_x1(p, t):
                refine(t.step, t.after, lambda: wait(dve, act_post, act_post_at(p, "rstd0")))
                for i in range(TILES):
                    t.step(f"x1_{i}", v.tensor_scalar(x1[:, i, :], O[:, i, :], moments[:, i, 0:1], rstd[:, i:i + 1],
                                                      ALU.subtract, ALU.mult))

            def post_x1T(phase, b):
                bank, n = job(phase, b, "xt")
                wait(dve, written[bank], n + 1)
                v.tensor_copy(x1T[:, :], M[bank][:, :]).then_inc(read[bank], 1)

            def post_shared(phase, b, p, t):
                wait(dve, act_post, act_post_at(p, "exp_gate"))
                t.step("g1", v.tensor_scalar(sg[:, :], eg[:, :], 1.0, None, ALU.add))
                t.after("g1")
                t.step("grec", v.reciprocal(eg[:, :], sg[:, :]))
                t.after("grec")
                bank, n = job(phase, b, "gate")
                v.tensor_tensor(sg[:, :], M[bank][:, :], eg[:, :], ALU.mult).then_inc(read[bank], 1)
                wait(dve, read[bank], n + 1)
                bank, n = job(phase, b, "up")
                wait(dve, written[bank], n + 1)
                v.tensor_tensor(hT[:, :], M[bank][:, :], sg[:, :], ALU.mult).then_inc(read[bank], 1)

            def post_route(phase, b, p, t):
                bank, n = job(phase, b, "logits")
                wait(dve, read[bank], n + 1)
                t.step("s1", v.tensor_scalar(scores[:, :], el[:, :], 1.0, None, ALU.add))
                t.after("s1")
                t.step("scores", v.reciprocal(scores[:, :], scores[:, :]))
                t.after("scores")
                ie = lambda a: a[:, :].rearrange("p (i e) -> p i e", i=TILES)
                t.step("sfc", v.tensor_tensor(ie(sfc), ie(scores), bias[:, :].unsqueeze(1).to_broadcast([P, TILES, EXPERTS]),
                                              ALU.add))
                t.after("sfc")
                s8 = sfc[:, :].rearrange("p (g e) -> p g e", e=PER_GROUP)
                t.step("hi4", v.tensor_tensor(hi4[:, :, :], s8[:, :, 0:4], s8[:, :, 4:8], ALU.max))
                t.step("lo4", v.tensor_tensor(lo4[:, :, :], s8[:, :, 0:4], s8[:, :, 4:8], ALU.min))
                t.after("lo4")
                t.step("hi2", v.tensor_tensor(hi2[:, :, :], hi4[:, :, 0:2], hi4[:, :, 2:4], ALU.max))
                t.step("t2", v.tensor_tensor(t2[:, :, :], hi4[:, :, 0:2], hi4[:, :, 2:4], ALU.min))
                t.step("u2", v.tensor_tensor(u2[:, :, :], lo4[:, :, 0:2], lo4[:, :, 2:4], ALU.max))
                t.after("u2")
                t.step("lo2", v.tensor_tensor(lo2[:, :, :], t2[:, :, :], u2[:, :, :], ALU.max))
                t.step("hi1", v.tensor_tensor(hi1[:, :], hi2[:, :, 0], hi2[:, :, 1], ALU.max))
                t.step("t1", v.tensor_tensor(t1[:, :], hi2[:, :, 0], hi2[:, :, 1], ALU.min))
                t.after("lo2")
                t.step("u1", v.tensor_tensor(u1[:, :], lo2[:, :, 0], lo2[:, :, 1], ALU.max))
                t.after("u1")
                t.step("lo1", v.tensor_tensor(lo1[:, :], t1[:, :], u1[:, :], ALU.max))
                t.after("lo1")
                t.step("gs", v.tensor_tensor(gs[:, :, :].rearrange("p i g -> p (i g)"), hi1[:, :], lo1[:, :], ALU.add))
                t.after("gs")
                full = [P, TILES, GROUPS, GROUPS]
                other = gs[:, :, :].unsqueeze(2).to_broadcast(full)
                own = gs[:, :, :].unsqueeze(3).to_broadcast(full)
                t.step("ge", v.tensor_tensor(ge[:, :, :, :], other, own, ALU.is_ge))
                t.step("gt", v.tensor_tensor(gt[:, :, :, :], other, own, ALU.is_gt))
                t.after("ge")
                t.step("geL", v.tensor_tensor(ge[:, :, :, :], ge[:, :, :, :], lower[:, :, :].unsqueeze(1).to_broadcast(full),
                                              ALU.mult))
                t.after("geL")
                t.step("beats", v.tensor_tensor(gt[:, :, :, :], ge[:, :, :, :], gt[:, :, :, :], ALU.max))
                t.after("beats")
                t.step("rank", v.tensor_reduce(rank[:, :], gt[:, :, :, :].rearrange("p i a c -> p (i a) c"), AX.X, ALU.add))
                t.after("rank")
                t.step("keep", v.tensor_scalar(keep[:, :], rank[:, :], float(TOP_GROUPS), None, ALU.is_lt))
                t.after("keep")
                t.step("tmp", v.tensor_tensor(tmp[:, :].rearrange("p (g e) -> p g e", e=PER_GROUP), s8,
                                              keep[:, :].unsqueeze(2).to_broadcast([P, TILES * GROUPS, PER_GROUP]), ALU.mult))
                t.after("tmp")
                t.step("tmp0", v.tensor_scalar(tmp[:, :], tmp[:, :], 0.0, None, ALU.add))
                t.after("tmp0")
                for i in range(TILES):
                    t.step(f"top{i}", v.max(top[:, i, :], ie(tmp)[:, i, :]))
                for i in range(TILES):
                    t.after(f"top{i}")
                    t.step(f"rest{i}", v.match_replace(ie(left)[:, i, :], top[:, i, :], ie(tmp)[:, i, :], BELOW_ALL))
                t.after("rest3")
                t.step("mask", v.tensor_tensor(mask[:, :], left[:, :], tmp[:, :], ALU.not_equal))
                t.after("mask")
                t.step("maskb", v.tensor_copy(mask_b[:, :, :].rearrange("p i e -> p (i e)"), mask[:, :]))

            def post_shared_out(phase, b, p):
                bank, n = job(phase, b, "down")
                wait(dve, written[bank], n + 1)
                v.tensor_tensor(tokens_of(Z, p), M[bank][:, :], x1[:, :, :].rearrange("p i d -> p (i d)"), ALU.add
                                ).then_inc(read[bank], 1)

            def post_record(p, t):
                ie = lambda a: a[:, :].rearrange("p (i e) -> p i e", i=TILES)
                t.step("wsel", v.tensor_tensor(wsel[:, :], mask[:, :], scores[:, :], ALU.mult))
                t.after("wsel")
                t.step("wsum", v.tensor_reduce(wsum[:, :], ie(wsel), AX.X, ALU.add))
                t.after("wsum")
                t.step("wsum2", v.tensor_scalar(wsum[:, :], wsum[:, :], 1e-20, 1.0 / SCALE, ALU.add, ALU.mult))
                t.after("wsum2")
                t.step("wrec", v.reciprocal(wsum[:, :], wsum[:, :]))
                t.after("wrec")
                wait(dve, record_free, p + 1)
                t.step("recw", v.tensor_tensor(rec[:, :, W_COL:W_COL + EXPERTS], ie(scores),
                                               wsum[:, :].unsqueeze(2).to_broadcast([P, TILES, EXPERTS]), ALU.mult))
                t.step("recx", v.tensor_copy(rec[:, :, 0:DIM], x1[:, :, :]))
                t.step("rectok", v.tensor_copy(rec[:, :, TOK_COL], token[:, :]))
                t.after("rectok")
                t.step("tokens", v.tensor_scalar(token[:, :], token[:, :], float(TOKENS), None, ALU.add))

            def post_pos(phase, b, p, t):
                bank, n = job(phase, b, "pos")
                ie = lambda a: a[:, :].rearrange("p (i e) -> p i e", i=TILES)
                wait(dve, written[bank], n + 1)
                v.tensor_tensor(ie(pos), M[bank][:, 0:TILES * EXPERTS].rearrange("p (i e) -> p i e", i=TILES),
                                count[:, :].unsqueeze(1).to_broadcast([P, TILES, EXPERTS]), ALU.add).then_inc(read[bank], 1)
                wait(dve, read[bank], n + 1)
                t.step("kept", v.scalar_tensor_tensor(kept[:, :], pos[:, :], float(CAP), mask[:, :], ALU.is_lt, ALU.mult))
                t.step("room", v.tensor_tensor(ie(key), slot_base[:, :].unsqueeze(1).to_broadcast([P, TILES, EXPERTS]),
                                               ie(pos), ALU.subtract))
                t.after("room")
                t.step("key", v.tensor_tensor(key[:, :], key[:, :], kept[:, :], ALU.mult))
                t.after("key")
                for i in range(TILES):
                    t.step(f"slots{i}", v.max(best[:, i, :], ie(key)[:, i, :]))
                t.after("slots3")
                t.step("index", v.tensor_scalar(index[:, :], best[:, :, :].rearrange("p i k -> p (i k)"), -1.0,
                                                float(SLOTS), ALU.mult, ALU.add))

            def post_totals(phase, b, p):
                bank, n = job(phase, b, "totals")
                wait(dve, written[bank], n + 1)
                v.tensor_tensor(count[:, :], M[bank][:, 0:EXPERTS], count[:, :], ALU.add).then_inc(read[bank], 1)

            def batch(phase, b):
                p, q = b - 1, b + 1
                t = Steps(post, POST_STEPS, p * len(POST_STEPS))
                w = Steps(prep, PREP_STEPS, q * len(PREP_STEPS))
                with_post, with_prep = phase != "first", phase != "last"
                row_maxima(b)
                if with_post:
                    leave(p, QUADS - 1)
                    wait(dve, pv_read, QUADS * b)
                    post_norm(p, t)
                if with_prep:
                    prep_parts(phase, b, q, w.step, w.after)
                if with_post:
                    post_x1(p, t)
                    post_x1T(phase, b)
                if with_prep:
                    prep_rows(w.step, w.after)
                if with_post:
                    post_shared(phase, b, p, t)
                    post_route(phase, b, p, t)
                    post_shared_out(phase, b, p)
                leave(b, 0)
                if with_post:
                    post_record(p, t)
                if with_prep:
                    take_turned(phase, b, 0)
                if with_post:
                    post_pos(phase, b, p, t)
                if with_prep:
                    take_turned(phase, b, 1)
                if with_post:
                    post_totals(phase, b, p)
                if with_prep:
                    take_turned(phase, b, 2)
                leave(b, 1)
                if with_prep:
                    for j in range(3, 6):
                        take_turned(phase, b, j)
                    prep_shift(q, w.step, w.after)
                leave(b, 2)
                if with_prep:
                    for j in range(6, 8):
                        take_turned(phase, b, j)
                    assert w.order == len(PREP_STEPS)
                if with_post:
                    assert t.order == len(POST_STEPS)

            v.memset(PV[0][:, :], 0.0).then_inc(banks_clear, 1)
            v.memset(PV[1][:, :], 0.0).then_inc(banks_clear, 1)
            dve.wait_ge(setup, SETUP)
            v.tensor_copy(slot_base[:, :], slot_base_i[:, :]).then_inc(small_ready, 1)
            v.tensor_copy(token[:, :], token_i[:, :]).then_inc(small_ready, 1)
            v.tensor_copy(blank[:, TOK_COL:REC], blank_i[:, :]).then_inc(small_ready, 1)
            dve.wait_ge(constants, 5)
            w = Steps(prep, PREP_STEPS, 0)
            prep_parts("prologue", 0, 0, w.step, w.after)
            prep_rows(w.step, w.after)
            for j in range(8):
                take_turned("prologue", 0, j)
            prep_shift(0, w.step, w.after)
            dve.wait_ge(small_turned, 1)
            v.tensor_copy(small_T[:, 0, 0:EXPERTS], PV[1][:, 0:EXPERTS]).then_inc(small_ready, 1)
            v.tensor_copy(small_T[:, 1:4, :], PV[1][:, P:4 * P].rearrange("p (a c) -> p a c", a=3)).then_inc(small_ready, 1)
            dve.wait_ge(small_loaded, 16 * 5)
            dve.wait_ge(small_ready, 5)
            iterations(dve, batch)

            p = BATCHES - 1
            t = Steps(post, POST_STEPS, p * len(POST_STEPS))
            leave(p, QUADS - 1)
            wait(dve, pv_read, QUADS * BATCHES)
            post_norm(p, t)
            post_x1(p, t)
            post_x1T("epilogue", BATCHES)
            post_shared("epilogue", BATCHES, p, t)
            post_route("epilogue", BATCHES, p, t)
            post_shared_out("epilogue", BATCHES, p)
            post_record(p, t)
            post_pos("epilogue", BATCHES, p, t)
            post_totals("epilogue", BATCHES, p)
            v.memset(w2bd, 0.0).then_inc(w2_cleared, 1)
            dve.wait_ge(w2_cleared, 1)
            for n in range(0, WEIGHT_JOBS, 2):
                dve.wait_ge(written[0], epilogue_end[0] + n // 2 + 1)
                src = M[0][:, :].rearrange("p (a c) -> p a c", a=4)
                if n < EXPERTS // 4:
                    v.tensor_copy(w13[:, 4 * n:4 * n + 4, :], src).then_inc(read[0], 1)
                else:
                    r = 4 * (n - EXPERTS // 4)
                    v.tensor_copy(w2bd[0:FF, r:r + 4, 0:DIM], src[0:FF, :, :])
                    v.tensor_copy(w2bd[FF:P, r:r + 4, DIM:2 * DIM], src[FF:P, :, :]).then_inc(read[0], 1)

            def silu_step(s, u):
                up_ = S[:, 2 + u % 2, :].rearrange("p (i c) -> p i c", i=GROUP_OF)
                e = eh[:, u % 2, :, :]
                wait(dve, exp_up, s + 1)
                if not isinstance(s, int) or s >= 2:
                    wait(dve, h_turned, s - 1)
                v.tensor_scalar(e, e, 1.0, None, ALU.add).then_inc(silu, 1)
                wait(dve, silu, 4 * s + 1)
                v.reciprocal(e, e).then_inc(silu, 1)
                wait(dve, silu, 4 * s + 2)
                v.tensor_tensor(e, up_[:, :, 0:FF], e, ALU.mult).then_inc(silu, 1)
                wait(dve, silu, 4 * s + 3)
                v.tensor_tensor(h[:, u % 2, :].rearrange("p (i f) -> p i f", i=GROUP_OF), up_[:, :, FF:2 * FF], e,
                                ALU.mult).then_inc(silu, 1)

            def copy_h(s, u):
                wait(dve, h_turned, s + 1)
                if not isinstance(s, int) or s >= 2:
                    wait(dve, down_done, s - 1)
                v.tensor_copy(ehT[:, u % 2, :], PV[u % 2][:, 0:2 * CAP]).then_inc(h_copied, 1)

            def weigh_step(s, u):
                wait(dve, down_done, s + 1)
                if not isinstance(s, int) or s >= 2:
                    for j in range(SUMS):
                        wait(dve, added[j], 16 * (s - 1))
                for i in range(GROUP_OF):
                    last = v.tensor_scalar(ye[:, u % 2, i, :], M[u % 2][:, i * DIM:(i + 1) * DIM],
                                           slots_in[:, u % 4, bass.ds(i * REC + W_COL + GROUP_OF * s + i, 1)], None,
                                           ALU.mult)
                last.then_inc(weighted, 1)
                v.tensor_copy(target[:, u % 2, :], slots_in[:, u % 4, TOK_COL::REC]).then_inc(aimed, 1)

            def step(s, u):
                whole = not isinstance(s, int)
                if whole or 0 <= s - 1 < STEPS:
                    silu_step(s - 1, u - 1)
                if whole or 0 <= s - 2 < STEPS:
                    copy_h(s - 2, u - 2)
                if whole or 0 <= s - 3 < STEPS:
                    weigh_step(s - 3, u - 3)

            for s in range(1, 8):
                step(s, s)
            with dve.Fori(2, STEPS // 4) as r:
                for u in range(4):
                    step(4 * r + u, u + 4)
            for s in range(STEPS, STEPS + 3):
                step(s, s)

            def last_norm(q, even, u):
                t = Steps(fin, FIN_STEPS, q * len(FIN_STEPS))
                wait(dve, parts_loaded[u], 8 * even * SUMS + 16 * SUMS)
                a, c = square, rest
                t.step("a01", v.tensor_tensor(a[:, :], sums_in[:, SUMS * u, :], sums_in[:, SUMS * u + 1, :], ALU.add))
                t.step("a23", v.tensor_tensor(c[:, :], sums_in[:, SUMS * u + 2, :], sums_in[:, SUMS * u + 3, :], ALU.add))
                t.after("a23")
                t.step("sum", v.tensor_tensor(a[:, :], a[:, :], c[:, :], ALU.add))
                t.after("sum")
                t.step("y", v.tensor_tensor(O[:, :, :].rearrange("p i d -> p (i d)"), a[:, :], tokens_of(Z, q), ALU.add))
                t.after("y")
                moments_of(t.step, t.after)
                refine(t.step, t.after, lambda: wait(dve, act_fin, 2 * q + 2))
                if not isinstance(even, int) or even > 0:
                    wait(dve, stored[u], 8 * even)
                for i in range(TILES):
                    t.step(f"out{i}", v.tensor_scalar(normed[:, u, i * DIM:(i + 1) * DIM], O[:, i, :], moments[:, i, 0:1],
                                                      rstd[:, i:i + 1], ALU.subtract, ALU.mult))

            for u in range(2):
                last_norm(u, 0, u)
            with dve.Fori(1, BATCHES // 2) as r:
                for u in range(2):
                    last_norm(2 * r + u, 2 * r, u)


_INS = ["L0_attn_x", "L0_ffn_gate_weight", "L0_ffn_e_bias", "L0_ffn_w1", "L0_ffn_w2", "L0_ffn_w3",
        "L0_ffn_shared_gate", "L0_ffn_shared_up", "L0_ffn_shared_down"]


def kernel(**inputs):
    import numpy as np
    import concourse.bacc as bacc
    from concourse.bass_utils import run_bass_kernel_spmd

    nc = bacc.Bacc("TRN2", target_bir_lowering=False, num_devices=1)
    arrays, args = {}, []
    for name in _INS:
        a = np.ascontiguousarray(inputs[name])
        arrays[f"{name}_dram"] = a
        args.append(nc.dram_tensor(f"{name}_dram", a.shape, mybir.dt.from_np(a.dtype), kind="ExternalInput").ap())
    args.append(nc.dram_tensor("out_dram", (BATCHES, TOKENS, DIM), F32, kind="ExternalOutput").ap())
    post_norm_block(nc, *args)
    return run_bass_kernel_spmd(nc, [arrays], core_ids=[0]).results[0]["out_dram"]
```

```python
from contextlib import ExitStack

import concourse.bass as bass
from concourse import mybir

ALU = mybir.AluOpType
ACT = mybir.ActivationFunctionType
AX = mybir.AxisListType
F32 = mybir.dt.float32
BF16 = mybir.dt.bfloat16
I32 = mybir.dt.int32
U32 = mybir.dt.uint32

P = 128
BATCHES, TOKENS, DIM = 8, 512, 128
HEADS = 16
HD = DIM // HEADS
TILES = TOKENS // P
VCOLS = HD + 1
PARTS = 3
ROWS = 6 * HD
HEAD_ROWS = 64
SHIFT_LIMIT = 60.0

EXPERTS, TOP, GROUPS, TOP_GROUPS = 64, 8, 8, 4
PER_GROUP = EXPERTS // GROUPS
CAP = 128
SLOTS = EXPERTS * CAP
FF = 64
SCALE = 2.5
NORM_EPS = 1e-5
ALL_TOKENS = BATCHES * TOKENS
REC = DIM + EXPERTS + 1
W_COL, TOK_COL = DIM, DIM + EXPERTS
SUMS = 4
ACC_ROWS = ALL_TOKENS + CAP
GROUP_OF = 4
STEPS = EXPERTS // GROUP_OF
BELOW_ALL = -1e30
LARGEST_LOG = 1e19

QUAD = 4
QUADS = HEADS // QUAD
UNITS = 2 * QUADS
SLOTS_PER_BATCH = 2 * UNITS
CHUNKS = 2 * HEADS

BANK = {"mean": 0, "lr0": 0, "lr1": 1, "xt": 0, "gate": 1, "logits": 0, "up": 0, "lr2": 1, "down": 0, "lr3": 1,
        "pos": 0, "lr4": 1, "totals": 0, "lr5": 1, "lr6": 0, "lr7": 1}
SLOT_OF = {"mean": 0, "lr0": 4, "lr1": 5, "xt": 5, "gate": 6, "logits": 6, "up": 7, "lr2": 9, "down": 9, "lr3": 12,
           "pos": 13, "lr4": 13, "totals": 14, "lr5": 14, "lr6": 15, "lr7": 15}
COPY_SLOT = {0: 7, 1: 10, 2: 14, 3: 2}
TURN_SLOT = {0: 8, 1: 10, 2: 14, 3: 2}
PREP_JOBS = ["mean"] + [f"lr{j}" for j in range(8)]
POST_JOBS = ["xt", "gate", "logits", "up", "down", "pos", "totals"]
WEIGHT_JOBS = EXPERTS // 4 + EXPERTS // 8
PHASES = {"prologue": PREP_JOBS, "first": PREP_JOBS, "mid": list(SLOT_OF), "last": POST_JOBS, "epilogue": POST_JOBS}
RUNS = {"prologue": 1, "first": 1, "mid": BATCHES - 2, "last": 1, "epilogue": 1}

PREP_STEPS = ["high", "rest", "middle", "low", "square", "norms", "largest",
              "r24", "r40", "l0", "l24", "l40", "slow", "neg_small", "shift"]
POST_STEPS = (["y"] + [f"stats{i}" for i in range(4)] + [f"moments{i}" for i in range(4)]
              + ["veps", "r2", "vr2", "corr", "rstd"] + [f"x1_{i}" for i in range(4)]
              + ["g1", "s1", "scores", "sfc", "hi4", "lo4", "hi2", "t2", "u2", "lo2", "hi1", "t1", "u1",
                 "lo1", "gs", "ge", "gt", "geL", "beats", "rank", "keep", "tmp", "tmp0"]
              + [f"top{i}" for i in range(4)] + [f"rest{i}" for i in range(4)]
              + ["mask", "maskb", "wsel", "wsum", "wsum2", "wrec", "recw",
                 "kept", "room", "key"] + [f"slots{i}" for i in range(4)] + ["index"])
ACT_POST_STEPS = ["log", "rstd0", "exp_gate", "gate_log", "gate_sigmoid"]
SUM_STEPS = ["a01", "a23", "sum", "y"] + [f"stats{i}" for i in range(4)] + [f"moments{i}" for i in range(4)]
OUT_STEPS = ["veps", "r2", "vr2", "corr", "rstd"] + [f"out{i}" for i in range(4)]


def post_norm_block(nc, x, gate_w, e_bias, w1, w2, w3, s_gate, s_up, s_down, out):
    with ExitStack() as ctx:
        def sb(name, shape, dt=F32):
            return ctx.enter_context(nc.sbuf_tensor(name, shape, dt))

        def psum(name, shape, dt=F32):
            return ctx.enter_context(nc.psum_tensor(name, shape, dt))

        def sem(name):
            return ctx.enter_context(nc.semaphore(name))

        records = nc.dram_tensor("records", (SLOTS, REC), F32, kind="Internal").ap()
        sums = [nc.dram_tensor(f"sums{j}", (ACC_ROWS, DIM), F32, kind="Internal").ap() for j in range(SUMS)]

        ident = sb("ident", [P, P])
        ident_b = sb("ident_b", [P, P], BF16)
        mean_w = sb("mean_w", [P, P])
        before_b = sb("before_b", [P, P], BF16)
        ones_b = sb("ones_b", [P, P], BF16)
        lower = sb("lower", [P, GROUPS, GROUPS])
        slot_base_i = sb("slot_base_i", [P, EXPERTS], I32)
        slot_base = sb("slot_base", [P, EXPERTS])
        token_i = sb("token_i", [P, TILES], I32)
        token = sb("token", [P, TILES])
        eps = sb("eps", [P, 1])
        blank_i = sb("blank_i", [P, 1], I32)
        blank = sb("blank", [P, REC])
        bias = sb("bias", [P, EXPERTS])
        small_w = sb("small_w", [P, 4, P])
        small_T = sb("small_T", [P, 4, P])
        w13 = sb("w13", [P, EXPERTS, P])
        w2n = sb("w2n", [P, EXPERTS, FF])
        X = sb("X", [P, BATCHES * TILES * DIM])
        V = sb("V", [P, TILES, HEADS, VCOLS])
        centred = sb("centred", [P, 3, TILES * DIM])
        xc, rest, square = (centred[:, k, :] for k in range(3))
        norms = sb("norms", [P, TILES * HEADS])
        largest = sb("largest", [P, 1])
        largest_all = sb("largest_all", [P, 1])
        slow_flag = sb("slow_flag", [P, BATCHES], I32)
        neg_small = sb("neg_small", [P, 1])
        shift = sb("shift", [P, BATCHES])
        AK = sb("AK", [P, TILES, HEADS, HEAD_ROWS], BF16)
        AQ = sb("AQ", [P, TILES, HEADS, HEAD_ROWS], BF16)
        LR = sb("LR", [P, HEADS // 2, 2, TOKENS], BF16)
        E = sb("E", [P, 2, QUAD, 2, TOKENS])
        OT = sb("OT", [P, TOKENS])
        rden = sb("rden", [P, TILES, QUAD])
        O = sb("O", [P, TILES, DIM])
        row_max = sb("row_max", [P, HEADS, TILES])
        row_rest = sb("row_rest", [P, HEADS, TILES])
        stats = sb("stats", [P, TILES, 6])
        moments = sb("moments", [P, TILES, 2])
        log_v = sb("log_v", [P, TILES])
        rstd0 = sb("rstd0", [P, TILES])
        veps = sb("veps", [P, TILES])
        r2 = sb("r2", [P, TILES])
        rstd = sb("rstd", [P, TILES])
        x1 = sb("x1", [P, TILES, DIM])
        x1T = sb("x1T", [P, TOKENS])
        eg = sb("eg", [P, TOKENS])
        sg = sb("sg", [P, TOKENS])
        hT = sb("hT", [P, TOKENS])
        el = sb("el", [P, TILES * EXPERTS])
        scores = sb("scores", [P, TILES * EXPERTS])
        sfc = sb("sfc", [P, TILES * EXPERTS])
        hi4 = sb("hi4", [P, 32, 4])
        lo4 = sb("lo4", [P, 32, 4])
        hi2 = sb("hi2", [P, 32, 2])
        t2 = sb("t2", [P, 32, 2])
        u2 = sb("u2", [P, 32, 2])
        lo2 = sb("lo2", [P, 32, 2])
        hi1 = sb("hi1", [P, 32])
        t1 = sb("t1", [P, 32])
        u1 = sb("u1", [P, 32])
        lo1 = sb("lo1", [P, 32])
        gs = sb("gs", [P, TILES, GROUPS])
        ge = sb("ge", [P, TILES, GROUPS, GROUPS])
        gt = sb("gt", [P, TILES, GROUPS, GROUPS])
        rank = sb("rank", [P, TILES * GROUPS])
        keep = sb("keep", [P, TILES * GROUPS])
        tmp = sb("tmp", [P, TILES * EXPERTS])
        top = sb("top", [P, TILES, 8])
        left = sb("left", [P, TILES * EXPERTS])
        mask = sb("mask", [P, TILES * EXPERTS])
        mask_b = sb("mask_b", [P, TILES, EXPERTS], BF16)
        wsel = sb("wsel", [P, TILES * EXPERTS])
        wsum = sb("wsum", [P, TILES])
        count = sb("count", [P, EXPERTS])
        pos = sb("pos", [P, TILES * EXPERTS])
        kept = sb("kept", [P, TILES * EXPERTS])
        key = sb("key", [P, TILES * EXPERTS])
        best = sb("best", [P, TILES, 8])
        index = sb("index", [P, TILES * 8], U32)
        rec = sb("rec", [P, TILES, REC])
        Z = sb("Z", [P, BATCHES * TILES * DIM])
        w2bd = E[:, :, :, :, :].rearrange("p a b c d -> p (a b c d)").rearrange("p (r c) -> p r c", c=2 * DIM)
        free_f32 = AK[:, :, :, :].rearrange("p a b c -> p (a b c)").bitcast(F32)
        slots_flat = X[:, 0:4 * GROUP_OF * REC]
        slots_in = X[:, 0:4 * GROUP_OF * REC].rearrange("p (s r) -> p s r", s=4)
        eh = X[:, 4 * GROUP_OF * REC:4 * GROUP_OF * REC + 2 * GROUP_OF * FF].rearrange(
            "p (s i f) -> p s i f", s=2, i=GROUP_OF)
        xeT = free_f32[:, 0:2 * GROUP_OF * CAP].rearrange("p (s c) -> p s c", s=2)
        h = free_f32[:, 8 * CAP:8 * CAP + 8 * FF].rearrange("p (s f) -> p s f", s=2)
        ehT = free_f32[:, 8 * CAP + 8 * FF:12 * CAP + 8 * FF].rearrange("p (s c) -> p s c", s=2)
        ye = centred[:, 0:2, :].rearrange("p s (i d) -> p s i d", i=GROUP_OF)
        weight = sb("weight", [P, 4, GROUP_OF])
        number = sb("number", [P, 4, GROUP_OF])
        target = sb("target", [P, 2, GROUP_OF], U32)
        last_y = [O, x1]
        last_stats = sb("last_stats", [P, 2, TILES, 6])
        last_moments = sb("last_moments", [P, 2, TILES, 2])
        last_log = sb("last_log", [P, 2, TILES])
        last_rstd0 = sb("last_rstd0", [P, 2, TILES])
        last_rstd = sb("last_rstd", [P, 2, TILES])
        sums_in = LR[:, :, :, :].rearrange("p a b c -> p (a b c)").bitcast(F32).rearrange("p (s t) -> p s t", s=8)
        normed = AQ[:, :, :, :].rearrange("p a b c -> p (a b c)").bitcast(F32).rearrange("p (s t) -> p s t", s=4)

        S = psum("S", [P, 4, 512])
        PV = [psum(f"PV{o}", [P, 512]) for o in range(2)]
        M = [psum(f"M{o}", [P, 512]) for o in range(2)]
        Mb = [m[:, :].bitcast(BF16) for m in M]

        setup = sem("setup")
        constants = sem("constants")
        x_loaded = sem("x_loaded")
        small_loaded = sem("small_loaded")
        small_turned = sem("small_turned")
        small_ready = sem("small_ready")
        weights_loaded = sem("weights_loaded")
        records_blank = sem("records_blank")
        dram_blank = sem("dram_blank")
        written = [sem(f"written{o}") for o in range(2)]
        read = [sem(f"read{o}") for o in range(2)]
        prep = sem("prep")
        all_reduced = sem("all_reduced")
        scored = sem("scored")
        exp_done = sem("exp_done")
        unit_weighed = sem("unit_weighed")
        quad_copied = sem("quad_copied")
        quad_turned = sem("quad_turned")
        banks_clear = sem("banks_clear")
        pv_recip = sem("pv_recip")
        pv_read = sem("pv_read")
        v_built = sem("v_built")
        row_scored = sem("row_scored")
        row_read = sem("row_read")
        row_parts = sem("row_parts")
        post = sem("post")
        act_post = sem("act_post")
        scattered = sem("scattered")
        record_free = sem("record_free")
        record = sem("record")
        w2_cleared = sem("w2_cleared")
        w2_ready = sem("w2_ready")
        slots_loaded = sem("slots_loaded")
        x_turned = sem("x_turned")
        x_copied = sem("x_copied")
        up_done = sem("up_done")
        exp_up = sem("exp_up")
        silu = sem("silu")
        sigmoid = sem("sigmoid")
        h_turned = sem("h_turned")
        h_copied = sem("h_copied")
        down_done = sem("down_done")
        weighted = sem("weighted")
        taken = sem("taken")
        added = [sem(f"added{j}") for j in range(SUMS)]
        parts_loaded = [sem(f"parts_loaded{j}") for j in range(2)]
        summed = sem("summed")
        normed_out = sem("normed_out")
        act_fin = sem("act_fin")
        stored = [sem(f"stored{j}") for j in range(2)]
        carrier = sem("carrier")

        block = ctx.enter_context(nc.Block())

        def wait(eng, s, value):
            if isinstance(value, int):
                if value > 0:
                    eng.wait_ge(s, value)
            else:
                eng.wait_ge(s, value)
                eng.sem_inc(carrier, 1)

        def jobs_before(phase, b, bank):
            n = 0
            for name, jobs in PHASES.items():
                here = sum(BANK[j] == bank for j in jobs)
                if name == phase:
                    return n + (here * (b - 1) if name == "mid" else 0)
                n += here * RUNS[name]

        def job(phase, b, name):
            bank = BANK[name]
            here = [j for j in PHASES[phase] if BANK[j] == bank]
            return bank, jobs_before(phase, b, bank) + here.index(name)

        epilogue_end = [jobs_before("epilogue", 0, o) + sum(BANK[j] == o for j in POST_JOBS) for o in range(2)]

        def prep_at(q, step):
            return q * len(PREP_STEPS) + PREP_STEPS.index(step) + 1

        def post_at(p, step):
            return p * len(POST_STEPS) + POST_STEPS.index(step) + 1

        def act_post_at(p, step):
            return p * len(ACT_POST_STEPS) + ACT_POST_STEPS.index(step) + 1

        def sum_at(q, step):
            return q * len(SUM_STEPS) + SUM_STEPS.index(step) + 1

        def out_at(q, step):
            return q * len(OUT_STEPS) + OUT_STEPS.index(step) + 1

        def tokens_of(t, q, i=0, n=TILES):
            return t[:, bass.ds(q * TILES * DIM + i * DIM, n * DIM)]

        def iterations(eng, body):
            body("first", 0)
            with eng.Fori(1, BATCHES - 1) as b:
                body("mid", b)
            body("last", BATCHES - 1)

        SETUP = 16

        @block.sync
        def _(sp):
            for q in range(BATCHES):
                if q > 0:
                    sp.wait_ge(x_loaded, 16 * q)
                sp.dma_start(tokens_of(X, q).rearrange("p (i d) -> p i d", i=TILES),
                             x[q].rearrange("(i p) d -> p i d", p=P)).then_inc(x_loaded, 16)
                if q == 0:
                    sp.dma_start(small_w[0:EXPERTS, 0, :], gate_w).then_inc(small_loaded, 16)
                    sp.dma_start(small_w[:, 1, :], s_gate).then_inc(small_loaded, 16)
                    sp.dma_start(small_w[:, 2, :], s_up).then_inc(small_loaded, 16)
                    sp.dma_start(small_w[:, 3, :], s_down).then_inc(small_loaded, 16)
                    sp.dma_start(bias[:, :], e_bias.rearrange("(a e) -> a e", a=1).to_broadcast([P, EXPERTS])
                                 ).then_inc(small_loaded, 16)
            sp.wait_ge(setup, SETUP)
            sp.wait_ge(small_ready, 3)
            sp.dma_start(records.rearrange("(e c) r -> c e r", c=CAP),
                         blank[:, :].unsqueeze(1).to_broadcast([P, EXPERTS, REC])).then_inc(records_blank, 16)
            for j in range(SUMS):
                sp.dma_start(sums[j].rearrange("(p r) d -> p r d", p=P),
                             blank[:, 0:DIM].unsqueeze(1).to_broadcast([P, ACC_ROWS // P, DIM])
                             ).then_inc(dram_blank, 16)
            sp.dma_start(w13[0:FF, :, :], w1.rearrange("e f h -> f e h")).then_inc(weights_loaded, 16)
            sp.dma_start(w13[FF:P, :, :], w3.rearrange("e f h -> f e h")).then_inc(weights_loaded, 16)
            sp.dma_start(w2n[:, :, :], w2.rearrange("e h f -> h e f")).then_inc(weights_loaded, 16)
            sp.wait_ge(scattered, 16 * BATCHES * TILES * TOP)

            def load_slots(s, u):
                if not isinstance(s, int) or s >= 4:
                    wait(sp, x_turned, s - 3)
                    wait(sp, taken, s - 3)
                if not isinstance(s, int) or s >= 1:
                    wait(sp, slots_loaded, 16 * s)
                sp.dma_start(slots_in[:, u, :].rearrange("p (i r) -> p i r", i=GROUP_OF),
                             records[bass.ds(s * GROUP_OF * CAP, GROUP_OF * CAP), :].rearrange("(i c) r -> c i r", c=CAP)
                             ).then_inc(slots_loaded, 16)

            for s in range(4):
                load_slots(s, s)
            with sp.Fori(1, STEPS // 4) as r:
                for u in range(4):
                    load_slots(4 * r + u, u)

            for j in range(SUMS):
                sp.wait_ge(added[j], 16 * STEPS)

            def load_parts(q, u):
                if not isinstance(q, int) or q >= 2:
                    wait(sp, summed, sum_at(q - 2, "a23"))
                for j in range(SUMS):
                    sp.dma_start(sums_in[:, SUMS * u + j, :].rearrange("p (i d) -> p i d", i=TILES),
                                 sums[j][bass.ds(q * TOKENS, TOKENS), :].rearrange("(i p) d -> p i d", p=P)
                                 ).then_inc(parts_loaded[u], 16)

            def store(q, u):
                wait(sp, normed_out, out_at(q, "out3"))
                sp.dma_start(out[bass.ds(q, 1)].rearrange("a (i p) d -> p (a i) d", p=P),
                             normed[:, u, :].rearrange("p (i d) -> p i d", i=TILES)).then_inc(stored[u], 16)

            load_parts(0, 0)
            load_parts(1, 1)
            with sp.Fori(0, BATCHES // 2 - 1) as r:
                for u in range(2):
                    load_parts(2 * r + 2 + u, u)
                    store(2 * r + u, u)
            for u in range(2):
                store(BATCHES - 2 + u, u)
            for u in range(2):
                sp.wait_ge(stored[u], 16 * BATCHES // 2)

        @block.gpsimd
        def _(pool):
            def fill(t, value):
                nc.gpsimd.memset(t, value).then_inc(setup, 1)

            fill(mean_w[:, :], 1.0 / TOKENS)
            fill(ident[:, :], 0.0)
            fill(ident_b[:, :], 0.0)
            fill(ones_b[:, :], 1.0)
            fill(before_b[:, :], 1.0)
            fill(lower[:, :, :], 1.0)
            fill(AQ[:, :, :, :], 0.0)
            fill(AK[:, :, :, 0:ROWS], 0.0)
            fill(AK[:, :, :, ROWS:HEAD_ROWS], 0.0)
            fill(V[:, :, :, HD:VCOLS], 1.0)
            fill(count[:, :], 0.0)
            fill(eps[:, :], NORM_EPS)
            fill(blank[:, 0:TOK_COL], 0.0)
            nc.gpsimd.iota(slot_base_i[:, :], [[-CAP, EXPERTS]], base=SLOTS, channel_multiplier=0).then_inc(setup, 1)
            nc.gpsimd.iota(token_i[:, :], [[P, TILES]], base=0, channel_multiplier=1).then_inc(setup, 1)
            nc.gpsimd.iota(blank_i[:, :], [[0, 1]], base=ALL_TOKENS, channel_multiplier=1).then_inc(setup, 1)
            pool.wait_ge(setup, SETUP)
            for t, op, step, off in ((ident, ALU.not_equal, -1, 0), (ident_b, ALU.not_equal, -1, 0)):
                nc.gpsimd.affine_select(out=t[:, :], in_=t[:, :], compare_op=op, fill=1.0, base=off,
                                        pattern=[[step, P]], channel_multiplier=1).then_inc(constants, 1)
            nc.gpsimd.affine_select(out=before_b[:, :], in_=before_b[:, :], compare_op=ALU.is_gt, fill=0.0, base=0,
                                    pattern=[[1, P]], channel_multiplier=-1).then_inc(constants, 1)
            nc.gpsimd.affine_select(out=lower[:, :, :], in_=lower[:, :, :], compare_op=ALU.is_gt, fill=0.0, base=0,
                                    pattern=[[1, GROUPS], [-1, GROUPS]], channel_multiplier=0).then_inc(constants, 1)
            nc.gpsimd.memset(AK[:, :, :, ROWS:ROWS + PARTS], 1.0).then_inc(constants, 1)

            def reduce_all(q):
                wait(pool, prep, prep_at(q, "largest"))
                nc.gpsimd.partition_all_reduce(largest_all[:, :], largest[:, :], P, bass.bass_isa.ReduceOp.max
                                               ).then_inc(all_reduced, 1)

            def scatter(p):
                wait(pool, post, post_at(p, "x1_3"))
                nc.gpsimd.tensor_copy(rec[:, :, 0:DIM], x1[:, :, :]).then_inc(record, 1)
                nc.gpsimd.tensor_copy(rec[:, :, TOK_COL], token[:, :]).then_inc(record, 1)
                wait(pool, record, 3 * p + 3)
                nc.gpsimd.tensor_scalar(token[:, :], token[:, :], float(TOKENS), None, ALU.add).then_inc(record, 1)
                wait(pool, record, 3 * p + 4)
                wait(pool, post, post_at(p, "index"))
                for i in range(TILES):
                    for k in range(TOP):
                        pool.indirect_dma_start(
                            records, bass.IndirectOffsetOnAxis(ap=index[:, i * TOP + k:i * TOP + k + 1], axis=0),
                            rec[:, i, :], None, bounds_check=SLOTS - 1, oob_is_err=False).then_inc(scattered, 16)
                wait(pool, scattered, 16 * TILES * TOP * (p + 1))
                pool.sem_inc(record_free, 1)

            def batch(phase, b):
                if phase != "last":
                    reduce_all(b + 1)
                if phase != "first":
                    scatter(b - 1)

            reduce_all(0)
            pool.wait_ge(records_blank, 16)
            pool.wait_ge(small_ready, 3)
            pool.sem_inc(record_free, 1)
            pool.sem_inc(record, 1)
            iterations(pool, batch)
            scatter(BATCHES - 1)
            pool.wait_ge(dram_blank, 16 * SUMS)

            def add_rows(s, u):
                wait(pool, weighted, s + 1)
                for j in range(SUMS):
                    if not isinstance(s, int) or s >= 1:
                        wait(pool, added[j], 16 * s)
                    pool.indirect_dma_start(
                        sums[j], bass.IndirectOffsetOnAxis(ap=target[:, u, j:j + 1], axis=0),
                        ye[:, u, j, :], None, bounds_check=ACC_ROWS - 1, oob_is_err=True,
                        compute_op=ALU.add).then_inc(added[j], 16)

            for s in range(2):
                add_rows(s, s)
            with pool.Fori(1, STEPS // 2) as r:
                for u in range(2):
                    add_rows(2 * r + u, u)

        @block.tensor
        def _(pe):
            def begin(phase, b, name):
                bank, n = job(phase, b, name)
                wait(pe, read[bank], n)
                return bank

            def mean(phase, b, q):
                wait(pe, x_loaded, 16 * (q + 1))
                m = begin(phase, b, "mean")
                for i in range(TILES):
                    mm = pe.matmul(M[m][:, 0:DIM], mean_w[:, :], tokens_of(X, q, i, 1), start=i == 0, stop=i == TILES - 1)
                mm.then_inc(written[m], 1)

            def turn(phase, b, q, j):
                if j == 0:
                    wait(pe, prep, prep_at(q, "l40"))
                m = begin(phase, b, f"lr{j}")
                for side, A in enumerate((AK, AQ)):
                    for i in range(TILES):
                        mm = pe.transpose(Mb[m][:, side * TOKENS + i * P:side * TOKENS + (i + 1) * P],
                                          A[:, i, 2 * j:2 * j + 2, :].rearrange("p a c -> p (a c)"), ident_b[:, :])
                mm.then_inc(written[m], 1)

            def xt(phase, b, p):
                wait(pe, post, post_at(p, "x1_3"))
                m = begin(phase, b, "xt")
                for i in range(TILES):
                    mm = pe.transpose(M[m][:, i * P:(i + 1) * P], x1[:, i, :], ident[:, :])
                mm.then_inc(written[m], 1)

            def xt_copied(phase, b):
                bank, n = job(phase, b, "xt")
                wait(pe, read[bank], n + 1)

            def gate(phase, b, p):
                xt_copied(phase, b)
                m = begin(phase, b, "gate")
                pe.matmul(M[m][:, :], small_T[:, 1, :], x1T[:, :], start=True, stop=True).then_inc(written[m], 1)

            def logits(phase, b, p):
                m = begin(phase, b, "logits")
                for i in range(TILES):
                    mm = pe.matmul(M[m][:, i * EXPERTS:(i + 1) * EXPERTS], x1T[:, i * P:(i + 1) * P],
                                   small_T[:, 0, 0:EXPERTS], start=True, stop=True)
                mm.then_inc(written[m], 1)

            def up(phase, b, p):
                m = begin(phase, b, "up")
                pe.matmul(M[m][:, :], small_T[:, 2, :], x1T[:, :], start=True, stop=True).then_inc(written[m], 1)

            def down(phase, b, p):
                bank, n = job(phase, b, "up")
                wait(pe, read[bank], n + 1)
                m = begin(phase, b, "down")
                for i in range(TILES):
                    mm = pe.matmul(M[m][:, i * DIM:(i + 1) * DIM], hT[:, i * P:(i + 1) * P], small_T[:, 3, :],
                                   start=True, stop=True)
                mm.then_inc(written[m], 1)

            def positions(phase, b, p):
                wait(pe, post, post_at(p, "maskb"))
                m = begin(phase, b, "pos")
                for i in range(TILES):
                    o = M[m][:, i * EXPERTS:(i + 1) * EXPERTS]
                    mm = pe.matmul(o, before_b[:, :], mask_b[:, i, :], start=True, stop=i == 0)
                    for k in range(i):
                        mm = pe.matmul(o, ones_b[:, :], mask_b[:, k, :], start=False, stop=k == i - 1)
                mm.then_inc(written[m], 1)

            def totals(phase, b, p):
                m = begin(phase, b, "totals")
                for i in range(TILES):
                    mm = pe.matmul(M[m][:, 0:EXPERTS], ones_b[:, :], mask_b[:, i, :], start=i == 0, stop=i == TILES - 1)
                mm.then_inc(written[m], 1)

            def run_job(phase, b, name):
                if name == "mean":
                    mean(phase, b, b + 1)
                elif name.startswith("lr"):
                    turn(phase, b, b + 1, int(name[2:]))
                else:
                    {"xt": xt, "gate": gate, "logits": logits, "up": up, "down": down, "pos": positions,
                     "totals": totals}[name](phase, b, b - 1)

            def score(b, u, i):
                pair, tile, n = QUAD * (u // 2) // 2 + i // 2, 2 * (u % 2) + i % 2, QUAD * u + i
                if not isinstance(b, int) or b > 0 or n >= 2:
                    wait(pe, exp_done, b * CHUNKS + n - 1)
                for j in range(2):
                    rows = slice(HEAD_ROWS * j, HEAD_ROWS * (j + 1))
                    mm = pe.matmul(S[:, 2 * (n % 2) + j, :], LR[rows, pair, 0, tile * P:(tile + 1) * P],
                                   LR[rows, pair, 1, :], start=True, stop=True)
                mm.then_inc(scored, 1)

            def weigh(b, u, k):
                g, c = u // 2, u % 2
                wait(pe, exp_done, b * CHUNKS + QUAD * (u + 1) - 1 + k)
                if k == 0:
                    if u in (0, UNITS - 2):
                        wait(pe, v_built, 2 * b + (1 if u == 0 else 2))
                    if c == 0 and (g >= 2 or not isinstance(b, int) or b > 0):
                        wait(pe, pv_read, QUADS * b + g - 1)
                for i in range(QUAD):
                    mm = pe.matmul(PV[g % 2][32 * i:32 * i + VCOLS, :], V[:, 2 * c + k, QUAD * g + i, :],
                                   E[:, u % 2, i, k, :], start=c == 0 and k == 0, stop=c == 1 and k == 1,
                                   tile_position=(0, 32 * i))
                if k == 1:
                    mm.then_inc(unit_weighed, 1)

            def turn_quad(b, g):
                wait(pe, quad_copied, QUADS * b + g + 1)
                for i in range(TILES):
                    mm = pe.transpose(PV[g % 2][:, i * P:(i + 1) * P], OT[:, i * P:(i + 1) * P], ident[:, :])
                mm.then_inc(quad_turned, 1)

            def row_maxima(phase, b):
                flag = pe.value_load(slow_flag[0:1, bass.ds(b, 1)], min_val=0, max_val=1)
                with pe.If(flag > 0):
                    for o in range(2):
                        wait(pe, read[o], jobs_before(phase, b, o))
                    if not isinstance(b, int) or b > 0:
                        wait(pe, exp_done, b * CHUNKS)
                    for hd in range(HEADS):
                        q, half = hd // 2, HEAD_ROWS * (hd % 2)
                        if hd > 0 or not isinstance(b, int) or b > 0:
                            wait(pe, row_read, b * 24 + hd)
                        for i in range(TILES):
                            mm = pe.matmul(S[:, i, :], LR[half:half + HEAD_ROWS, q, 1, i * P:(i + 1) * P],
                                           LR[half:half + HEAD_ROWS, q, 0, :], start=True, stop=True)
                        mm.then_inc(row_scored, 1)
                    wait(pe, row_parts, b * 6 + 5)
                    Sb = S[:, 0, :].bitcast(BF16)
                    for q in range(HEADS // 2):
                        wait(pe, row_read, b * 24 + HEADS + q)
                        for i in range(TILES):
                            mm = pe.transpose(Sb[:, i * P:(i + 1) * P],
                                              AQ[:, i, 2 * q:2 * q + 2, :].rearrange("p a c -> p (a c)"), ident_b[:, :])
                        mm.then_inc(row_scored, 1)
                    wait(pe, row_read, b * 24 + 24)
                with pe.Else():
                    pe.sem_inc(row_scored, 24)

            def batch(phase, b):
                for o in range(2):
                    wait(pe, read[o], jobs_before(phase, b, o) - 1)
                wait(pe, prep, prep_at(b, "shift"))
                row_maxima(phase, b)
                for slot in range(SLOTS_PER_BATCH):
                    u, half = slot // 2, slot % 2
                    score(b, u, 2 * half)
                    if u > 0:
                        weigh(b, u - 1, half)
                    elif phase != "first":
                        weigh(b - 1, UNITS - 1, half)
                    score(b, u, 2 * half + 1)
                    for g in range(QUADS - 1):
                        if slot == TURN_SLOT[g]:
                            turn_quad(b, g)
                    if slot == TURN_SLOT[QUADS - 1] and phase != "first":
                        turn_quad(b - 1, QUADS - 1)
                    for name, at in SLOT_OF.items():
                        if at == slot and name in PHASES[phase]:
                            run_job(phase, b, name)

            pe.wait_ge(constants, 5)
            mean("prologue", 0, 0)
            for j in range(8):
                turn("prologue", 0, 0, j)
            pe.wait_ge(small_loaded, 16 * 5)
            pe.wait_ge(banks_clear, 2)
            for k in range(4):
                rows = EXPERTS if k == 0 else P
                mm = pe.transpose(PV[1][:, k * P:k * P + rows], small_w[0:rows, k, :], ident[0:rows, 0:rows])
            mm.then_inc(small_turned, 1)
            pe.wait_ge(small_ready, 5)
            iterations(pe, batch)
            for half in range(2):
                weigh(BATCHES - 1, UNITS - 1, half)
            turn_quad(BATCHES - 1, QUADS - 1)
            for name in POST_JOBS:
                run_job("epilogue", BATCHES, name)

            pe.wait_ge(weights_loaded, 16 * 3)
            for n in range(WEIGHT_JOBS):
                bank = n % 2
                pe.wait_ge(read[bank], epilogue_end[bank] + n // 2)
                for i in range(4):
                    if n < EXPERTS // 4:
                        src = w13[:, 4 * n + i, :]
                    else:
                        r = 4 * (n - EXPERTS // 4) + i
                        src = w2n[:, 2 * r:2 * r + 2, :].rearrange("p a c -> p (a c)")
                    mm = pe.transpose(M[bank][:, i * P:(i + 1) * P], src, ident[:, :])
                mm.then_inc(written[bank], 1)

            def turn_x(s, u):
                if not isinstance(s, int) or s >= 2:
                    wait(pe, x_copied, s - 1)
                wait(pe, slots_loaded, 16 * (s + 1))
                for i in range(GROUP_OF):
                    mm = pe.transpose(S[:, u % 2, i * CAP:(i + 1) * CAP], slots_in[:, u % 4, i * REC:i * REC + DIM],
                                      ident[:, :])
                mm.then_inc(x_turned, 1)

            def up_step(s, u):
                if not isinstance(s, int) or s >= 2:
                    wait(pe, silu, 3 * s - 3)
                wait(pe, x_copied, s + 1)
                for i in range(GROUP_OF):
                    mm = pe.matmul(S[:, 2 + u % 2, i * P:(i + 1) * P], xeT[:, u % 2, i * CAP:(i + 1) * CAP],
                                   w13_flat[:, bass.ds((GROUP_OF * s + i) * P, P)], start=True, stop=True)
                mm.then_inc(up_done, 1)

            def turn_h(s, u):
                if not isinstance(s, int) or s >= 2:
                    wait(pe, h_copied, s - 1)
                wait(pe, silu, 3 * s + 3)
                for r in range(2):
                    mm = pe.transpose(PV[u % 2][:, r * P:(r + 1) * P], h[:, u % 2, r * P:(r + 1) * P], ident[:, :])
                mm.then_inc(h_turned, 1)

            def down_step(s, u):
                wait(pe, h_copied, s + 1)
                for r in range(2):
                    mm = pe.matmul(M[u % 2][:, 2 * r * DIM:(2 * r + 2) * DIM], ehT[:, u % 2, r * CAP:(r + 1) * CAP],
                                   w2bd_flat[:, bass.ds((2 * s + r) * 2 * DIM, 2 * DIM)], start=True, stop=True)
                mm.then_inc(down_done, 1)

            w13_flat = w13[:, :, :].rearrange("p e c -> p (e c)")
            w2bd_flat = w2bd.rearrange("p r c -> p (r c)")
            for o in range(2):
                pe.wait_ge(read[o], epilogue_end[o] + WEIGHT_JOBS // 2)
            pe.wait_ge(pv_read, QUADS * BATCHES)
            pe.wait_ge(exp_done, CHUNKS * BATCHES)

            def step(s, u):
                whole = not isinstance(s, int)
                if whole or s < STEPS:
                    turn_x(s, u)
                if whole or 0 <= s - 1 < STEPS:
                    up_step(s - 1, u - 1)
                if whole or 0 <= s - 2 < STEPS:
                    turn_h(s - 2, u - 2)
                if whole or 0 <= s - 3 < STEPS:
                    if whole or s - 3 >= 2:
                        wait(pe, weighted, s - 4)
                    down_step(s - 3, u - 3)

            for s in range(8):
                step(s, s)
            with pe.Fori(2, STEPS // 4) as r:
                for u in range(4):
                    step(4 * r + u, u + 4)
            for s in range(STEPS, STEPS + 3):
                step(s, s)

        @block.scalar
        def _(act):
            def norm_start(p):
                wait(act, post, post_at(p, "moments3"))
                nc.scalar.activation(log_v[:, :], moments[:, :, 1], ACT.Ln, bias=eps[:, :]).then_inc(act_post, 1)
                wait(act, act_post, act_post_at(p, "log"))
                nc.scalar.activation(rstd0[:, :], log_v[:, :], ACT.Exp, scale=-0.5).then_inc(act_post, 1)

            def copy_x1T(phase, b):
                bank, n = job(phase, b, "xt")
                wait(act, written[bank], n + 1)
                nc.scalar.copy(x1T[:, :], M[bank][:, :]).then_inc(read[bank], 1)

            def gate_sigmoid(p):
                wait(act, post, post_at(p, "g1"))
                nc.scalar.activation(eg[:, :], sg[:, :], ACT.Ln).then_inc(act_post, 1)
                wait(act, act_post, act_post_at(p, "gate_log"))
                nc.scalar.activation(eg[:, :], eg[:, :], ACT.Exp, scale=-1.0).then_inc(act_post, 1)

            def exp_gate(phase, b, p):
                bank, n = job(phase, b, "gate")
                wait(act, written[bank], n + 1)
                nc.scalar.activation(eg[:, :], M[bank][:, :], ACT.Exp, scale=-1.0).then_inc(act_post, 1)

            def exp_logits(phase, b, p):
                bank, n = job(phase, b, "logits")
                wait(act, written[bank], n + 1)
                nc.scalar.activation(el[:, :], M[bank][:, 0:TILES * EXPERTS], ACT.Exp, scale=-1.0
                                     ).then_inc(read[bank], 1)

            def build_v(b, lo, hi):
                nc.scalar.copy(V[:, :, lo:hi, 0:HD], tokens_of(X, b).rearrange("p (i h d) -> p i h d", i=TILES, h=HEADS)
                               [:, :, lo:hi, :]).then_inc(v_built, 1)

            def copy_quad(b, g):
                wait(act, unit_weighed, UNITS * b + 2 * g + 2)
                if not isinstance(b, int) or b > 0 or g > 0:
                    wait(act, quad_turned, QUADS * b + g)
                nc.scalar.copy(OT[:, :], PV[g % 2][:, :]).then_inc(quad_copied, 1)

            def batch(phase, b):
                wait(act, prep, prep_at(b, "shift"))
                for slot in range(SLOTS_PER_BATCH):
                    u = slot // 2
                    for i in range(2 * (slot % 2), 2 * (slot % 2) + 2):
                        n = QUAD * u + i
                        if i == 0 and (u >= 2 or not isinstance(b, int) or b > 0):
                            wait(act, unit_weighed, b * UNITS + u - 1)
                        wait(act, scored, b * CHUNKS + n + 1)
                        nc.scalar.activation(E[:, u % 2, 2 * (i // 2):2 * (i // 2) + 2, i % 2, :], S[:, 2 * (n % 2):2 * (n % 2) + 2, :], ACT.Exp,
                                             bias=shift[:, bass.ds(b, 1)]).then_inc(exp_done, 1)
                        if i % 2 == 0:
                            if phase != "first" and slot == SLOT_OF["xt"] + 1:
                                copy_x1T(phase, b)
                            if phase != "first" and slot == SLOT_OF["gate"] + 1:
                                exp_logits(phase, b, b - 1)
                                exp_gate(phase, b, b - 1)
                            for g in range(QUADS - 1):
                                if slot == COPY_SLOT[g]:
                                    copy_quad(b, g)
                            if slot == COPY_SLOT[QUADS - 1] and phase != "first":
                                copy_quad(b - 1, QUADS - 1)
                    if slot == 0:
                        wait(act, x_loaded, 16 * (b + 1))
                        if not isinstance(b, int) or b > 0:
                            wait(act, unit_weighed, b * UNITS - 1)
                        build_v(b, 0, HEADS - QUAD)
                    if slot == 2:
                        wait(act, unit_weighed, b * UNITS)
                        build_v(b, HEADS - QUAD, HEADS)
                    if phase != "first":
                        if slot == 4:
                            norm_start(b - 1)
                        if slot == SLOT_OF["gate"] + 1:
                            gate_sigmoid(b - 1)

            nc.scalar.preload_act_table_set("natural_log_exp_and_others")
            act.wait_ge(setup, SETUP)
            act.wait_ge(banks_clear, 2)
            iterations(act, batch)
            copy_quad(BATCHES - 1, QUADS - 1)
            norm_start(BATCHES - 1)
            copy_x1T("epilogue", BATCHES)
            exp_gate("epilogue", BATCHES, BATCHES - 1)
            exp_logits("epilogue", BATCHES, BATCHES - 1)
            gate_sigmoid(BATCHES - 1)

            for n in range(1, WEIGHT_JOBS, 2):
                act.wait_ge(written[1], epilogue_end[1] + n // 2 + 1)
                if n < EXPERTS // 4:
                    nc.scalar.copy(w13[:, 4 * n:4 * n + 4, :], M[1][:, :].rearrange("p (a c) -> p a c", a=4)
                                   ).then_inc(read[1], 1)
                else:
                    r = 4 * (n - EXPERTS // 4)
                    act.wait_ge(w2_cleared, 1)
                    src = M[1][:, :].rearrange("p (a c) -> p a c", a=4)
                    nc.scalar.copy(w2bd[0:FF, r:r + 4, 0:DIM], src[0:FF, :, :])
                    nc.scalar.copy(w2bd[FF:P, r:r + 4, DIM:2 * DIM], src[FF:P, :, :]).then_inc(read[1], 1)

            def copy_x(s, u):
                wait(act, x_turned, s + 1)
                if not isinstance(s, int) or s >= 2:
                    wait(act, up_done, s - 1)
                nc.scalar.copy(xeT[:, u % 2, :], S[:, u % 2, :]).then_inc(x_copied, 1)

            def exp_step(s, u):
                wait(act, up_done, s + 1)
                if not isinstance(s, int) or s >= 2:
                    wait(act, silu, 3 * s - 3)
                e = eh[:, u % 2, :, :]
                nc.scalar.activation(e, S[:, 2 + u % 2, :].rearrange("p (i c) -> p i c", i=GROUP_OF)[:, :, 0:FF],
                                     ACT.Exp, scale=-1.0).then_inc(exp_up, 1)

            def sigmoid_step(s, u):
                e = eh[:, u % 2, :, :]
                wait(act, silu, 3 * s + 1)
                nc.scalar.activation(e, e, ACT.Ln).then_inc(sigmoid, 1)
                wait(act, sigmoid, 2 * s + 1)
                nc.scalar.activation(e, e, ACT.Exp, scale=-1.0).then_inc(sigmoid, 1)

            def step(s, u):
                whole = not isinstance(s, int)
                if whole or s < STEPS:
                    copy_x(s, u)
                if whole or 0 <= s - 1 < STEPS:
                    exp_step(s - 1, u - 1)
                    sigmoid_step(s - 1, u - 1)

            step(0, 0)
            step(1, 1)
            with act.Fori(1, STEPS // 2) as r:
                for u in range(2):
                    step(2 * r + u, u + 2)
            step(STEPS, STEPS)

            def last_norm(q, u):
                wait(act, summed, sum_at(q, "moments3"))
                nc.scalar.activation(last_log[:, u, :], last_moments[:, u, :, 1], ACT.Ln, bias=eps[:, :]).then_inc(act_fin, 1)
                wait(act, act_fin, 2 * q + 1)
                nc.scalar.activation(last_rstd0[:, u, :], last_log[:, u, :], ACT.Exp, scale=-0.5).then_inc(act_fin, 1)

            with act.Fori(0, BATCHES // 2) as r:
                for u in range(2):
                    last_norm(2 * r + u, u)

        @block.vector
        def _(dve):
            v = nc.vector

            def refine(step, after, ready, moments, rstd0, rstd):
                step("veps", v.tensor_scalar(veps[:, :], moments[:, :, 1], NORM_EPS, None, ALU.add))
                ready()
                step("r2", v.tensor_tensor(r2[:, :], rstd0, rstd0, ALU.mult))
                after("r2")
                step("vr2", v.tensor_tensor(r2[:, :], r2[:, :], veps[:, :], ALU.mult))
                after("vr2")
                step("corr", v.tensor_scalar(r2[:, :], r2[:, :], -0.5, 1.5, ALU.mult, ALU.add))
                after("corr")
                step("rstd", v.tensor_tensor(rstd, r2[:, :], rstd0, ALU.mult))
                after("rstd")

            def moments_of(step, after, y, stats, moments):
                for i in range(TILES):
                    step(f"stats{i}", v.bn_stats(stats[:, i, :], y[:, i, :]))
                for i in range(TILES):
                    after(f"stats{i}")
                    step(f"moments{i}", v.bn_aggr(moments[:, i, :], stats[:, i, :]))

            def leave(b, g):
                src = PV[g % 2][:, :].rearrange("p (i h c) -> p i h c", i=TILES, h=QUAD)
                wait(dve, quad_turned, QUADS * b + g + 1)
                wait(dve, pv_read, QUADS * b + g)
                v.reciprocal(rden[:, :, :], src[:, :, :, HD]).then_inc(pv_recip, 1)
                wait(dve, pv_recip, QUADS * b + g + 1)
                dst = O[:, :, g * QUAD * HD:(g + 1) * QUAD * HD].rearrange("p i (h d) -> p i h d", h=QUAD)
                v.tensor_tensor(dst, src[:, :, :, 0:HD], rden[:, :, :].unsqueeze(3).to_broadcast([P, TILES, QUAD, HD]),
                                ALU.mult).then_inc(pv_read, 1)

            def row_maxima(b):
                flag = dve.value_load(slow_flag[0:1, bass.ds(b, 1)], min_val=0, max_val=1)
                with dve.If(flag > 0):
                    for hd in range(HEADS):
                        wait(dve, row_scored, b * 24 + hd + 1)
                        v.tensor_reduce(row_max[:, hd, :], S[:, :, :], AX.X, ALU.max, negate=True).then_inc(row_read, 1)
                    wait(dve, row_read, b * 24 + HEADS)
                    wait(dve, row_parts, b * 6)
                    left_over = row_max
                    for k in range(PARTS):
                        col = AQ[:, :, :, ROWS + k].rearrange("p i h -> p h i")
                        v.tensor_copy(col, left_over[:, :, :]).then_inc(row_parts, 1)
                        wait(dve, row_parts, b * 6 + 2 * k + 1)
                        if k < PARTS - 1:
                            v.tensor_tensor(row_rest[:, :, :], left_over[:, :, :], col, ALU.subtract).then_inc(row_parts, 1)
                            wait(dve, row_parts, b * 6 + 2 * k + 2)
                            left_over = row_rest
                    Sb = S[:, 0, :].bitcast(BF16)
                    for q in range(HEADS // 2):
                        wait(dve, row_scored, b * 24 + HEADS + q + 1)
                        v.tensor_copy(LR[:, q, 1, :], Sb[:, 0:TOKENS]).then_inc(row_read, 1)
                    v.memset(AQ[:, :, :, ROWS:ROWS + PARTS], 0.0).then_inc(row_parts, 1)
                with dve.Else():
                    dve.sem_inc(row_read, 24)
                    dve.sem_inc(row_parts, 6)

            def operand(A, lo, hi):
                return A[:, :, :, lo:hi].rearrange("p i h c -> p (i h) c")

            def prep_parts(phase, b, q, step, after):
                bank, n = job(phase, b, "mean")
                wait(dve, written[bank], n + 1)
                wait(dve, x_loaded, 16 * (q + 1))
                v.tensor_tensor(xc[:, :].rearrange("p (i d) -> p i d", i=TILES),
                                tokens_of(X, q).rearrange("p (i d) -> p i d", i=TILES),
                                M[bank][:, 0:DIM].unsqueeze(1).to_broadcast([P, TILES, DIM]),
                                ALU.subtract).then_inc(read[bank], 1)
                wait(dve, read[bank], n + 1)
                x3 = xc[:, :].rearrange("p (g d) -> p g d", d=HD)
                r3 = rest[:, :].rearrange("p (g d) -> p g d", d=HD)
                step("high", v.tensor_copy(operand(AQ, 0, HD), x3))
                after("high")
                step("rest", v.tensor_tensor(r3, x3, operand(AQ, 0, HD), ALU.subtract))
                after("rest")
                step("middle", v.tensor_copy(operand(AQ, HD, 2 * HD), r3))
                after("middle")
                step("low", v.tensor_tensor(operand(AQ, 2 * HD, 3 * HD), r3, operand(AQ, HD, 2 * HD), ALU.subtract))

            def prep_rows(step, after):
                step("square", v.tensor_tensor(square[:, :], xc[:, :], xc[:, :], ALU.mult))
                after("square")
                step("norms", v.tensor_reduce(norms[:, :], square[:, :].rearrange("p (g d) -> p g d", d=HD), AX.X, ALU.add))
                after("norms")
                step("largest", v.tensor_reduce(largest[:, :], norms[:, :], AX.X, ALU.max))

                def repeat(part, times):
                    return operand(AQ, part * HD, (part + 1) * HD).unsqueeze(2).to_broadcast(
                        [P, TILES * HEADS, times, HD])

                def key_rows(lo, times):
                    return operand(AK, lo * HD, (lo + times) * HD).rearrange("p g (r d) -> p g r d", r=times)

                step("r24", v.tensor_copy(operand(AQ, 3 * HD, 5 * HD), operand(AQ, 0, 2 * HD)))
                step("r40", v.tensor_copy(operand(AQ, 5 * HD, 6 * HD), operand(AQ, 0, HD)))
                step("l0", v.tensor_copy(key_rows(0, 3), repeat(0, 3)))
                step("l24", v.tensor_copy(key_rows(3, 2), repeat(1, 2)))
                step("l40", v.tensor_copy(key_rows(5, 1), repeat(2, 1)))

            def prep_shift(q, step, after):
                wait(dve, all_reduced, q + 1)
                step("slow", v.tensor_scalar(slow_flag[:, bass.ds(q, 1)], largest_all[:, :], SHIFT_LIMIT, None, ALU.is_gt))
                step("neg_small", v.tensor_scalar(neg_small[:, :], largest_all[:, :], SHIFT_LIMIT, -1.0,
                                                  ALU.is_le, ALU.mult))
                after("neg_small")
                step("shift", v.tensor_tensor(shift[:, bass.ds(q, 1)], neg_small[:, :], largest_all[:, :], ALU.mult))

            def take_turned(phase, b, j):
                bank, n = job(phase, b, f"lr{j}")
                wait(dve, written[bank], n + 1)
                v.tensor_copy(LR[:, j, :, :].rearrange("p a t -> p (a t)"), Mb[bank]).then_inc(read[bank], 1)

            class Steps:
                def __init__(self, s, names, base):
                    self.s, self.names, self.base, self.order = s, names, base, 0

                def step(self, name, ins):
                    assert self.names[self.order] == name, (self.names[self.order], name)
                    self.order += 1
                    ins.then_inc(self.s, 1)

                def after(self, name):
                    wait(dve, self.s, self.base + self.names.index(name) + 1)

            def post_norm(p, t):
                t.step("y", v.tensor_tensor(O[:, :, :].rearrange("p i d -> p (i d)"), O[:, :, :].rearrange("p i d -> p (i d)"),
                                            tokens_of(X, p), ALU.add))
                t.after("y")
                moments_of(t.step, t.after, O, stats, moments)

            def post_x1(p, t):
                t.after("moments3")
                refine(t.step, t.after, lambda: wait(dve, act_post, act_post_at(p, "rstd0")),
                       moments, rstd0[:, :], rstd[:, :])
                wait(dve, record, 3 * p + 1)
                for i in range(TILES):
                    t.step(f"x1_{i}", v.tensor_scalar(x1[:, i, :], O[:, i, :], moments[:, i, 0:1], rstd[:, i:i + 1],
                                                      ALU.subtract, ALU.mult))

            def post_shared(phase, b, p, t):
                wait(dve, act_post, act_post_at(p, "exp_gate"))
                t.step("g1", v.tensor_scalar(sg[:, :], eg[:, :], LARGEST_LOG, 1.0, ALU.min, ALU.add))

            def post_shared_h(phase, b, p, t):
                wait(dve, act_post, act_post_at(p, "gate_sigmoid"))
                bank, n = job(phase, b, "gate")
                v.tensor_tensor(sg[:, :], M[bank][:, :], eg[:, :], ALU.mult).then_inc(read[bank], 1)
                wait(dve, read[bank], n + 1)
                bank, n = job(phase, b, "up")
                wait(dve, written[bank], n + 1)
                v.tensor_tensor(hT[:, :], M[bank][:, :], sg[:, :], ALU.mult).then_inc(read[bank], 1)

            def post_scores(phase, b, p, t):
                bank, n = job(phase, b, "logits")
                wait(dve, read[bank], n + 1)
                t.step("s1", v.tensor_scalar(scores[:, :], el[:, :], 1.0, None, ALU.add))
                t.after("s1")
                t.step("scores", v.reciprocal(scores[:, :], scores[:, :]))

            def post_route(p, t):
                t.after("scores")
                ie = lambda a: a[:, :].rearrange("p (i e) -> p i e", i=TILES)
                t.step("sfc", v.tensor_tensor(ie(sfc), ie(scores), bias[:, :].unsqueeze(1).to_broadcast([P, TILES, EXPERTS]),
                                              ALU.add))
                t.after("sfc")
                s8 = sfc[:, :].rearrange("p (g e) -> p g e", e=PER_GROUP)
                t.step("hi4", v.tensor_tensor(hi4[:, :, :], s8[:, :, 0:4], s8[:, :, 4:8], ALU.max))
                t.step("lo4", v.tensor_tensor(lo4[:, :, :], s8[:, :, 0:4], s8[:, :, 4:8], ALU.min))
                t.after("lo4")
                t.step("hi2", v.tensor_tensor(hi2[:, :, :], hi4[:, :, 0:2], hi4[:, :, 2:4], ALU.max))
                t.step("t2", v.tensor_tensor(t2[:, :, :], hi4[:, :, 0:2], hi4[:, :, 2:4], ALU.min))
                t.step("u2", v.tensor_tensor(u2[:, :, :], lo4[:, :, 0:2], lo4[:, :, 2:4], ALU.max))
                t.after("u2")
                t.step("lo2", v.tensor_tensor(lo2[:, :, :], t2[:, :, :], u2[:, :, :], ALU.max))
                t.step("hi1", v.tensor_tensor(hi1[:, :], hi2[:, :, 0], hi2[:, :, 1], ALU.max))
                t.step("t1", v.tensor_tensor(t1[:, :], hi2[:, :, 0], hi2[:, :, 1], ALU.min))
                t.after("lo2")
                t.step("u1", v.tensor_tensor(u1[:, :], lo2[:, :, 0], lo2[:, :, 1], ALU.max))
                t.after("u1")
                t.step("lo1", v.tensor_tensor(lo1[:, :], t1[:, :], u1[:, :], ALU.max))
                t.after("lo1")
                t.step("gs", v.tensor_tensor(gs[:, :, :].rearrange("p i g -> p (i g)"), hi1[:, :], lo1[:, :], ALU.add))
                t.after("gs")
                full = [P, TILES, GROUPS, GROUPS]
                other = gs[:, :, :].unsqueeze(2).to_broadcast(full)
                own = gs[:, :, :].unsqueeze(3).to_broadcast(full)
                t.step("ge", v.tensor_tensor(ge[:, :, :, :], other, own, ALU.is_ge))
                t.step("gt", v.tensor_tensor(gt[:, :, :, :], other, own, ALU.is_gt))
                t.after("ge")
                t.step("geL", v.tensor_tensor(ge[:, :, :, :], ge[:, :, :, :], lower[:, :, :].unsqueeze(1).to_broadcast(full),
                                              ALU.mult))
                t.after("geL")
                t.step("beats", v.tensor_tensor(gt[:, :, :, :], ge[:, :, :, :], gt[:, :, :, :], ALU.max))
                t.after("beats")
                t.step("rank", v.tensor_reduce(rank[:, :], gt[:, :, :, :].rearrange("p i a c -> p (i a) c"), AX.X, ALU.add))
                t.after("rank")
                t.step("keep", v.tensor_scalar(keep[:, :], rank[:, :], float(TOP_GROUPS), None, ALU.is_lt))
                t.after("keep")
                t.step("tmp", v.tensor_tensor(tmp[:, :].rearrange("p (g e) -> p g e", e=PER_GROUP), s8,
                                              keep[:, :].unsqueeze(2).to_broadcast([P, TILES * GROUPS, PER_GROUP]), ALU.mult))
                t.after("tmp")
                t.step("tmp0", v.tensor_scalar(tmp[:, :], tmp[:, :], 0.0, None, ALU.add))
                t.after("tmp0")
                for i in range(TILES):
                    t.step(f"top{i}", v.max(top[:, i, :], ie(tmp)[:, i, :]))
                for i in range(TILES):
                    t.after(f"top{i}")
                    t.step(f"rest{i}", v.match_replace(ie(left)[:, i, :], top[:, i, :], ie(tmp)[:, i, :], BELOW_ALL))
                t.after("rest3")
                t.step("mask", v.tensor_tensor(mask[:, :], left[:, :], tmp[:, :], ALU.not_equal))
                t.after("mask")
                t.step("maskb", v.tensor_copy(mask_b[:, :, :].rearrange("p i e -> p (i e)"), mask[:, :]))

            def post_shared_out(phase, b, p):
                bank, n = job(phase, b, "down")
                wait(dve, written[bank], n + 1)
                v.tensor_tensor(tokens_of(Z, p), M[bank][:, :], x1[:, :, :].rearrange("p i d -> p (i d)"), ALU.add
                                ).then_inc(read[bank], 1)

            def post_record(p, t):
                ie = lambda a: a[:, :].rearrange("p (i e) -> p i e", i=TILES)
                t.step("wsel", v.tensor_tensor(wsel[:, :], mask[:, :], scores[:, :], ALU.mult))
                t.after("wsel")
                t.step("wsum", v.tensor_reduce(wsum[:, :], ie(wsel), AX.X, ALU.add))
                t.after("wsum")
                t.step("wsum2", v.tensor_scalar(wsum[:, :], wsum[:, :], 1e-20, 1.0 / SCALE, ALU.add, ALU.mult))
                t.after("wsum2")
                t.step("wrec", v.reciprocal(wsum[:, :], wsum[:, :]))
                t.after("wrec")
                wait(dve, record_free, p + 1)
                t.step("recw", v.tensor_tensor(rec[:, :, W_COL:W_COL + EXPERTS], ie(scores),
                                               wsum[:, :].unsqueeze(2).to_broadcast([P, TILES, EXPERTS]), ALU.mult))

            def post_pos(phase, b, p, t):
                bank, n = job(phase, b, "pos")
                ie = lambda a: a[:, :].rearrange("p (i e) -> p i e", i=TILES)
                wait(dve, written[bank], n + 1)
                v.tensor_tensor(ie(pos), M[bank][:, 0:TILES * EXPERTS].rearrange("p (i e) -> p i e", i=TILES),
                                count[:, :].unsqueeze(1).to_broadcast([P, TILES, EXPERTS]), ALU.add).then_inc(read[bank], 1)
                wait(dve, read[bank], n + 1)
                t.step("kept", v.scalar_tensor_tensor(kept[:, :], pos[:, :], float(CAP), mask[:, :], ALU.is_lt, ALU.mult))
                t.step("room", v.tensor_tensor(ie(key), slot_base[:, :].unsqueeze(1).to_broadcast([P, TILES, EXPERTS]),
                                               ie(pos), ALU.subtract))
                t.after("room")
                t.step("key", v.tensor_tensor(key[:, :], key[:, :], kept[:, :], ALU.mult))
                t.after("key")
                for i in range(TILES):
                    t.step(f"slots{i}", v.max(best[:, i, :], ie(key)[:, i, :]))
                t.after("slots3")
                t.step("index", v.tensor_scalar(index[:, :], best[:, :, :].rearrange("p i k -> p (i k)"), -1.0,
                                                float(SLOTS), ALU.mult, ALU.add))

            def post_totals(phase, b, p):
                bank, n = job(phase, b, "totals")
                wait(dve, written[bank], n + 1)
                v.tensor_tensor(count[:, :], M[bank][:, 0:EXPERTS], count[:, :], ALU.add).then_inc(read[bank], 1)

            def batch(phase, b):
                p, q = b - 1, b + 1
                t = Steps(post, POST_STEPS, p * len(POST_STEPS))
                w = Steps(prep, PREP_STEPS, q * len(PREP_STEPS))
                with_post, with_prep = phase != "first", phase != "last"
                row_maxima(b)
                if with_prep:
                    prep_parts(phase, b, q, w.step, w.after)
                    prep_rows(w.step, w.after)
                if with_post:
                    leave(p, QUADS - 1)
                    wait(dve, pv_read, QUADS * b)
                    post_norm(p, t)
                if with_prep:
                    take_turned(phase, b, 0)
                if with_post:
                    post_x1(p, t)
                if with_prep:
                    take_turned(phase, b, 1)
                if with_post:
                    post_shared(phase, b, p, t)
                    post_scores(phase, b, p, t)
                    post_shared_h(phase, b, p, t)
                leave(b, 0)
                if with_post:
                    post_route(p, t)
                    post_shared_out(phase, b, p)
                if with_prep:
                    take_turned(phase, b, 2)
                if with_post:
                    post_record(p, t)
                leave(b, 1)
                if with_prep:
                    take_turned(phase, b, 3)
                if with_post:
                    post_pos(phase, b, p, t)
                if with_prep:
                    take_turned(phase, b, 4)
                if with_post:
                    post_totals(phase, b, p)
                if with_prep:
                    take_turned(phase, b, 5)
                    prep_shift(q, w.step, w.after)
                leave(b, 2)
                if with_prep:
                    take_turned(phase, b, 6)
                    take_turned(phase, b, 7)
                    assert w.order == len(PREP_STEPS)
                if with_post:
                    assert t.order == len(POST_STEPS)

            v.memset(PV[0][:, :], 0.0).then_inc(banks_clear, 1)
            v.memset(PV[1][:, :], 0.0).then_inc(banks_clear, 1)
            dve.wait_ge(setup, SETUP)
            v.tensor_copy(slot_base[:, :], slot_base_i[:, :]).then_inc(small_ready, 1)
            v.tensor_copy(token[:, :], token_i[:, :]).then_inc(small_ready, 1)
            v.tensor_copy(blank[:, TOK_COL:REC], blank_i[:, :]).then_inc(small_ready, 1)
            dve.wait_ge(constants, 5)
            w = Steps(prep, PREP_STEPS, 0)
            prep_parts("prologue", 0, 0, w.step, w.after)
            prep_rows(w.step, w.after)
            for j in range(8):
                take_turned("prologue", 0, j)
            prep_shift(0, w.step, w.after)
            dve.wait_ge(small_turned, 1)
            v.tensor_copy(small_T[:, 0, 0:EXPERTS], PV[1][:, 0:EXPERTS]).then_inc(small_ready, 1)
            v.tensor_copy(small_T[:, 1:4, :], PV[1][:, P:4 * P].rearrange("p (a c) -> p a c", a=3)).then_inc(small_ready, 1)
            dve.wait_ge(small_loaded, 16 * 5)
            dve.wait_ge(small_ready, 5)
            iterations(dve, batch)

            p = BATCHES - 1
            t = Steps(post, POST_STEPS, p * len(POST_STEPS))
            leave(p, QUADS - 1)
            wait(dve, pv_read, QUADS * BATCHES)
            post_norm(p, t)
            post_x1(p, t)
            post_shared("epilogue", BATCHES, p, t)
            post_scores("epilogue", BATCHES, p, t)
            post_shared_h("epilogue", BATCHES, p, t)
            post_route(p, t)
            post_shared_out("epilogue", BATCHES, p)
            post_record(p, t)
            post_pos("epilogue", BATCHES, p, t)
            post_totals("epilogue", BATCHES, p)
            v.memset(w2bd, 0.0).then_inc(w2_cleared, 1)
            dve.wait_ge(w2_cleared, 1)
            for n in range(0, WEIGHT_JOBS, 2):
                dve.wait_ge(written[0], epilogue_end[0] + n // 2 + 1)
                src = M[0][:, :].rearrange("p (a c) -> p a c", a=4)
                if n < EXPERTS // 4:
                    v.tensor_copy(w13[:, 4 * n:4 * n + 4, :], src).then_inc(read[0], 1)
                else:
                    r = 4 * (n - EXPERTS // 4)
                    v.tensor_copy(w2bd[0:FF, r:r + 4, 0:DIM], src[0:FF, :, :])
                    v.tensor_copy(w2bd[FF:P, r:r + 4, DIM:2 * DIM], src[FF:P, :, :]).then_inc(read[0], 1)

            def add_one(s, u):
                e = eh[:, u % 2, :, :]
                wait(dve, exp_up, s + 1)
                v.tensor_scalar(e, e, LARGEST_LOG, 1.0, ALU.min, ALU.add).then_inc(silu, 1)

            def silu_step(s, u):
                up_ = S[:, 2 + u % 2, :].rearrange("p (i c) -> p i c", i=GROUP_OF)
                e = eh[:, u % 2, :, :]
                wait(dve, sigmoid, 2 * s + 2)
                if not isinstance(s, int) or s >= 2:
                    wait(dve, h_turned, s - 1)
                v.tensor_tensor(e, up_[:, :, 0:FF], e, ALU.mult).then_inc(silu, 1)
                wait(dve, silu, 3 * s + 2)
                v.tensor_tensor(h[:, u % 2, :].rearrange("p (i f) -> p i f", i=GROUP_OF), up_[:, :, FF:2 * FF], e,
                                ALU.mult).then_inc(silu, 1)

            def copy_h(s, u):
                wait(dve, h_turned, s + 1)
                if not isinstance(s, int) or s >= 2:
                    wait(dve, down_done, s - 1)
                v.tensor_copy(ehT[:, u % 2, :], PV[u % 2][:, 0:2 * CAP]).then_inc(h_copied, 1)

            def take_weights(s, u):
                wait(dve, slots_loaded, 16 * (s + 1))
                if not isinstance(s, int) or s >= 4:
                    wait(dve, weighted, s - 3)
                v.tensor_copy(weight[:, u % 4, :], slots_flat[:, bass.ds((u % 4) * GROUP_OF * REC + W_COL + GROUP_OF * s,
                                                                        GROUP_OF, step=REC + 1)])
                v.tensor_copy(number[:, u % 4, :], slots_in[:, u % 4, TOK_COL::REC]).then_inc(taken, 1)

            def weigh_step(s, u):
                wait(dve, down_done, s + 1)
                wait(dve, taken, s + 1)
                if not isinstance(s, int) or s >= 2:
                    for j in range(SUMS):
                        wait(dve, added[j], 16 * (s - 1))
                v.tensor_copy(target[:, u % 2, :], number[:, u % 4, :])
                for i in range(GROUP_OF):
                    last = v.tensor_scalar(ye[:, u % 2, i, :], M[u % 2][:, i * DIM:(i + 1) * DIM],
                                           weight[:, u % 4, i:i + 1], None, ALU.mult)
                last.then_inc(weighted, 1)

            def step(s, u):
                whole = not isinstance(s, int)
                if whole or s < STEPS:
                    take_weights(s, u)
                if whole or 0 <= s - 1 < STEPS:
                    add_one(s - 1, u - 1)
                if whole or 0 <= s - 2 < STEPS:
                    copy_h(s - 2, u - 2)
                if whole or 0 <= s - 3 < STEPS:
                    weigh_step(s - 3, u - 3)
                if whole or 0 <= s - 1 < STEPS:
                    silu_step(s - 1, u - 1)

            for s in range(8):
                step(s, s)
            with dve.Fori(2, STEPS // 4) as r:
                for u in range(4):
                    step(4 * r + u, u + 4)
            for s in range(STEPS, STEPS + 3):
                step(s, s)

            def last_sum(q, even, u):
                t = Steps(summed, SUM_STEPS, q * len(SUM_STEPS))
                wait(dve, parts_loaded[u], 8 * even * SUMS + 16 * SUMS)
                if not isinstance(q, int) or q > 0:
                    wait(dve, summed, sum_at(q - 1, "y"))
                a, c, y = square, rest, last_y[u]
                t.step("a01", v.tensor_tensor(a[:, :], sums_in[:, SUMS * u, :], sums_in[:, SUMS * u + 1, :], ALU.add))
                t.step("a23", v.tensor_tensor(c[:, :], sums_in[:, SUMS * u + 2, :], sums_in[:, SUMS * u + 3, :], ALU.add))
                t.after("a23")
                t.step("sum", v.tensor_tensor(a[:, :], a[:, :], c[:, :], ALU.add))
                t.after("sum")
                if not isinstance(q, int) or q > 1:
                    wait(dve, normed_out, out_at(q - 2, "out3"))
                t.step("y", v.tensor_tensor(y[:, :, :].rearrange("p i d -> p (i d)"), a[:, :], tokens_of(Z, q), ALU.add))
                t.after("y")
                moments_of(t.step, t.after, y, last_stats[:, u], last_moments[:, u])

            def last_out(q, even, u):
                t = Steps(normed_out, OUT_STEPS, q * len(OUT_STEPS))
                wait(dve, summed, sum_at(q, "moments3"))
                if not isinstance(q, int) or q > 0:
                    wait(dve, normed_out, out_at(q - 1, "rstd"))
                refine(t.step, t.after, lambda: wait(dve, act_fin, 2 * q + 2), last_moments[:, u], last_rstd0[:, u, :],
                       last_rstd[:, u, :])
                if not isinstance(even, int) or even > 0:
                    wait(dve, stored[u], 8 * even)
                for i in range(TILES):
                    t.step(f"out{i}", v.tensor_scalar(normed[:, u, i * DIM:(i + 1) * DIM], last_y[u][:, i, :],
                                                      last_moments[:, u, i, 0:1], last_rstd[:, u, i:i + 1],
                                                      ALU.subtract, ALU.mult))

            last_sum(0, 0, 0)
            last_sum(1, 0, 1)
            last_out(0, 0, 0)
            last_sum(2, 2, 0)
            last_out(1, 0, 1)
            with dve.Fori(1, BATCHES // 2 - 1) as r:
                last_sum(2 * r + 1, 2 * r, 1)
                last_out(2 * r, 2 * r, 0)
                last_sum(2 * r + 2, 2 * r + 2, 0)
                last_out(2 * r + 1, 2 * r, 1)
            last_sum(BATCHES - 1, BATCHES - 2, 1)
            last_out(BATCHES - 2, BATCHES - 2, 0)
            last_out(BATCHES - 1, BATCHES - 2, 1)


_INS = ["L0_attn_x", "L0_ffn_gate_weight", "L0_ffn_e_bias", "L0_ffn_w1", "L0_ffn_w2", "L0_ffn_w3",
        "L0_ffn_shared_gate", "L0_ffn_shared_up", "L0_ffn_shared_down"]


def kernel(**inputs):
    import numpy as np
    import concourse.bacc as bacc
    from concourse.bass_utils import run_bass_kernel_spmd

    nc = bacc.Bacc("TRN2", target_bir_lowering=False, num_devices=1)
    arrays, args = {}, []
    for name in _INS:
        a = np.ascontiguousarray(inputs[name])
        arrays[f"{name}_dram"] = a
        args.append(nc.dram_tensor(f"{name}_dram", a.shape, mybir.dt.from_np(a.dtype), kind="ExternalInput").ap())
    args.append(nc.dram_tensor("out_dram", (BATCHES, TOKENS, DIM), F32, kind="ExternalOutput").ap())
    post_norm_block(nc, *args)
    return run_bass_kernel_spmd(nc, [arrays], core_ids=[0]).results[0]["out_dram"]
```

```python
from contextlib import ExitStack

import concourse.bass as bass
from concourse import mybir

ALU = mybir.AluOpType
ACT = mybir.ActivationFunctionType
AX = mybir.AxisListType
F32 = mybir.dt.float32
BF16 = mybir.dt.bfloat16
I32 = mybir.dt.int32
U32 = mybir.dt.uint32

P = 128
BATCHES, TOKENS, DIM = 8, 512, 128
HEADS = 16
HD = DIM // HEADS
TILES = TOKENS // P
VCOLS = HD + 1
PARTS = 3
ROWS = 6 * HD
HEAD_ROWS = 64
SHIFT_LIMIT = 60.0

EXPERTS, TOP, GROUPS, TOP_GROUPS = 64, 8, 8, 4
PER_GROUP = EXPERTS // GROUPS
CAP = 128
SLOTS = EXPERTS * CAP
FF = 64
SCALE = 2.5
NORM_EPS = 1e-5
ALL_TOKENS = BATCHES * TOKENS
REC = DIM + EXPERTS + 1
W_COL, TOK_COL = DIM, DIM + EXPERTS
SUMS = 4
ACC_ROWS = ALL_TOKENS + CAP
GROUP_OF = 4
STEPS = EXPERTS // GROUP_OF
BELOW_ALL = -1e30
LARGEST_LOG = 1e19

QUAD = 4
QUADS = HEADS // QUAD
UNITS = 2 * QUADS
SLOTS_PER_BATCH = 2 * UNITS
CHUNKS = 2 * HEADS

BANK = {"mean": 1, "lr0": 0, "lr1": 1, "xt": 0, "gate": 1, "logits": 0, "up": 0, "lr2": 1, "down": 0, "lr3": 1,
        "pos": 0, "lr4": 1, "totals": 0, "lr5": 1, "lr6": 0, "lr7": 1}
SLOT_OF = {"mean": 0, "lr0": 3, "lr1": 4, "xt": 5, "logits": 6, "gate": 6, "up": 7, "lr2": 9, "down": 9, "lr3": 11,
           "pos": 12, "lr4": 13, "totals": 13, "lr5": 14, "lr6": 15, "lr7": 15}
NORM_SLOT, X1T_SLOT, EXP_SLOT, SIGMOID_SLOT = 3, 5, 6, 7
ACT_TAKES = {3: 11, 6: 15}
COPY_SLOT = {0: 7, 1: 10, 2: 14, 3: 2}
TURN_SLOT = {0: 8, 1: 10, 2: 14, 3: 2}
PREP_JOBS = ["mean"] + [f"lr{j}" for j in range(8)]
POST_JOBS = ["xt", "logits", "gate", "up", "down", "pos", "totals"]
WEIGHT_JOBS = EXPERTS // 4 + EXPERTS // 8
PHASES = {"prologue": ["mean"], "first": PREP_JOBS, "mid": list(SLOT_OF), "last": POST_JOBS, "epilogue": POST_JOBS}
RUNS = {"prologue": 1, "first": 1, "mid": BATCHES - 2, "last": 1, "epilogue": 1}

PREP_STEPS = ["high", "rest", "middle", "low", "r24", "r40", "l0", "l24", "l40",
              "square", "norms", "largest", "slow", "neg_small", "shift"]
POST_STEPS = (["y"] + [f"stats{i}" for i in range(4)] + [f"moments{i}" for i in range(4)]
              + ["veps", "r2", "vr2", "corr", "rstd"] + [f"x1_{i}" for i in range(4)]
              + ["g1", "s1", "scores", "sfc", "hi4", "lo4", "hi2", "t2", "u2", "lo2", "hi1", "t1", "u1",
                 "lo1", "gs", "ge", "gt", "geL", "beats", "rank", "keep", "tmp", "tmp0"]
              + [f"top{i}" for i in range(4)] + [f"rest{i}" for i in range(4)]
              + ["mask", "maskb", "wsel", "wsum", "wsum2", "wrec", "recw",
                 "kept", "room", "key"] + [f"slots{i}" for i in range(4)] + ["index"])
ACT_POST_STEPS = ["log", "rstd0", "exp_gate", "gate_log", "gate_sigmoid"]
SUM_STEPS = ["sum", "y"] + [f"stats{i}" for i in range(4)] + [f"moments{i}" for i in range(4)]
SCALE_STEPS = ["minus_mean", "veps", "r2", "vr2", "corr", "rstd", "offset"]


def post_norm_block(nc, x, gate_w, e_bias, w1, w2, w3, s_gate, s_up, s_down, out):
    with ExitStack() as ctx:
        def sb(name, shape, dt=F32):
            return ctx.enter_context(nc.sbuf_tensor(name, shape, dt))

        def psum(name, shape, dt=F32):
            return ctx.enter_context(nc.psum_tensor(name, shape, dt))

        def sem(name):
            return ctx.enter_context(nc.semaphore(name))

        records = nc.dram_tensor("records", (SLOTS, REC), F32, kind="Internal").ap()
        sums = [nc.dram_tensor(f"sums{j}", (ACC_ROWS, DIM), F32, kind="Internal").ap() for j in range(SUMS)]

        ident = sb("ident", [P, P])
        ident_b = sb("ident_b", [P, P], BF16)
        mean_w = sb("mean_w", [P, P])
        before_b = sb("before_b", [P, P], BF16)
        ones_b = sb("ones_b", [P, P], BF16)
        lower = sb("lower", [P, GROUPS, GROUPS])
        slot_base_i = sb("slot_base_i", [P, EXPERTS], I32)
        slot_base = sb("slot_base", [P, EXPERTS])
        token_i = sb("token_i", [P, TILES], I32)
        token = sb("token", [P, TILES])
        eps = sb("eps", [P, 1])
        blank_i = sb("blank_i", [P, 1], I32)
        blank = sb("blank", [P, REC])
        bias = sb("bias", [P, EXPERTS])
        small_w = sb("small_w", [P, 4, P])
        small_T = sb("small_T", [P, 4, P])
        large = sb("large", [P, 2 * EXPERTS * P])
        w13 = large[:, 0:EXPERTS * P].rearrange("p (e c) -> p e c", c=P)
        w2n = sb("w2n", [P, EXPERTS, FF])
        X = sb("X", [P, BATCHES * TILES * DIM])
        V = sb("V", [P, TILES, HEADS, VCOLS])
        centred = sb("centred", [P, 3, TILES * DIM])
        xc, rest, square = (centred[:, k, :] for k in range(3))
        norms = sb("norms", [P, TILES * HEADS])
        largest = sb("largest", [P, 1])
        largest_all = sb("largest_all", [P, 1])
        slow_flag = sb("slow_flag", [P, BATCHES], I32)
        neg_small = sb("neg_small", [P, 1])
        shift = sb("shift", [P, BATCHES])
        shift_now = sb("shift_now", [P, 1])
        AK = sb("AK", [P, TILES, HEADS, HEAD_ROWS], BF16)
        AQ = sb("AQ", [P, TILES, HEADS, HEAD_ROWS], BF16)
        LR = sb("LR", [P, HEADS // 2, 2, TOKENS], BF16)
        E = large[:, EXPERTS * P:].rearrange("p (u i k t) -> p u i k t", u=2, i=QUAD, k=2)
        OT = sb("OT", [P, TOKENS])
        rden = sb("rden", [P, TILES, QUAD])
        O = sb("O", [P, TILES, DIM])
        row_max = sb("row_max", [P, HEADS, TILES])
        row_rest = sb("row_rest", [P, HEADS, TILES])
        stats = sb("stats", [P, TILES, 6])
        moments = sb("moments", [P, TILES, 2])
        log_v = sb("log_v", [P, TILES])
        rstd0 = sb("rstd0", [P, TILES])
        veps = sb("veps", [P, TILES])
        r2 = sb("r2", [P, TILES])
        rstd = sb("rstd", [P, TILES])
        x1 = sb("x1", [P, TILES, DIM])
        x1T = sb("x1T", [P, TOKENS])
        eg = sb("eg", [P, TOKENS])
        sg = sb("sg", [P, TOKENS])
        hT = sb("hT", [P, TOKENS])
        el = sb("el", [P, TILES * EXPERTS])
        scores = sb("scores", [P, TILES * EXPERTS])
        sfc = sb("sfc", [P, TILES * EXPERTS])
        hi4 = sb("hi4", [P, 32, 4])
        lo4 = sb("lo4", [P, 32, 4])
        hi2 = sb("hi2", [P, 32, 2])
        t2 = sb("t2", [P, 32, 2])
        u2 = sb("u2", [P, 32, 2])
        lo2 = sb("lo2", [P, 32, 2])
        hi1 = sb("hi1", [P, 32])
        t1 = sb("t1", [P, 32])
        u1 = sb("u1", [P, 32])
        lo1 = sb("lo1", [P, 32])
        gs = sb("gs", [P, TILES, GROUPS])
        ge = sb("ge", [P, TILES, GROUPS, GROUPS])
        gt = sb("gt", [P, TILES, GROUPS, GROUPS])
        rank = sb("rank", [P, TILES * GROUPS])
        keep = sb("keep", [P, TILES * GROUPS])
        tmp = sb("tmp", [P, TILES * EXPERTS])
        top = sb("top", [P, TILES, 8])
        left = sb("left", [P, TILES * EXPERTS])
        mask = sb("mask", [P, TILES * EXPERTS])
        mask_b = sb("mask_b", [P, TILES, EXPERTS], BF16)
        wsel = sb("wsel", [P, TILES * EXPERTS])
        wsum = sb("wsum", [P, TILES])
        count = sb("count", [P, EXPERTS])
        pos = sb("pos", [P, TILES * EXPERTS])
        kept = sb("kept", [P, TILES * EXPERTS])
        key = sb("key", [P, TILES * EXPERTS])
        best = sb("best", [P, TILES, 8])
        index = sb("index", [P, TILES * 8], U32)
        rec = sb("rec", [P, TILES, REC])
        last_rec = centred[:, 0:2, :].rearrange("p k t -> p (k t)")[:, 0:TILES * REC].rearrange("p (i r) -> p i r", i=TILES)
        last_index = sb("last_index", [P, TILES * 8], U32)
        Z = sb("Z", [P, BATCHES * TILES * DIM])
        w2bd = large[:, EXPERTS * P:].rearrange("p (r c) -> p r c", c=2 * DIM)
        free_f32 = AK[:, :, :, :].rearrange("p a b c -> p (a b c)").bitcast(F32)
        slots_flat = X[:, 0:4 * GROUP_OF * REC]
        slots_in = X[:, 0:4 * GROUP_OF * REC].rearrange("p (s r) -> p s r", s=4)
        eh = X[:, 4 * GROUP_OF * REC:4 * GROUP_OF * REC + 2 * GROUP_OF * FF].rearrange(
            "p (s i f) -> p s i f", s=2, i=GROUP_OF)
        xeT = free_f32[:, 0:2 * GROUP_OF * CAP].rearrange("p (s c) -> p s c", s=2)
        h = free_f32[:, 8 * CAP:8 * CAP + 8 * FF].rearrange("p (s f) -> p s f", s=2)
        ehT = free_f32[:, 8 * CAP + 8 * FF:12 * CAP + 8 * FF].rearrange("p (s c) -> p s c", s=2)
        ye = centred[:, 0:2, :].rearrange("p s (i d) -> p s i d", i=GROUP_OF)
        weight = sb("weight", [P, 4, GROUP_OF])
        number = sb("number", [P, 4, GROUP_OF])
        target = sb("target", [P, 2, GROUP_OF], U32)
        last_stats = sb("last_stats", [P, 2, TILES, 6])
        last_moments = sb("last_moments", [P, 2, TILES, 2])
        last_log = sb("last_log", [P, 2, TILES])
        last_rstd0 = sb("last_rstd0", [P, 2, TILES])
        last_rstd = sb("last_rstd", [P, 2, TILES])
        last_offset = sb("last_offset", [P, 2, TILES])
        minus_mean = sb("minus_mean", [P, TILES])
        last_veps = sb("last_veps", [P, TILES])
        last_r2 = sb("last_r2", [P, TILES])

        def y(q, i):
            return large[:, bass.ds(q * SUMS * TILES * DIM + i * DIM, DIM)]

        def part(q, j):
            return large[:, bass.ds((q * SUMS + j) * TILES * DIM, TILES * DIM)]

        normed = AQ[:, :, :, :].rearrange("p a b c -> p (a b c)").bitcast(F32).rearrange("p (s t) -> p s t", s=4)

        S = psum("S", [P, 4, 512])
        PV = [psum(f"PV{o}", [P, 512]) for o in range(2)]
        M = [psum(f"M{o}", [P, 512]) for o in range(2)]
        Mb = [m[:, :].bitcast(BF16) for m in M]

        setup = sem("setup")
        constants = sem("constants")
        x_loaded = sem("x_loaded")
        small_loaded = sem("small_loaded")
        small_turned = sem("small_turned")
        small_ready = sem("small_ready")
        weights_loaded = sem("weights_loaded")
        records_blank = sem("records_blank")
        dram_blank = sem("dram_blank")
        written = [sem(f"written{o}") for o in range(2)]
        read = [sem(f"read{o}") for o in range(2)]
        prep = sem("prep")
        all_reduced = sem("all_reduced")
        scored = sem("scored")
        exp_done = sem("exp_done")
        unit_weighed = sem("unit_weighed")
        quad_copied = sem("quad_copied")
        quad_turned = sem("quad_turned")
        banks_clear = sem("banks_clear")
        first_turned = sem("first_turned")
        first_taken = [sem(f"first_taken{o}") for o in range(2)]
        pv_recip = sem("pv_recip")
        pv_read = sem("pv_read")
        v_built = sem("v_built")
        shift_taken = sem("shift_taken")
        row_scored = sem("row_scored")
        row_read = sem("row_read")
        row_parts = sem("row_parts")
        post = sem("post")
        act_post = sem("act_post")
        scattered = sem("scattered")
        record_free = sem("record_free")
        record = sem("record")
        w2_cleared = sem("w2_cleared")
        slots_loaded = [sem(f"slots_loaded{j}") for j in range(4)]
        x_turned = sem("x_turned")
        x_copied = sem("x_copied")
        up_done = sem("up_done")
        exp_up = sem("exp_up")
        silu = sem("silu")
        sigmoid = sem("sigmoid")
        h_turned = sem("h_turned")
        h_copied = sem("h_copied")
        down_done = sem("down_done")
        weighted = sem("weighted")
        taken = sem("taken")
        added = [sem(f"added{j}") for j in range(SUMS)]
        parts_loaded = [sem(f"parts_loaded{j}") for j in range(2)]
        halved = sem("halved")
        summed = sem("summed")
        last_scaled = sem("last_scaled")
        normed_done = sem("normed_done")
        act_fin = sem("act_fin")
        stored = [sem(f"stored{j}") for j in range(2)]
        carrier = sem("carrier")

        block = ctx.enter_context(nc.Block())

        def wait(eng, s, value):
            if isinstance(value, int):
                if value > 0:
                    eng.wait_ge(s, value)
            else:
                eng.wait_ge(s, value)
                eng.sem_inc(carrier, 1)

        class Steps:
            def __init__(self, eng, s, names, base):
                self.eng, self.s, self.names, self.base, self.order = eng, s, names, base, 0

            def step(self, name, ins):
                assert self.names[self.order] == name, (self.names[self.order], name)
                self.order += 1
                ins.then_inc(self.s, 1)

            def after(self, name):
                wait_next(self.eng, self.s, self.base + self.names.index(name) + 1)

            def after_alone(self, name):
                wait(self.eng, self.s, self.base + self.names.index(name) + 1)

        def wait_next(eng, s, value):
            if not isinstance(value, int) or value > 0:
                eng.wait_ge(s, value)

        def jobs_before(phase, b, bank):
            n = 0
            for name, jobs in PHASES.items():
                here = sum(BANK[j] == bank for j in jobs)
                if name == phase:
                    return n + (here * (b - 1) if name == "mid" else 0)
                n += here * RUNS[name]

        def job(phase, b, name):
            bank = BANK[name]
            here = [j for j in PHASES[phase] if BANK[j] == bank]
            return bank, jobs_before(phase, b, bank) + here.index(name)

        epilogue_end = [jobs_before("epilogue", 0, o) + sum(BANK[j] == o for j in POST_JOBS) for o in range(2)]

        def prep_at(q, step):
            return q * len(PREP_STEPS) + PREP_STEPS.index(step) + 1

        def post_at(p, step):
            return p * len(POST_STEPS) + POST_STEPS.index(step) + 1

        def act_post_at(p, step):
            return p * len(ACT_POST_STEPS) + ACT_POST_STEPS.index(step) + 1

        def sum_at(q, step):
            return q * len(SUM_STEPS) + SUM_STEPS.index(step) + 1

        def scale_at(q, step):
            return q * len(SCALE_STEPS) + SCALE_STEPS.index(step) + 1

        def tokens_of(t, q, i=0, n=TILES):
            return t[:, bass.ds(q * TILES * DIM + i * DIM, n * DIM)]

        def loads_of(s, u):
            return 4 * (s - u % 4) + 16

        def last_of_all(p):
            return isinstance(p, int) and p == BATCHES - 1

        def record_of(p):
            return (last_rec, last_index) if last_of_all(p) else (rec, index)

        def iterations(eng, body):
            body("first", 0)
            with eng.Fori(1, BATCHES - 1) as b:
                body("mid", b)
            body("last", BATCHES - 1)

        SETUP = 16

        @block.sync
        def _(sp):
            for q in range(BATCHES):
                if q > 0:
                    sp.wait_ge(x_loaded, 16 * q)
                sp.dma_start(tokens_of(X, q).rearrange("p (i d) -> p i d", i=TILES),
                             x[q].rearrange("(i p) d -> p i d", p=P)).then_inc(x_loaded, 16)
                if q == 0:
                    sp.dma_start(small_w[0:EXPERTS, 0, :], gate_w).then_inc(small_loaded, 16)
                    sp.dma_start(small_w[:, 1, :], s_gate).then_inc(small_loaded, 16)
                    sp.dma_start(small_w[:, 2, :], s_up).then_inc(small_loaded, 16)
                    sp.dma_start(small_w[:, 3, :], s_down).then_inc(small_loaded, 16)
                    sp.dma_start(bias[:, :], e_bias.rearrange("(a e) -> a e", a=1).to_broadcast([P, EXPERTS])
                                 ).then_inc(small_loaded, 16)
            sp.wait_ge(setup, SETUP)
            sp.wait_ge(small_ready, 3)
            sp.dma_start(records.rearrange("(e c) r -> c e r", c=CAP),
                         blank[:, :].unsqueeze(1).to_broadcast([P, EXPERTS, REC])).then_inc(records_blank, 16)
            for j in range(SUMS):
                sp.dma_start(sums[j].rearrange("(p r) d -> p r d", p=P),
                             blank[:, 0:DIM].unsqueeze(1).to_broadcast([P, ACC_ROWS // P, DIM])
                             ).then_inc(dram_blank, 16)
            sp.dma_start(w13[0:FF, :, :], w1.rearrange("e f h -> f e h")).then_inc(weights_loaded, 16)
            sp.dma_start(w13[FF:P, :, :], w3.rearrange("e f h -> f e h")).then_inc(weights_loaded, 16)
            sp.dma_start(w2n[:, :, :], w2.rearrange("e h f -> h e f")).then_inc(weights_loaded, 16)
            sp.wait_ge(scattered, 16 * BATCHES * TILES * TOP)

            def load_slots(s, u):
                if not isinstance(s, int) or s >= 4:
                    wait(sp, x_turned, s - 3)
                    wait(sp, taken, s - 3)
                sp.dma_start(slots_in[:, u, :].rearrange("p (i r) -> p i r", i=GROUP_OF),
                             records[bass.ds(s * GROUP_OF * CAP, GROUP_OF * CAP), :].rearrange("(i c) r -> c i r", c=CAP)
                             ).then_inc(slots_loaded[u], 16)

            for s in range(4):
                load_slots(s, s)
            with sp.Fori(1, STEPS // 4) as r:
                for u in range(4):
                    load_slots(4 * r + u, u)

            for j in range(SUMS):
                sp.wait_ge(added[j], 16 * STEPS)

            def load_parts(q, even, u):
                if not isinstance(q, int) or q >= 2:
                    wait(sp, parts_loaded[u], 8 * SUMS * even)
                for j in range(SUMS):
                    sp.dma_start(part(q, j).rearrange("p (i d) -> p i d", i=TILES),
                                 sums[j][bass.ds(q * TOKENS, TOKENS), :].rearrange("(i p) d -> p i d", p=P)
                                 ).then_inc(parts_loaded[u], 16)

            def store(q, u):
                wait(sp, normed_done, q + 1)
                sp.dma_start(out[bass.ds(q, 1)].rearrange("a (i p) d -> p (a i) d", p=P),
                             normed[:, u, :].rearrange("p (i d) -> p i d", i=TILES)).then_inc(stored[u], 16)

            for u in range(2):
                load_parts(u, 0, u)
            with sp.Fori(1, BATCHES // 2) as r:
                for u in range(2):
                    load_parts(2 * r + u, 2 * r, u)
            with sp.Fori(0, BATCHES // 2) as r:
                for u in range(2):
                    store(2 * r + u, u)
            for u in range(2):
                sp.wait_ge(stored[u], 16 * BATCHES // 2)

        @block.gpsimd
        def _(pool):
            def fill(t, value):
                nc.gpsimd.memset(t, value).then_inc(setup, 1)

            fill(mean_w[:, :], 1.0 / TOKENS)
            fill(ident[:, :], 0.0)
            fill(ident_b[:, :], 0.0)
            fill(ones_b[:, :], 1.0)
            fill(before_b[:, :], 1.0)
            fill(lower[:, :, :], 1.0)
            fill(AQ[:, :, :, ROWS:HEAD_ROWS], 0.0)
            fill(AK[:, :, :, ROWS:ROWS + PARTS], 1.0)
            fill(AK[:, :, :, ROWS + PARTS:HEAD_ROWS], 0.0)
            fill(V[:, :, :, HD:VCOLS], 1.0)
            fill(count[:, :], 0.0)
            fill(eps[:, :], NORM_EPS)
            fill(blank[:, 0:TOK_COL], 0.0)
            nc.gpsimd.iota(slot_base_i[:, :], [[-CAP, EXPERTS]], base=SLOTS, channel_multiplier=0).then_inc(setup, 1)
            nc.gpsimd.iota(token_i[:, :], [[P, TILES]], base=0, channel_multiplier=1).then_inc(setup, 1)
            nc.gpsimd.iota(blank_i[:, :], [[0, 1]], base=ALL_TOKENS, channel_multiplier=1).then_inc(setup, 1)
            pool.wait_ge(setup, SETUP)
            for t in (ident, ident_b):
                nc.gpsimd.affine_select(out=t[:, :], in_=t[:, :], compare_op=ALU.not_equal, fill=1.0, base=0,
                                        pattern=[[-1, P]], channel_multiplier=1).then_inc(constants, 1)
            nc.gpsimd.affine_select(out=before_b[:, :], in_=before_b[:, :], compare_op=ALU.is_gt, fill=0.0, base=0,
                                    pattern=[[1, P]], channel_multiplier=-1).then_inc(constants, 1)
            nc.gpsimd.affine_select(out=lower[:, :, :], in_=lower[:, :, :], compare_op=ALU.is_gt, fill=0.0, base=0,
                                    pattern=[[1, GROUPS], [-1, GROUPS]], channel_multiplier=0).then_inc(constants, 1)

            def reduce_all(q):
                wait(pool, prep, prep_at(q, "largest"))
                nc.gpsimd.partition_all_reduce(largest_all[:, :], largest[:, :], P, bass.bass_isa.ReduceOp.max
                                               ).then_inc(all_reduced, 1)

            def scatter(p):
                rec, index = record_of(p)
                wait(pool, post, post_at(p, "x1_3"))
                if not last_of_all(p):
                    nc.gpsimd.tensor_copy(rec[:, :, 0:DIM], x1[:, :, :]).then_inc(record, 1)
                nc.gpsimd.tensor_copy(rec[:, :, TOK_COL], token[:, :]).then_inc(record, 1)
                wait(pool, record, 3 * p + 3)
                nc.gpsimd.tensor_scalar(token[:, :], token[:, :], float(TOKENS), None, ALU.add).then_inc(record, 1)
                wait(pool, record, 3 * p + 4)
                wait(pool, post, post_at(p, "index"))
                for i in range(TILES):
                    for k in range(TOP):
                        pool.indirect_dma_start(
                            records, bass.IndirectOffsetOnAxis(ap=index[:, i * TOP + k:i * TOP + k + 1], axis=0),
                            rec[:, i, :], None, bounds_check=SLOTS - 1, oob_is_err=False).then_inc(scattered, 16)

            def free_record(p):
                wait(pool, scattered, 16 * TILES * TOP * (p + 1))
                pool.sem_inc(record_free, 1)

            def batch(phase, b):
                if phase != "last":
                    reduce_all(b + 1)
                if phase != "first":
                    scatter(b - 1)
                if phase == "mid":
                    free_record(b - 1)

            reduce_all(0)
            pool.wait_ge(records_blank, 16)
            pool.wait_ge(small_ready, 3)
            pool.sem_inc(record_free, 1)
            pool.sem_inc(record, 1)
            iterations(pool, batch)
            scatter(BATCHES - 1)
            pool.wait_ge(dram_blank, 16 * SUMS)

            def add_rows(s, u):
                wait(pool, weighted, s + 1)
                for j in range(SUMS):
                    if not isinstance(s, int) or s >= 1:
                        wait(pool, added[j], 16 * s)
                    pool.indirect_dma_start(
                        sums[j], bass.IndirectOffsetOnAxis(ap=target[:, u, j:j + 1], axis=0),
                        ye[:, u, j, :], None, bounds_check=ACC_ROWS - 1, oob_is_err=True,
                        compute_op=ALU.add).then_inc(added[j], 16)

            for s in range(2):
                add_rows(s, s)
            with pool.Fori(1, STEPS // 2) as r:
                for u in range(2):
                    add_rows(2 * r + u, u)

            def scales(q, u):
                g = nc.gpsimd
                t = Steps(pool, last_scaled, SCALE_STEPS, q * len(SCALE_STEPS))
                wait(pool, summed, sum_at(q, "moments3"))
                if not isinstance(q, int) or q >= 1:
                    wait(pool, last_scaled, scale_at(q - 1, "offset"))
                if not isinstance(q, int) or q >= 2:
                    wait(pool, normed_done, q - 1)
                t.step("minus_mean", g.tensor_scalar(minus_mean[:, :], last_moments[:, u, :, 0], -1.0, None, ALU.mult))
                t.step("veps", g.tensor_scalar(last_veps[:, :], last_moments[:, u, :, 1], NORM_EPS, None, ALU.add))
                wait(pool, act_fin, 2 * q + 2)
                t.step("r2", g.tensor_tensor(last_r2[:, :], last_rstd0[:, u, :], last_rstd0[:, u, :], ALU.mult))
                t.after("r2")
                t.step("vr2", g.tensor_tensor(last_r2[:, :], last_r2[:, :], last_veps[:, :], ALU.mult))
                t.after_alone("vr2")
                t.step("corr", g.tensor_scalar(last_r2[:, :], last_r2[:, :], -0.5, 1.5, ALU.mult, ALU.add))
                t.after("corr")
                t.step("rstd", g.tensor_tensor(last_rstd[:, u, :], last_r2[:, :], last_rstd0[:, u, :], ALU.mult))
                t.after("rstd")
                t.step("offset", g.tensor_tensor(last_offset[:, u, :], minus_mean[:, :], last_rstd[:, u, :], ALU.mult))

            for u in range(2):
                scales(u, u)
            with pool.Fori(1, BATCHES // 2) as r:
                for u in range(2):
                    scales(2 * r + u, u)

        @block.tensor
        def _(pe):
            def begin(phase, b, name):
                bank, n = job(phase, b, name)
                wait_next(pe, read[bank], n)
                return bank

            def mean(phase, b, q):
                wait_next(pe, x_loaded, 16 * (q + 1))
                m = begin(phase, b, "mean")
                for i in range(TILES):
                    mm = pe.matmul(M[m][:, 0:DIM], mean_w[:, :], tokens_of(X, q, i, 1), start=i == 0, stop=i == TILES - 1)
                mm.then_inc(written[m], 1)

            def turn_into(bank, j):
                for side, A in enumerate((AK, AQ)):
                    for i in range(TILES):
                        mm = pe.transpose(bank[:, side * TOKENS + i * P:side * TOKENS + (i + 1) * P],
                                          A[:, i, 2 * j:2 * j + 2, :].rearrange("p a c -> p (a c)"), ident_b[:, :])
                return mm

            def turn(phase, b, q, j):
                if j == 0:
                    wait_next(pe, prep, prep_at(q, "l40"))
                m = begin(phase, b, f"lr{j}")
                turn_into(Mb[m], j).then_inc(written[m], 1)

            def xt(phase, b, p):
                wait_next(pe, post, post_at(p, "x1_3"))
                m = begin(phase, b, "xt")
                for i in range(TILES):
                    mm = pe.transpose(M[m][:, i * P:(i + 1) * P], x1[:, i, :], ident[:, :])
                mm.then_inc(written[m], 1)

            def xt_copied(phase, b):
                bank, n = job(phase, b, "xt")
                wait_next(pe, read[bank], n + 1)

            def gate(phase, b, p):
                m = begin(phase, b, "gate")
                pe.matmul(M[m][:, :], small_T[:, 1, :], x1T[:, :], start=True, stop=True).then_inc(written[m], 1)

            def logits(phase, b, p):
                xt_copied(phase, b)
                m = begin(phase, b, "logits")
                for i in range(TILES):
                    mm = pe.matmul(M[m][:, i * EXPERTS:(i + 1) * EXPERTS], x1T[:, i * P:(i + 1) * P],
                                   small_T[:, 0, 0:EXPERTS], start=True, stop=True)
                mm.then_inc(written[m], 1)

            def up(phase, b, p):
                m = begin(phase, b, "up")
                pe.matmul(M[m][:, :], small_T[:, 2, :], x1T[:, :], start=True, stop=True).then_inc(written[m], 1)

            def down(phase, b, p):
                bank, n = job(phase, b, "up")
                wait_next(pe, read[bank], n + 1)
                m = begin(phase, b, "down")
                for i in range(TILES):
                    mm = pe.matmul(M[m][:, i * DIM:(i + 1) * DIM], hT[:, i * P:(i + 1) * P], small_T[:, 3, :],
                                   start=True, stop=True)
                mm.then_inc(written[m], 1)

            def positions(phase, b, p):
                wait_next(pe, post, post_at(p, "maskb"))
                m = begin(phase, b, "pos")
                for i in range(TILES):
                    o = M[m][:, i * EXPERTS:(i + 1) * EXPERTS]
                    mm = pe.matmul(o, before_b[:, :], mask_b[:, i, :], start=True, stop=i == 0)
                    for k in range(i):
                        mm = pe.matmul(o, ones_b[:, :], mask_b[:, k, :], start=False, stop=k == i - 1)
                mm.then_inc(written[m], 1)

            def totals(phase, b, p):
                m = begin(phase, b, "totals")
                for i in range(TILES):
                    mm = pe.matmul(M[m][:, 0:EXPERTS], ones_b[:, :], mask_b[:, i, :], start=i == 0, stop=i == TILES - 1)
                mm.then_inc(written[m], 1)

            def run_job(phase, b, name):
                if name == "mean":
                    mean(phase, b, b + 1)
                elif name.startswith("lr"):
                    turn(phase, b, b + 1, int(name[2:]))
                else:
                    {"xt": xt, "gate": gate, "logits": logits, "up": up, "down": down, "pos": positions,
                     "totals": totals}[name](phase, b, b - 1)

            def score(b, u, i):
                pair, tile, n = QUAD * (u // 2) // 2 + i // 2, 2 * (u % 2) + i % 2, QUAD * u + i
                if not isinstance(b, int) or b > 0 or n >= 2:
                    wait(pe, exp_done, b * CHUNKS + n - 1)
                for j in range(2):
                    rows = slice(HEAD_ROWS * j, HEAD_ROWS * (j + 1))
                    mm = pe.matmul(S[:, 2 * (n % 2) + j, :], LR[rows, pair, 0, tile * P:(tile + 1) * P],
                                   LR[rows, pair, 1, :], start=True, stop=True)
                mm.then_inc(scored, 1)

            def weigh(b, u, k):
                g, c = u // 2, u % 2
                wait_next(pe, exp_done, b * CHUNKS + QUAD * (u + 1) - 1 + k)
                if k == 0:
                    if u in (0, UNITS - 2):
                        wait_next(pe, v_built, 2 * b + (1 if u == 0 else 2))
                    if c == 0 and (g >= 2 or not isinstance(b, int) or b > 0):
                        wait_next(pe, pv_read, QUADS * b + g - 1)
                for i in range(QUAD):
                    mm = pe.matmul(PV[g % 2][32 * i:32 * i + VCOLS, :], V[:, 2 * c + k, QUAD * g + i, :],
                                   E[:, u % 2, i, k, :], start=c == 0 and k == 0, stop=c == 1 and k == 1,
                                   tile_position=(0, 32 * i))
                if k == 1:
                    mm.then_inc(unit_weighed, 1)

            def turn_quad(b, g):
                wait_next(pe, quad_copied, QUADS * b + g + 1)
                for i in range(TILES):
                    mm = pe.transpose(PV[g % 2][:, i * P:(i + 1) * P], OT[:, i * P:(i + 1) * P], ident[:, :])
                mm.then_inc(quad_turned, 1)

            def row_maxima(phase, b):
                flag = pe.value_load(slow_flag[0:1, bass.ds(b, 1)], min_val=0, max_val=1)
                with pe.If(flag > 0):
                    for o in range(2):
                        wait(pe, read[o], jobs_before(phase, b, o))
                    if not isinstance(b, int) or b > 0:
                        wait(pe, exp_done, b * CHUNKS)
                    for hd in range(HEADS):
                        q, half = hd // 2, HEAD_ROWS * (hd % 2)
                        if hd > 0 or not isinstance(b, int) or b > 0:
                            wait(pe, row_read, b * 24 + hd)
                        for i in range(TILES):
                            mm = pe.matmul(S[:, i, :], LR[half:half + HEAD_ROWS, q, 1, i * P:(i + 1) * P],
                                           LR[half:half + HEAD_ROWS, q, 0, :], start=True, stop=True)
                        mm.then_inc(row_scored, 1)
                    wait(pe, row_parts, b * 6 + 5)
                    Sb = S[:, 0, :].bitcast(BF16)
                    for q in range(HEADS // 2):
                        wait(pe, row_read, b * 24 + HEADS + q)
                        for i in range(TILES):
                            mm = pe.transpose(Sb[:, i * P:(i + 1) * P],
                                              AQ[:, i, 2 * q:2 * q + 2, :].rearrange("p a c -> p (a c)"), ident_b[:, :])
                        mm.then_inc(row_scored, 1)
                    wait(pe, row_read, b * 24 + 24)
                with pe.Else():
                    pe.sem_inc(row_scored, 24)

            def batch(phase, b):
                for o in range(2):
                    wait(pe, read[o], jobs_before(phase, b, o) - 1)
                wait(pe, prep, prep_at(b, "shift"))
                row_maxima(phase, b)
                for slot in range(SLOTS_PER_BATCH):
                    u, half = slot // 2, slot % 2
                    score(b, u, 2 * half)
                    if slot == 0 and "mean" in PHASES[phase]:
                        run_job(phase, b, "mean")
                    if u > 0:
                        weigh(b, u - 1, half)
                    elif phase != "first":
                        weigh(b - 1, UNITS - 1, half)
                    score(b, u, 2 * half + 1)
                    for g in range(QUADS - 1):
                        if slot == TURN_SLOT[g]:
                            turn_quad(b, g)
                    if slot == TURN_SLOT[QUADS - 1] and phase != "first":
                        turn_quad(b - 1, QUADS - 1)
                    for name, at in SLOT_OF.items():
                        if at == slot and name in PHASES[phase] and name != "mean":
                            run_job(phase, b, name)

            pe.wait_ge(setup, 1)
            mean("prologue", 0, 0)
            pe.wait_ge(constants, 4)
            pe.wait_ge(setup, SETUP)
            pe.wait_ge(prep, prep_at(0, "l40"))
            for j in range(HEADS // 2):
                if j >= 4:
                    pe.wait_ge(first_taken[j % 2], j // 2 - 1)
                turn_into(S[:, j % 4, :].bitcast(BF16), j).then_inc(first_turned, 1)
            pe.wait_ge(small_loaded, 16 * 5)
            pe.wait_ge(banks_clear, 2)
            for k in range(4):
                rows = EXPERTS if k == 0 else P
                mm = pe.transpose(PV[1][:, k * P:k * P + rows], small_w[0:rows, k, :], ident[0:rows, 0:rows])
            mm.then_inc(small_turned, 1)
            for o in range(2):
                pe.wait_ge(first_taken[o], 4)
            pe.wait_ge(small_ready, 5)
            iterations(pe, batch)
            for half in range(2):
                weigh(BATCHES - 1, UNITS - 1, half)
            turn_quad(BATCHES - 1, QUADS - 1)
            for name in POST_JOBS:
                run_job("epilogue", BATCHES, name)

            pe.wait_ge(weights_loaded, 16 * 3)
            for n in range(WEIGHT_JOBS):
                bank = n % 2
                pe.wait_ge(read[bank], epilogue_end[bank] + n // 2)
                for i in range(4):
                    if n < EXPERTS // 4:
                        src = w13[:, 4 * n + i, :]
                    else:
                        r = 4 * (n - EXPERTS // 4) + i
                        src = w2n[:, 2 * r:2 * r + 2, :].rearrange("p a c -> p (a c)")
                    mm = pe.transpose(M[bank][:, i * P:(i + 1) * P], src, ident[:, :])
                mm.then_inc(written[bank], 1)

            def turn_x(s, u):
                if not isinstance(s, int) or s >= 2:
                    wait_next(pe, x_copied, s - 1)
                wait_next(pe, slots_loaded[u % 4], loads_of(s, u))
                for i in range(GROUP_OF):
                    mm = pe.transpose(S[:, u % 2, i * CAP:(i + 1) * CAP], slots_in[:, u % 4, i * REC:i * REC + DIM],
                                      ident[:, :])
                mm.then_inc(x_turned, 1)

            def up_step(s, u):
                if not isinstance(s, int) or s >= 2:
                    wait_next(pe, silu, 3 * s - 3)
                wait_next(pe, x_copied, s + 1)
                for i in range(GROUP_OF):
                    mm = pe.matmul(S[:, 2 + u % 2, i * P:(i + 1) * P], xeT[:, u % 2, i * CAP:(i + 1) * CAP],
                                   w13_flat[:, bass.ds((GROUP_OF * s + i) * P, P)], start=True, stop=True)
                mm.then_inc(up_done, 1)

            def turn_h(s, u):
                if not isinstance(s, int) or s >= 2:
                    wait_next(pe, h_copied, s - 1)
                wait_next(pe, silu, 3 * s + 3)
                for r in range(2):
                    mm = pe.transpose(PV[u % 2][:, r * P:(r + 1) * P], h[:, u % 2, r * P:(r + 1) * P], ident[:, :])
                mm.then_inc(h_turned, 1)

            def down_step(s, u):
                wait_next(pe, h_copied, s + 1)
                for r in range(2):
                    mm = pe.matmul(M[u % 2][:, 2 * r * DIM:(2 * r + 2) * DIM], ehT[:, u % 2, r * CAP:(r + 1) * CAP],
                                   w2bd_flat[:, bass.ds((2 * s + r) * 2 * DIM, 2 * DIM)], start=True, stop=True)
                mm.then_inc(down_done, 1)

            w13_flat = w13[:, :, :].rearrange("p e c -> p (e c)")
            w2bd_flat = w2bd.rearrange("p r c -> p (r c)")
            for o in range(2):
                pe.wait_ge(read[o], epilogue_end[o] + WEIGHT_JOBS // 2)
            pe.wait_ge(pv_read, QUADS * BATCHES)
            pe.wait_ge(exp_done, CHUNKS * BATCHES)

            def step(s, u):
                whole = not isinstance(s, int)
                if whole or s < STEPS:
                    turn_x(s, u)
                if whole or 0 <= s - 1 < STEPS:
                    up_step(s - 1, u - 1)
                if whole or 0 <= s - 2 < STEPS:
                    turn_h(s - 2, u - 2)
                if whole or 0 <= s - 3 < STEPS:
                    if whole or s - 3 >= 2:
                        wait(pe, weighted, s - 4)
                    down_step(s - 3, u - 3)

            for s in range(8):
                step(s, s)
            with pe.Fori(2, STEPS // 4) as r:
                for u in range(4):
                    step(4 * r + u, u + 4)
            for s in range(STEPS, STEPS + 3):
                step(s, s)

        @block.scalar
        def _(act):
            def norm_start(p):
                wait_next(act, post, post_at(p, "moments3"))
                nc.scalar.activation(log_v[:, :], moments[:, :, 1], ACT.Ln, bias=eps[:, :]).then_inc(act_post, 1)
                wait_next(act, act_post, act_post_at(p, "log"))
                nc.scalar.activation(rstd0[:, :], log_v[:, :], ACT.Exp, scale=-0.5).then_inc(act_post, 1)

            def copy_x1T(phase, b):
                bank, n = job(phase, b, "xt")
                wait_next(act, written[bank], n + 1)
                nc.scalar.copy(x1T[:, :], M[bank][:, :]).then_inc(read[bank], 1)

            def gate_sigmoid(p):
                wait_next(act, post, post_at(p, "g1"))
                nc.scalar.activation(eg[:, :], sg[:, :], ACT.Ln).then_inc(act_post, 1)
                wait_next(act, act_post, act_post_at(p, "gate_log"))
                nc.scalar.activation(eg[:, :], eg[:, :], ACT.Exp, scale=-1.0).then_inc(act_post, 1)

            def exp_gate(phase, b, p):
                bank, n = job(phase, b, "gate")
                wait_next(act, written[bank], n + 1)
                nc.scalar.activation(eg[:, :], M[bank][:, :], ACT.Exp, scale=-1.0).then_inc(act_post, 1)

            def exp_logits(phase, b, p):
                bank, n = job(phase, b, "logits")
                wait_next(act, written[bank], n + 1)
                nc.scalar.activation(el[:, :], M[bank][:, 0:TILES * EXPERTS], ACT.Exp, scale=-1.0
                                     ).then_inc(read[bank], 1)

            def build_v(b, lo, hi):
                nc.scalar.copy(V[:, :, lo:hi, 0:HD], tokens_of(X, b).rearrange("p (i h d) -> p i h d", i=TILES, h=HEADS)
                               [:, :, lo:hi, :]).then_inc(v_built, 1)

            def take_turned(phase, b, j):
                bank, n = job(phase, b, f"lr{j}")
                wait(act, written[bank], n + 1)
                nc.scalar.copy(LR[:, j, :, :].rearrange("p a t -> p (a t)"), Mb[bank]).then_inc(read[bank], 1)

            def copy_quad(b, g):
                wait_next(act, unit_weighed, UNITS * b + 2 * g + 2)
                if not isinstance(b, int) or b > 0 or g > 0:
                    wait_next(act, quad_turned, QUADS * b + g)
                nc.scalar.copy(OT[:, :], PV[g % 2][:, :]).then_inc(quad_copied, 1)

            def batch(phase, b):
                wait(act, exp_done, b * CHUNKS)
                wait(act, prep, prep_at(b, "shift"))
                nc.scalar.copy(shift_now[:, :], shift[:, bass.ds(b, 1)]).then_inc(shift_taken, 1)
                wait(act, shift_taken, b + 1)
                for slot in range(SLOTS_PER_BATCH):
                    u = slot // 2
                    for i in range(2 * (slot % 2), 2 * (slot % 2) + 2):
                        n = QUAD * u + i
                        if i == 0 and (u >= 2 or not isinstance(b, int) or b > 0):
                            wait(act, unit_weighed, b * UNITS + u - 1)
                        wait_next(act, scored, b * CHUNKS + n + 1)
                        nc.scalar.activation(E[:, u % 2, 2 * (i // 2):2 * (i // 2) + 2, i % 2, :],
                                             S[:, 2 * (n % 2):2 * (n % 2) + 2, :], ACT.Exp,
                                             bias=shift_now[:, :]).then_inc(exp_done, 1)
                        if i % 2 == 0:
                            for g in range(QUADS - 1):
                                if slot == COPY_SLOT[g]:
                                    copy_quad(b, g)
                            if slot == COPY_SLOT[QUADS - 1] and phase != "first":
                                copy_quad(b - 1, QUADS - 1)
                    if slot == 0:
                        wait(act, x_loaded, 16 * (b + 1))
                        if not isinstance(b, int) or b > 0:
                            wait(act, unit_weighed, b * UNITS - 1)
                        build_v(b, 0, HEADS - QUAD)
                    if slot == 2:
                        wait(act, unit_weighed, b * UNITS)
                        build_v(b, HEADS - QUAD, HEADS)
                    if phase != "last":
                        for j, at in ACT_TAKES.items():
                            if slot == at:
                                take_turned(phase, b, j)
                    if phase != "first":
                        if slot == EXP_SLOT:
                            exp_logits(phase, b, b - 1)
                            exp_gate(phase, b, b - 1)
                        if slot == X1T_SLOT:
                            copy_x1T(phase, b)
                        if slot == NORM_SLOT:
                            norm_start(b - 1)
                        if slot == SIGMOID_SLOT:
                            gate_sigmoid(b - 1)

            nc.scalar.preload_act_table_set("natural_log_exp_and_others")
            act.wait_ge(setup, SETUP)
            act.wait_ge(banks_clear, 2)
            for j in range(1, HEADS // 2, 2):
                act.wait_ge(first_turned, j + 1)
                nc.scalar.copy(LR[:, j, :, :].rearrange("p a t -> p (a t)"), S[:, j % 4, :].bitcast(BF16)
                               ).then_inc(first_taken[1], 1)
            iterations(act, batch)
            copy_quad(BATCHES - 1, QUADS - 1)
            norm_start(BATCHES - 1)
            copy_x1T("epilogue", BATCHES)
            act.wait_ge(post, post_at(BATCHES - 1, "x1_3"))
            nc.scalar.copy(last_rec[:, :, 0:DIM], x1[:, :, :]).then_inc(record, 1)
            exp_gate("epilogue", BATCHES, BATCHES - 1)
            exp_logits("epilogue", BATCHES, BATCHES - 1)
            gate_sigmoid(BATCHES - 1)

            for n in range(1, WEIGHT_JOBS, 2):
                act.wait_ge(written[1], epilogue_end[1] + n // 2 + 1)
                if n < EXPERTS // 4:
                    nc.scalar.copy(w13[:, 4 * n:4 * n + 4, :], M[1][:, :].rearrange("p (a c) -> p a c", a=4)
                                   ).then_inc(read[1], 1)
                else:
                    r = 4 * (n - EXPERTS // 4)
                    act.wait_ge(w2_cleared, 1)
                    src = M[1][:, :].rearrange("p (a c) -> p a c", a=4)
                    nc.scalar.copy(w2bd[0:FF, r:r + 4, 0:DIM], src[0:FF, :, :])
                    nc.scalar.copy(w2bd[FF:P, r:r + 4, DIM:2 * DIM], src[FF:P, :, :]).then_inc(read[1], 1)

            def copy_x(s, u):
                wait_next(act, x_turned, s + 1)
                if not isinstance(s, int) or s >= 2:
                    wait_next(act, up_done, s - 1)
                nc.scalar.copy(xeT[:, u % 2, :], S[:, u % 2, :]).then_inc(x_copied, 1)

            def exp_step(s, u):
                wait_next(act, up_done, s + 1)
                if not isinstance(s, int) or s >= 2:
                    wait_next(act, silu, 3 * s - 3)
                e = eh[:, u % 2, :, :]
                nc.scalar.activation(e, S[:, 2 + u % 2, :].rearrange("p (i c) -> p i c", i=GROUP_OF)[:, :, 0:FF],
                                     ACT.Exp, scale=-1.0).then_inc(exp_up, 1)

            def sigmoid_step(s, u):
                e = eh[:, u % 2, :, :]
                wait_next(act, silu, 3 * s + 1)
                nc.scalar.activation(e, e, ACT.Ln).then_inc(sigmoid, 1)
                wait_next(act, sigmoid, 2 * s + 1)
                nc.scalar.activation(e, e, ACT.Exp, scale=-1.0).then_inc(sigmoid, 1)

            def step(s, u):
                whole = not isinstance(s, int)
                if whole or s < STEPS:
                    copy_x(s, u)
                if whole or 0 <= s - 1 < STEPS:
                    exp_step(s - 1, u - 1)
                    sigmoid_step(s - 1, u - 1)

            step(0, 0)
            step(1, 1)
            with act.Fori(1, STEPS // 2) as r:
                for u in range(2):
                    step(2 * r + u, u + 2)
            step(STEPS, STEPS)

            def last_rsqrt(q, u):
                wait_next(act, summed, sum_at(q, "moments3"))
                nc.scalar.activation(last_log[:, u, :], last_moments[:, u, :, 1], ACT.Ln, bias=eps[:, :]
                                     ).then_inc(act_fin, 1)
                wait_next(act, act_fin, 2 * q + 1)
                nc.scalar.activation(last_rstd0[:, u, :], last_log[:, u, :], ACT.Exp, scale=-0.5).then_inc(act_fin, 1)

            def last_out(q, even, u):
                wait(act, last_scaled, scale_at(q, "offset"))
                if not isinstance(even, int) or even > 0:
                    wait(act, stored[u], 8 * even)
                for i in range(TILES):
                    last = nc.scalar.activation(normed[:, u, i * DIM:(i + 1) * DIM], y(q, i),
                                                ACT.Identity, bias=last_offset[:, u, i:i + 1],
                                                scale=last_rstd[:, u, i:i + 1])
                last.then_inc(normed_done, 1)

            for u in range(2):
                last_rsqrt(u, u)
                last_out(u, 0, u)
            with act.Fori(1, BATCHES // 2) as r:
                for u in range(2):
                    last_rsqrt(2 * r + u, u)
                    last_out(2 * r + u, 2 * r, u)

        @block.vector
        def _(dve):
            v = nc.vector

            def refine(step, after, ready, moments, rstd0, rstd):
                step("veps", v.tensor_scalar(veps[:, :], moments[:, :, 1], NORM_EPS, None, ALU.add))
                ready()
                step("r2", v.tensor_tensor(r2[:, :], rstd0, rstd0, ALU.mult))
                after("r2")
                step("vr2", v.tensor_tensor(r2[:, :], r2[:, :], veps[:, :], ALU.mult))
                after("vr2")
                step("corr", v.tensor_scalar(r2[:, :], r2[:, :], -0.5, 1.5, ALU.mult, ALU.add))
                after("corr")
                step("rstd", v.tensor_tensor(rstd, r2[:, :], rstd0, ALU.mult))
                after("rstd")

            def moments_of(step, after_alone, y, stats, moments):
                for i in range(TILES):
                    step(f"stats{i}", v.bn_stats(stats[:, i, :], y[:, i, :]))
                after_alone("stats3")
                for i in range(TILES):
                    step(f"moments{i}", v.bn_aggr(moments[:, i, :], stats[:, i, :]))

            def leave(b, g):
                src = PV[g % 2][:, :].rearrange("p (i h c) -> p i h c", i=TILES, h=QUAD)
                wait(dve, quad_turned, QUADS * b + g + 1)
                wait_next(dve, pv_read, QUADS * b + g)
                v.reciprocal(rden[:, :, :], src[:, :, :, HD]).then_inc(pv_recip, 1)
                wait(dve, pv_recip, QUADS * b + g + 1)
                dst = O[:, :, g * QUAD * HD:(g + 1) * QUAD * HD].rearrange("p i (h d) -> p i h d", h=QUAD)
                v.tensor_tensor(dst, src[:, :, :, 0:HD], rden[:, :, :].unsqueeze(3).to_broadcast([P, TILES, QUAD, HD]),
                                ALU.mult).then_inc(pv_read, 1)

            def row_maxima(b):
                flag = dve.value_load(slow_flag[0:1, bass.ds(b, 1)], min_val=0, max_val=1)
                with dve.If(flag > 0):
                    for hd in range(HEADS):
                        wait_next(dve, row_scored, b * 24 + hd + 1)
                        v.tensor_reduce(row_max[:, hd, :], S[:, :, :], AX.X, ALU.max, negate=True).then_inc(row_read, 1)
                    wait(dve, row_read, b * 24 + HEADS)
                    wait(dve, row_parts, b * 6)
                    left_over = row_max
                    for k in range(PARTS):
                        col = AQ[:, :, :, ROWS + k].rearrange("p i h -> p h i")
                        v.tensor_copy(col, left_over[:, :, :]).then_inc(row_parts, 1)
                        wait(dve, row_parts, b * 6 + 2 * k + 1)
                        if k < PARTS - 1:
                            v.tensor_tensor(row_rest[:, :, :], left_over[:, :, :], col, ALU.subtract).then_inc(row_parts, 1)
                            wait(dve, row_parts, b * 6 + 2 * k + 2)
                            left_over = row_rest
                    Sb = S[:, 0, :].bitcast(BF16)
                    for q in range(HEADS // 2):
                        wait_next(dve, row_scored, b * 24 + HEADS + q + 1)
                        v.tensor_copy(LR[:, q, 1, :], Sb[:, 0:TOKENS]).then_inc(row_read, 1)
                    v.memset(AQ[:, :, :, ROWS:ROWS + PARTS], 0.0).then_inc(row_parts, 1)
                with dve.Else():
                    dve.sem_inc(row_read, 24)
                    dve.sem_inc(row_parts, 6)

            def operand(A, lo, hi):
                return A[:, :, :, lo:hi].rearrange("p i h c -> p (i h) c")

            def prep_parts(phase, b, q, step, after):
                bank, n = job(phase, b, "mean")
                wait(dve, written[bank], n + 1)
                wait_next(dve, x_loaded, 16 * (q + 1))
                v.tensor_tensor(xc[:, :].rearrange("p (i d) -> p i d", i=TILES),
                                tokens_of(X, q).rearrange("p (i d) -> p i d", i=TILES),
                                M[bank][:, 0:DIM].unsqueeze(1).to_broadcast([P, TILES, DIM]),
                                ALU.subtract).then_inc(read[bank], 1)
                wait(dve, read[bank], n + 1)
                x3 = xc[:, :].rearrange("p (g d) -> p g d", d=HD)
                r3 = rest[:, :].rearrange("p (g d) -> p g d", d=HD)
                step("high", v.tensor_copy(operand(AQ, 0, HD), x3))
                after("high")
                step("rest", v.tensor_tensor(r3, x3, operand(AQ, 0, HD), ALU.subtract))
                after("rest")
                step("middle", v.tensor_copy(operand(AQ, HD, 2 * HD), r3))
                after("middle")
                step("low", v.tensor_tensor(operand(AQ, 2 * HD, 3 * HD), r3, operand(AQ, HD, 2 * HD), ALU.subtract))

            def prep_norms(step, after):
                step("square", v.tensor_tensor(square[:, :], xc[:, :], xc[:, :], ALU.mult))
                after("square")
                step("norms", v.tensor_reduce(norms[:, :], square[:, :].rearrange("p (g d) -> p g d", d=HD), AX.X, ALU.add))
                after("norms")
                step("largest", v.tensor_reduce(largest[:, :], norms[:, :], AX.X, ALU.max))

            def prep_rows(step, after):
                after("low")

                def repeat(part, times):
                    return operand(AQ, part * HD, (part + 1) * HD).unsqueeze(2).to_broadcast(
                        [P, TILES * HEADS, times, HD])

                def key_rows(lo, times):
                    return operand(AK, lo * HD, (lo + times) * HD).rearrange("p g (r d) -> p g r d", r=times)

                step("r24", v.tensor_copy(operand(AQ, 3 * HD, 5 * HD), operand(AQ, 0, 2 * HD)))
                step("r40", v.tensor_copy(operand(AQ, 5 * HD, 6 * HD), operand(AQ, 0, HD)))
                step("l0", v.tensor_copy(key_rows(0, 3), repeat(0, 3)))
                step("l24", v.tensor_copy(key_rows(3, 2), repeat(1, 2)))
                step("l40", v.tensor_copy(key_rows(5, 1), repeat(2, 1)))

            def prep_shift(q, step, after):
                wait_next(dve, all_reduced, q + 1)
                step("slow", v.tensor_scalar(slow_flag[:, bass.ds(q, 1)], largest_all[:, :], SHIFT_LIMIT, None, ALU.is_gt))
                step("neg_small", v.tensor_scalar(neg_small[:, :], largest_all[:, :], SHIFT_LIMIT, -1.0,
                                                  ALU.is_le, ALU.mult))
                after("neg_small")
                step("shift", v.tensor_tensor(shift[:, bass.ds(q, 1)], neg_small[:, :], largest_all[:, :], ALU.mult))

            def take_turned(phase, b, j):
                bank, n = job(phase, b, f"lr{j}")
                wait_next(dve, written[bank], n + 1)
                v.tensor_copy(LR[:, j, :, :].rearrange("p a t -> p (a t)"), Mb[bank]).then_inc(read[bank], 1)

            def post_norm(p, t):
                t.step("y", v.tensor_tensor(O[:, :, :].rearrange("p i d -> p (i d)"), O[:, :, :].rearrange("p i d -> p (i d)"),
                                            tokens_of(X, p), ALU.add))
                t.after("y")
                moments_of(t.step, t.after_alone, O, stats, moments)

            def post_x1(p, t):
                t.after("moments3")
                refine(t.step, t.after, lambda: wait(dve, act_post, act_post_at(p, "rstd0")),
                       moments, rstd0[:, :], rstd[:, :])
                wait(dve, record, 3 * p + 1)
                for i in range(TILES):
                    t.step(f"x1_{i}", v.tensor_scalar(x1[:, i, :], O[:, i, :], moments[:, i, 0:1], rstd[:, i:i + 1],
                                                      ALU.subtract, ALU.mult))

            def post_shared(phase, b, p, t):
                wait_next(dve, act_post, act_post_at(p, "exp_gate"))
                t.step("g1", v.tensor_scalar(sg[:, :], eg[:, :], LARGEST_LOG, 1.0, ALU.min, ALU.add))

            def post_shared_h(phase, b, p, t):
                wait(dve, act_post, act_post_at(p, "gate_sigmoid"))
                bank, n = job(phase, b, "gate")
                v.tensor_tensor(sg[:, :], M[bank][:, :], eg[:, :], ALU.mult).then_inc(read[bank], 1)
                wait(dve, read[bank], n + 1)
                bank, n = job(phase, b, "up")
                wait_next(dve, written[bank], n + 1)
                v.tensor_tensor(hT[:, :], M[bank][:, :], sg[:, :], ALU.mult).then_inc(read[bank], 1)

            def post_scores(phase, b, p, t):
                bank, n = job(phase, b, "logits")
                wait_next(dve, read[bank], n + 1)
                t.step("s1", v.tensor_scalar(scores[:, :], el[:, :], 1.0, None, ALU.add))
                t.after("s1")
                t.step("scores", v.reciprocal(scores[:, :], scores[:, :]))

            def post_groups(p, t):
                t.after("scores")
                ie = lambda a: a[:, :].rearrange("p (i e) -> p i e", i=TILES)
                t.step("sfc", v.tensor_tensor(ie(sfc), ie(scores), bias[:, :].unsqueeze(1).to_broadcast([P, TILES, EXPERTS]),
                                              ALU.add))
                t.after("sfc")
                s8 = sfc[:, :].rearrange("p (g e) -> p g e", e=PER_GROUP)
                t.step("hi4", v.tensor_tensor(hi4[:, :, :], s8[:, :, 0:4], s8[:, :, 4:8], ALU.max))
                t.step("lo4", v.tensor_tensor(lo4[:, :, :], s8[:, :, 0:4], s8[:, :, 4:8], ALU.min))
                t.after("lo4")
                t.step("hi2", v.tensor_tensor(hi2[:, :, :], hi4[:, :, 0:2], hi4[:, :, 2:4], ALU.max))
                t.step("t2", v.tensor_tensor(t2[:, :, :], hi4[:, :, 0:2], hi4[:, :, 2:4], ALU.min))
                t.step("u2", v.tensor_tensor(u2[:, :, :], lo4[:, :, 0:2], lo4[:, :, 2:4], ALU.max))
                t.after("u2")
                t.step("lo2", v.tensor_tensor(lo2[:, :, :], t2[:, :, :], u2[:, :, :], ALU.max))
                t.step("hi1", v.tensor_tensor(hi1[:, :], hi2[:, :, 0], hi2[:, :, 1], ALU.max))
                t.step("t1", v.tensor_tensor(t1[:, :], hi2[:, :, 0], hi2[:, :, 1], ALU.min))
                t.after("lo2")
                t.step("u1", v.tensor_tensor(u1[:, :], lo2[:, :, 0], lo2[:, :, 1], ALU.max))
                t.after("u1")
                t.step("lo1", v.tensor_tensor(lo1[:, :], t1[:, :], u1[:, :], ALU.max))
                t.after("lo1")
                t.step("gs", v.tensor_tensor(gs[:, :, :].rearrange("p i g -> p (i g)"), hi1[:, :], lo1[:, :], ALU.add))
                t.after("gs")
                full = [P, TILES, GROUPS, GROUPS]
                other = gs[:, :, :].unsqueeze(2).to_broadcast(full)
                own = gs[:, :, :].unsqueeze(3).to_broadcast(full)
                t.step("ge", v.tensor_tensor(ge[:, :, :, :], other, own, ALU.is_ge))
                t.step("gt", v.tensor_tensor(gt[:, :, :, :], other, own, ALU.is_gt))
                t.after("ge")
                t.step("geL", v.tensor_tensor(ge[:, :, :, :], ge[:, :, :, :], lower[:, :, :].unsqueeze(1).to_broadcast(full),
                                              ALU.mult))
                t.after("geL")
                t.step("beats", v.tensor_tensor(gt[:, :, :, :], ge[:, :, :, :], gt[:, :, :, :], ALU.max))
                t.after("beats")
                t.step("rank", v.tensor_reduce(rank[:, :], gt[:, :, :, :].rearrange("p i a c -> p (i a) c"), AX.X, ALU.add))
                t.after("rank")
                t.step("keep", v.tensor_scalar(keep[:, :], rank[:, :], float(TOP_GROUPS), None, ALU.is_lt))
                t.after("keep")
                t.step("tmp", v.tensor_tensor(tmp[:, :].rearrange("p (g e) -> p g e", e=PER_GROUP), s8,
                                              keep[:, :].unsqueeze(2).to_broadcast([P, TILES * GROUPS, PER_GROUP]), ALU.mult))

            def post_top(p, t):
                ie = lambda a: a[:, :].rearrange("p (i e) -> p i e", i=TILES)
                t.after("tmp")
                t.step("tmp0", v.tensor_scalar(tmp[:, :], tmp[:, :], 0.0, None, ALU.add))
                t.after_alone("tmp0")
                for i in range(TILES):
                    t.step(f"top{i}", v.max(top[:, i, :], ie(tmp)[:, i, :]))
                t.after_alone("top3")
                for i in range(TILES):
                    t.step(f"rest{i}", v.match_replace(ie(left)[:, i, :], top[:, i, :], ie(tmp)[:, i, :], BELOW_ALL))
                t.after("rest3")
                t.step("mask", v.tensor_tensor(mask[:, :], left[:, :], tmp[:, :], ALU.not_equal))
                t.after("mask")
                t.step("maskb", v.tensor_copy(mask_b[:, :, :].rearrange("p i e -> p (i e)"), mask[:, :]))

            def post_shared_out(phase, b, p):
                bank, n = job(phase, b, "down")
                wait_next(dve, written[bank], n + 1)
                v.tensor_tensor(tokens_of(Z, p), M[bank][:, :], x1[:, :, :].rearrange("p i d -> p (i d)"), ALU.add
                                ).then_inc(read[bank], 1)

            def post_record(p, t):
                ie = lambda a: a[:, :].rearrange("p (i e) -> p i e", i=TILES)
                t.step("wsel", v.tensor_tensor(wsel[:, :], mask[:, :], scores[:, :], ALU.mult))
                t.after("wsel")
                t.step("wsum", v.tensor_reduce(wsum[:, :], ie(wsel), AX.X, ALU.add))
                t.after("wsum")
                t.step("wsum2", v.tensor_scalar(wsum[:, :], wsum[:, :], 1e-20, 1.0 / SCALE, ALU.add, ALU.mult))
                t.after("wsum2")
                t.step("wrec", v.reciprocal(wsum[:, :], wsum[:, :]))
                t.after("wrec")
                rec, _ = record_of(p)
                if not last_of_all(p):
                    wait_next(dve, record_free, p + 1)
                t.step("recw", v.tensor_tensor(rec[:, :, W_COL:W_COL + EXPERTS], ie(scores),
                                               wsum[:, :].unsqueeze(2).to_broadcast([P, TILES, EXPERTS]), ALU.mult))

            def post_pos(phase, b, p, t):
                bank, n = job(phase, b, "pos")
                ie = lambda a: a[:, :].rearrange("p (i e) -> p i e", i=TILES)
                wait_next(dve, written[bank], n + 1)
                v.tensor_tensor(ie(pos), M[bank][:, 0:TILES * EXPERTS].rearrange("p (i e) -> p i e", i=TILES),
                                count[:, :].unsqueeze(1).to_broadcast([P, TILES, EXPERTS]), ALU.add).then_inc(read[bank], 1)
                wait_next(dve, read[bank], n + 1)
                t.step("kept", v.scalar_tensor_tensor(kept[:, :], pos[:, :], float(CAP), mask[:, :], ALU.is_lt, ALU.mult))
                t.step("room", v.tensor_tensor(ie(key), slot_base[:, :].unsqueeze(1).to_broadcast([P, TILES, EXPERTS]),
                                               ie(pos), ALU.subtract))
                t.after("room")
                t.step("key", v.tensor_tensor(key[:, :], key[:, :], kept[:, :], ALU.mult))
                t.after_alone("key")
                for i in range(TILES):
                    t.step(f"slots{i}", v.max(best[:, i, :], ie(key)[:, i, :]))
                t.after("slots3")
                _, index = record_of(p)
                t.step("index", v.tensor_scalar(index[:, :], best[:, :, :].rearrange("p i k -> p (i k)"), -1.0,
                                                float(SLOTS), ALU.mult, ALU.add))

            def post_totals(phase, b, p):
                bank, n = job(phase, b, "totals")
                wait_next(dve, written[bank], n + 1)
                v.tensor_tensor(count[:, :], M[bank][:, 0:EXPERTS], count[:, :], ALU.add).then_inc(read[bank], 1)

            def batch(phase, b):
                p, q = b - 1, b + 1
                t = Steps(dve, post, POST_STEPS, p * len(POST_STEPS))
                w = Steps(dve, prep, PREP_STEPS, q * len(PREP_STEPS))
                with_post, with_prep = phase != "first", phase != "last"
                row_maxima(b)
                if with_prep:
                    prep_parts(phase, b, q, w.step, w.after)
                    prep_rows(w.step, w.after)
                if with_post:
                    leave(p, QUADS - 1)
                    wait(dve, pv_read, QUADS * b)
                    post_norm(p, t)
                if with_prep:
                    take_turned(phase, b, 0)
                if with_post:
                    post_x1(p, t)
                if with_prep:
                    prep_norms(w.step, w.after)
                    take_turned(phase, b, 1)
                if with_post:
                    post_shared(phase, b, p, t)
                    post_scores(phase, b, p, t)
                    post_shared_h(phase, b, p, t)
                leave(b, 0)
                if with_post:
                    post_groups(p, t)
                if with_prep:
                    take_turned(phase, b, 2)
                if with_post:
                    post_top(p, t)
                    post_shared_out(phase, b, p)
                    post_record(p, t)
                leave(b, 1)
                if with_post:
                    post_pos(phase, b, p, t)
                if with_prep:
                    take_turned(phase, b, 4)
                if with_post:
                    post_totals(phase, b, p)
                if with_prep:
                    take_turned(phase, b, 5)
                    prep_shift(q, w.step, w.after)
                leave(b, 2)
                if with_prep:
                    take_turned(phase, b, 7)
                    assert w.order == len(PREP_STEPS)
                if with_post:
                    assert t.order == len(POST_STEPS)

            v.memset(PV[0][:, :], 0.0).then_inc(banks_clear, 1)
            v.memset(PV[1][:, :], 0.0).then_inc(banks_clear, 1)
            w = Steps(dve, prep, PREP_STEPS, 0)
            prep_parts("prologue", 0, 0, w.step, w.after)
            prep_rows(w.step, w.after)
            prep_norms(w.step, w.after)
            for j in range(0, HEADS // 2, 2):
                dve.wait_ge(first_turned, j + 1)
                v.tensor_copy(LR[:, j, :, :].rearrange("p a t -> p (a t)"), S[:, j % 4, :].bitcast(BF16)
                              ).then_inc(first_taken[0], 1)
            prep_shift(0, w.step, w.after)
            dve.wait_ge(setup, SETUP)
            dve.wait_ge(constants, 4)
            v.tensor_copy(slot_base[:, :], slot_base_i[:, :]).then_inc(small_ready, 1)
            v.tensor_copy(token[:, :], token_i[:, :]).then_inc(small_ready, 1)
            v.tensor_copy(blank[:, TOK_COL:REC], blank_i[:, :]).then_inc(small_ready, 1)
            dve.wait_ge(small_turned, 1)
            v.tensor_copy(small_T[:, 0, 0:EXPERTS], PV[1][:, 0:EXPERTS]).then_inc(small_ready, 1)
            v.tensor_copy(small_T[:, 1:4, :], PV[1][:, P:4 * P].rearrange("p (a c) -> p a c", a=3)).then_inc(small_ready, 1)
            dve.wait_ge(small_loaded, 16 * 5)
            dve.wait_ge(small_ready, 5)
            iterations(dve, batch)

            p = BATCHES - 1
            t = Steps(dve, post, POST_STEPS, p * len(POST_STEPS))
            leave(p, QUADS - 1)
            wait(dve, pv_read, QUADS * BATCHES)
            post_norm(p, t)
            post_x1(p, t)
            post_shared("epilogue", BATCHES, p, t)
            post_scores("epilogue", BATCHES, p, t)
            post_shared_h("epilogue", BATCHES, p, t)
            post_groups(p, t)
            post_top(p, t)
            post_shared_out("epilogue", BATCHES, p)
            post_record(p, t)
            post_pos("epilogue", BATCHES, p, t)
            post_totals("epilogue", BATCHES, p)
            v.memset(w2bd, 0.0).then_inc(w2_cleared, 1)
            dve.wait_ge(w2_cleared, 1)
            for n in range(0, WEIGHT_JOBS, 2):
                dve.wait_ge(written[0], epilogue_end[0] + n // 2 + 1)
                src = M[0][:, :].rearrange("p (a c) -> p a c", a=4)
                if n < EXPERTS // 4:
                    v.tensor_copy(w13[:, 4 * n:4 * n + 4, :], src).then_inc(read[0], 1)
                else:
                    r = 4 * (n - EXPERTS // 4)
                    v.tensor_copy(w2bd[0:FF, r:r + 4, 0:DIM], src[0:FF, :, :])
                    v.tensor_copy(w2bd[FF:P, r:r + 4, DIM:2 * DIM], src[FF:P, :, :]).then_inc(read[0], 1)

            def add_one(s, u):
                e = eh[:, u % 2, :, :]
                wait_next(dve, exp_up, s + 1)
                v.tensor_scalar(e, e, LARGEST_LOG, 1.0, ALU.min, ALU.add).then_inc(silu, 1)

            def silu_step(s, u):
                up_ = S[:, 2 + u % 2, :].rearrange("p (i c) -> p i c", i=GROUP_OF)
                e = eh[:, u % 2, :, :]
                wait(dve, sigmoid, 2 * s + 2)
                if not isinstance(s, int) or s >= 2:
                    wait_next(dve, h_turned, s - 1)
                v.tensor_tensor(e, up_[:, :, 0:FF], e, ALU.mult).then_inc(silu, 1)
                wait_next(dve, silu, 3 * s + 2)
                v.tensor_tensor(h[:, u % 2, :].rearrange("p (i f) -> p i f", i=GROUP_OF), up_[:, :, FF:2 * FF], e,
                                ALU.mult).then_inc(silu, 1)

            def copy_h(s, u):
                wait(dve, h_turned, s + 1)
                if not isinstance(s, int) or s >= 2:
                    wait_next(dve, down_done, s - 1)
                v.tensor_copy(ehT[:, u % 2, :], PV[u % 2][:, 0:2 * CAP]).then_inc(h_copied, 1)

            def take_weights(s, u):
                wait(dve, slots_loaded[u % 4], loads_of(s, u))
                if not isinstance(s, int) or s >= 4:
                    wait(dve, weighted, s - 3)
                v.tensor_copy(weight[:, u % 4, :], slots_flat[:, bass.ds((u % 4) * GROUP_OF * REC + W_COL + GROUP_OF * s,
                                                                        GROUP_OF, step=REC + 1)])
                v.tensor_copy(number[:, u % 4, :], slots_in[:, u % 4, TOK_COL::REC]).then_inc(taken, 1)

            def weigh_step(s, u):
                wait(dve, down_done, s + 1)
                wait(dve, taken, s + 1)
                if not isinstance(s, int) or s >= 2:
                    for j in range(SUMS):
                        wait_next(dve, added[j], 16 * (s - 1))
                v.tensor_copy(target[:, u % 2, :], number[:, u % 4, :])
                for i in range(GROUP_OF):
                    last = v.tensor_scalar(ye[:, u % 2, i, :], M[u % 2][:, i * DIM:(i + 1) * DIM],
                                           weight[:, u % 4, i:i + 1], None, ALU.mult)
                last.then_inc(weighted, 1)

            def step(s, u):
                whole = not isinstance(s, int)
                if whole or s < STEPS:
                    take_weights(s, u)
                if whole or 0 <= s - 1 < STEPS:
                    add_one(s - 1, u - 1)
                if whole or 0 <= s - 2 < STEPS:
                    copy_h(s - 2, u - 2)
                if whole or 0 <= s - 3 < STEPS:
                    weigh_step(s - 3, u - 3)
                if whole or 0 <= s - 1 < STEPS:
                    silu_step(s - 1, u - 1)

            for s in range(8):
                step(s, s)
            with dve.Fori(2, STEPS // 4) as r:
                for u in range(4):
                    step(4 * r + u, u + 4)
            for s in range(STEPS, STEPS + 3):
                step(s, s)

            def halves(q, j):
                v.tensor_tensor(part(q, j), part(q, j), part(q, j + 1), ALU.add).then_inc(halved, 1)

            def last_sum(q, following, u):
                t = Steps(dve, summed, SUM_STEPS, q * len(SUM_STEPS))
                wait_next(dve, halved, 2 * q + 2)
                t.step("sum", v.tensor_tensor(part(q, 0), part(q, 0), part(q, 2), ALU.add))
                if following is not None:
                    wait(dve, parts_loaded[1 - u], following)
                    halves(q + 1, 0)
                t.after("sum")
                t.step("y", v.tensor_tensor(part(q, 0), part(q, 0), tokens_of(Z, q), ALU.add))
                if following is not None:
                    halves(q + 1, 2)
                t.after("y")
                if not isinstance(q, int) or q >= 2:
                    wait(dve, last_scaled, scale_at(q - 2, "offset"))
                for i in range(TILES):
                    t.step(f"stats{i}", v.bn_stats(last_stats[:, u, i, :], y(q, i)))
                t.after_alone("stats3")
                for i in range(TILES):
                    t.step(f"moments{i}", v.bn_aggr(last_moments[:, u, i, :], last_stats[:, u, i, :]))

            batch_parts = 16 * SUMS
            dve.wait_ge(parts_loaded[0], batch_parts)
            halves(0, 0)
            halves(0, 2)
            last_sum(0, batch_parts, 0)
            with dve.Fori(1, BATCHES // 2) as r:
                last_sum(2 * r - 1, batch_parts * (r + 1), 1)
                last_sum(2 * r, batch_parts * (r + 1), 0)
            last_sum(BATCHES - 1, None, 1)


_INS = ["L0_attn_x", "L0_ffn_gate_weight", "L0_ffn_e_bias", "L0_ffn_w1", "L0_ffn_w2", "L0_ffn_w3",
        "L0_ffn_shared_gate", "L0_ffn_shared_up", "L0_ffn_shared_down"]


def kernel(**inputs):
    import numpy as np
    import concourse.bacc as bacc
    from concourse.bass_utils import run_bass_kernel_spmd

    nc = bacc.Bacc("TRN2", target_bir_lowering=False, num_devices=1)
    arrays, args = {}, []
    for name in _INS:
        a = np.ascontiguousarray(inputs[name])
        arrays[f"{name}_dram"] = a
        args.append(nc.dram_tensor(f"{name}_dram", a.shape, mybir.dt.from_np(a.dtype), kind="ExternalInput").ap())
    args.append(nc.dram_tensor("out_dram", (BATCHES, TOKENS, DIM), F32, kind="ExternalOutput").ap())
    post_norm_block(nc, *args)
    return run_bass_kernel_spmd(nc, [arrays], core_ids=[0]).results[0]["out_dram"]
```
